# Optimizing a Trainium2 kernel written in Bass

```python
import numpy as np
import jax
import jax.numpy as jnp

def _softmax(x, axis=-1):
    return jax.nn.softmax(x, axis=axis)

def _gelu(x):
    return jax.nn.gelu(x, approximate=True)

def _silu(x):
    return jax.nn.silu(x)

def _sigmoid(x):
    return jax.nn.sigmoid(x)

def _layernorm(x, axis=-1, eps=1e-05):
    m = jnp.mean(x, axis=axis, keepdims=True)
    v = jnp.var(x, axis=axis, keepdims=True)
    return (x - m) / jnp.sqrt(v + eps)

def _scatter_add(tgt, idx, src, axis=0):
    return tgt.at[idx].add(src)

def _segment_sum(src, seg, n):
    return jax.ops.segment_sum(src, seg, n)
kernel_name = 'mk_xattn_ffn_d2_seqx_r4_6f47c1'

def setup_inputs(seed: int=0):
    np.random.seed(seed)
    _w = jnp.asarray

    def _rec_inputs():
        import jax
        import jax.numpy as jnp
        _rk = jax.random.key(seed)
        x = -0.0002928 + 1 * jax.random.normal(jax.random.fold_in(_rk, 1), (16, 256, 512), jnp.float32)
        _lenS = 256 - jax.random.randint(jax.random.fold_in(_rk, 7), (16,), 0, max(1, 256 // 4) + 1, jnp.int32)
        _lenS2 = 256 - jax.random.randint(jax.random.fold_in(_rk, 8), (16,), 0, max(1, 256 // 4) + 1, jnp.int32)
        _ctx_2048P = jax.random.normal(jax.random.fold_in(_rk, 11), (16, 16, 512), jnp.float32)
        _ctx_2048c = jax.random.dirichlet(jax.random.fold_in(_rk, 511), 0.3 * jnp.ones((16,), jnp.float32), (16, 256))
        _ctx_2048t = jnp.einsum('bsk,bkd->bsd', _ctx_2048c, _ctx_2048P)
        _ctx_2048t = _ctx_2048t * jax.lax.rsqrt(jnp.mean(jnp.square(_ctx_2048t)) + 1e-12) * 0.953939
        ctx_2048 = -1.39393e-06 + 0.999914 * (_ctx_2048t + 0.3 * jax.random.normal(jax.random.fold_in(_rk, 611), (16, 256, 512), jnp.float32))
        return (x, ctx_2048)
    x, ctx_2048 = _rec_inputs()

    def _L0_xattn_setup():
        import jax, jax.numpy as jnp
        import numpy as np
        B, S, E, NH = (2, 256, 512, 16)
        DH = E // NH
        EPS = 1e-06

        def _mlstm_forward(q, k, v, Wi, bi, Wf, bf, ln_scale):
            b, s, e = q.shape
            nh = Wi.shape[1]
            dh = e // nh
            x = jnp.concatenate([q, k, v], axis=-1)
            ig = (x @ Wi + bi).transpose(0, 2, 1)[..., None]
            fg = (x @ Wf + bf).transpose(0, 2, 1)[..., None]
            split = lambda t: t.reshape(b, s, nh, dh).transpose(0, 2, 1, 3)
            qh, kh, vh = (split(q), split(k), split(v))
            log_f = jax.nn.log_sigmoid(fg)
            log_f_cum = jnp.concatenate([jnp.zeros((b, nh, 1, 1), q.dtype), jnp.cumsum(log_f, axis=2)], axis=2)
            fg_mat = log_f_cum - jnp.transpose(log_f_cum, (0, 1, 3, 2))
            ltr = jnp.tril(jnp.ones((s, s), dtype=bool))
            log_fg = jnp.where(ltr, fg_mat[:, :, 1:, 1:], -jnp.inf)
            log_D = log_fg + jnp.transpose(ig, (0, 1, 3, 2))
            max_log_D = jnp.max(log_D, axis=-1, keepdims=True)
            D = jnp.exp(log_D - max_log_D)
            qk = jnp.einsum('bhsd,bhtd->bhst', qh, kh) / jnp.sqrt(jnp.asarray(dh, q.dtype))
            C = qk * D
            normalizer = jnp.maximum(jnp.abs(C.sum(-1, keepdims=True)), jnp.exp(-max_log_D))
            Cn = C / (normalizer + EPS)
            h = jnp.einsum('bhst,bhtd->bhsd', Cn, vh)
            mu = h.mean(-1, keepdims=True)
            var = ((h - mu) ** 2).mean(-1, keepdims=True)
            hn = (h - mu) * jax.lax.rsqrt(var + EPS)
            hn = hn * ln_scale.reshape(1, nh, 1, dh)
            return hn.transpose(0, 2, 1, 3).reshape(b, s, e)
        key = jax.random.key(seed)
        ks = jax.random.split(key, 6)
        q = jax.random.normal(ks[0], (B, S, E), dtype=jnp.float32)
        k = jax.random.normal(ks[1], (B, S, E), dtype=jnp.float32)
        v = jax.random.normal(ks[2], (B, S, E), dtype=jnp.float32)
        Wi = jax.random.normal(ks[3], (3 * E, NH), dtype=jnp.float32) * 0.02
        bi = jax.random.normal(ks[4], (NH,), dtype=jnp.float32) * 0.1
        Wf = jax.random.normal(ks[5], (3 * E, NH), dtype=jnp.float32) * 0.02
        bf = jnp.linspace(3.0, 6.0, NH, dtype=jnp.float32)
        ln_scale = jnp.ones((E,), dtype=jnp.float32)
        return {'q': q, 'k': k, 'v': v, 'Wi': Wi, 'bi': bi, 'Wf': Wf, 'bf': bf, 'ln_scale': ln_scale}
    _L0_xattn_all = _L0_xattn_setup()
    _L0_xattn_in = {k: v for k, v in _L0_xattn_all.items() if k in ('Wi', 'bi', 'Wf', 'bf', 'ln_scale')}
    del _L0_xattn_all

    def _L0_ffn_setup():
        import jax, jax.numpy as jnp
        import numpy as np
        TOP_K = 8
        NUM_GROUPS = 8
        key = jax.random.key(seed)
        ks = jax.random.split(key, 6)
        T_B, T_S, H, I, E, G = (1, 512, 512, 192, 32, NUM_GROUPS)
        hidden_states = jax.random.normal(ks[0], (T_B, T_S, H), dtype=jnp.float32)
        gate_weight = jax.random.normal(ks[1], (E, H), dtype=jnp.float32) * 0.02
        gate_up_proj = jax.random.normal(ks[2], (E, 2 * I, H), dtype=jnp.float32) * 0.02
        down_proj = jax.random.normal(ks[3], (E, H, I), dtype=jnp.float32) * 0.02
        merge_groups = jax.random.randint(ks[4], (E,), 0, G, dtype=jnp.int64)
        merge_groups = merge_groups.at[:G].set(jnp.arange(G, dtype=jnp.int64))
        dominant_experts = jax.random.randint(ks[5], (G,), 0, E, dtype=jnp.int64)
        return {'hidden_states': hidden_states, 'gate_weight': gate_weight, 'gate_up_proj': gate_up_proj, 'down_proj': down_proj, 'merge_groups': merge_groups, 'dominant_experts': dominant_experts}
    _L0_ffn_all = _L0_ffn_setup()
    _L0_ffn_in = {k: v for k, v in _L0_ffn_all.items() if k in ('gate_weight', 'gate_up_proj', 'down_proj', 'merge_groups', 'dominant_experts')}
    del _L0_ffn_all

    def _L1_xattn_setup():
        import jax, jax.numpy as jnp
        import numpy as np
        key = jax.random.key(seed)
        k1, k2, k3, k4, k5 = jax.random.split(key, 5)
        B, D_MODEL, L = (2, 256, 512)
        HEAD_DIM = 8
        H = D_MODEL // HEAD_DIM
        return {'k': jax.random.normal(k1, (B, D_MODEL, L), dtype=jnp.float32), 'v': jax.random.normal(k2, (B, D_MODEL, L), dtype=jnp.float32), 'q': jax.random.normal(k3, (B, D_MODEL, L), dtype=jnp.float32), 'ssm_kernel': jax.random.normal(k4, (H, L), dtype=jnp.float32), 'D': jax.random.normal(k5, (H,), dtype=jnp.float32), 'head_dim': HEAD_DIM}
    _L1_xattn_all = _L1_xattn_setup()
    _L1_xattn_in = {k: v for k, v in _L1_xattn_all.items() if k in ('ssm_kernel', 'D')}
    del _L1_xattn_all

    def _L1_ffn_setup():
        import jax, jax.numpy as jnp
        import numpy as np
        TOP_K = 2
        CAPACITY_FACTOR = 1.0

        def _ffn(x, w1, w2):
            h = x @ w1
            x1, x2 = jnp.split(h, 2, axis=-1)
            return x1 * jax.nn.silu(x2) @ w2
        key = jax.random.key(seed)
        ks = jax.random.split(key, 6)
        B, S, D, F, E_r, E_s = (4, 512, 512, 256, 7, 1)
        sc_in = 1.0 / np.sqrt(D)
        sc_mid = 1.0 / np.sqrt(F)
        return {'x': jax.random.normal(ks[0], (B, S, D), dtype=jnp.float32), 'gate_w': jax.random.normal(ks[1], (D, E_r), dtype=jnp.float32) * sc_in, 'expert_bias': jnp.zeros((E_r,), dtype=jnp.float32), 'shared_w1': jax.random.normal(ks[2], (E_s, D, 2 * F), dtype=jnp.float32) * sc_in, 'shared_w2': jax.random.normal(ks[3], (E_s, F, D), dtype=jnp.float32) * sc_mid, 'routed_w1': jax.random.normal(ks[4], (E_r, D, 2 * F), dtype=jnp.float32) * sc_in, 'routed_w2': jax.random.normal(ks[5], (E_r, F, D), dtype=jnp.float32) * sc_mid}
    _L1_ffn_all = _L1_ffn_setup()
    _L1_ffn_in = {k: v for k, v in _L1_ffn_all.items() if k in ('gate_w', 'expert_bias', 'shared_w1', 'shared_w2', 'routed_w1', 'routed_w2')}
    del _L1_ffn_all
    return {'x': x, 'ctx_2048': ctx_2048, 'L0_xattn_Wi': _L0_xattn_in['Wi'], 'L0_xattn_bi': _L0_xattn_in['bi'], 'L0_xattn_Wf': _L0_xattn_in['Wf'], 'L0_xattn_bf': _L0_xattn_in['bf'], 'L0_xattn_ln_scale': _L0_xattn_in['ln_scale'], 'L0_ffn_gate_weight': _L0_ffn_in['gate_weight'], 'L0_ffn_gate_up_proj': _L0_ffn_in['gate_up_proj'], 'L0_ffn_down_proj': _L0_ffn_in['down_proj'], 'L0_ffn_merge_groups': _L0_ffn_in['merge_groups'], 'L0_ffn_dominant_experts': _L0_ffn_in['dominant_experts'], 'L1_xattn_ssm_kernel': _L1_xattn_in['ssm_kernel'], 'L1_xattn_D': _L1_xattn_in['D'], 'L1_ffn_gate_w': _L1_ffn_in['gate_w'], 'L1_ffn_expert_bias': _L1_ffn_in['expert_bias'], 'L1_ffn_shared_w1': _L1_ffn_in['shared_w1'], 'L1_ffn_shared_w2': _L1_ffn_in['shared_w2'], 'L1_ffn_routed_w1': _L1_ffn_in['routed_w1'], 'L1_ffn_routed_w2': _L1_ffn_in['routed_w2']}

def reference(x, ctx_2048, L0_xattn_Wi, L0_xattn_bi, L0_xattn_Wf, L0_xattn_bf, L0_xattn_ln_scale, L0_ffn_gate_weight, L0_ffn_gate_up_proj, L0_ffn_down_proj, L0_ffn_merge_groups, L0_ffn_dominant_experts, L1_xattn_ssm_kernel, L1_xattn_D, L1_ffn_gate_w, L1_ffn_expert_bias, L1_ffn_shared_w1, L1_ffn_shared_w2, L1_ffn_routed_w1, L1_ffn_routed_w2):
    import jax
    import jax.numpy as jnp

    def _L0_xattn_ref(q, k, v, Wi, bi, Wf, bf, ln_scale):
        import jax, jax.numpy as jnp
        import numpy as np
        B, S, E, NH = (2, 256, 512, 16)
        DH = E // NH
        EPS = 1e-06

        def _mlstm_forward(q, k, v, Wi, bi, Wf, bf, ln_scale):
            b, s, e = q.shape
            nh = Wi.shape[1]
            dh = e // nh
            x = jnp.concatenate([q, k, v], axis=-1)
            ig = (x @ Wi + bi).transpose(0, 2, 1)[..., None]
            fg = (x @ Wf + bf).transpose(0, 2, 1)[..., None]
            split = lambda t: t.reshape(b, s, nh, dh).transpose(0, 2, 1, 3)
            qh, kh, vh = (split(q), split(k), split(v))
            log_f = jax.nn.log_sigmoid(fg)
            log_f_cum = jnp.concatenate([jnp.zeros((b, nh, 1, 1), q.dtype), jnp.cumsum(log_f, axis=2)], axis=2)
            fg_mat = log_f_cum - jnp.transpose(log_f_cum, (0, 1, 3, 2))
            ltr = jnp.tril(jnp.ones((s, s), dtype=bool))
            log_fg = jnp.where(ltr, fg_mat[:, :, 1:, 1:], -jnp.inf)
            log_D = log_fg + jnp.transpose(ig, (0, 1, 3, 2))
            max_log_D = jnp.max(log_D, axis=-1, keepdims=True)
            D = jnp.exp(log_D - max_log_D)
            qk = jnp.einsum('bhsd,bhtd->bhst', qh, kh) / jnp.sqrt(jnp.asarray(dh, q.dtype))
            C = qk * D
            normalizer = jnp.maximum(jnp.abs(C.sum(-1, keepdims=True)), jnp.exp(-max_log_D))
            Cn = C / (normalizer + EPS)
            h = jnp.einsum('bhst,bhtd->bhsd', Cn, vh)
            mu = h.mean(-1, keepdims=True)
            var = ((h - mu) ** 2).mean(-1, keepdims=True)
            hn = (h - mu) * jax.lax.rsqrt(var + EPS)
            hn = hn * ln_scale.reshape(1, nh, 1, dh)
            return hn.transpose(0, 2, 1, 3).reshape(b, s, e)
        return _mlstm_forward(q, k, v, Wi, bi, Wf, bf, ln_scale)

    def _L0_ffn_ref(hidden_states, gate_weight, gate_up_proj, down_proj, merge_groups, dominant_experts):
        import jax, jax.numpy as jnp
        import numpy as np
        TOP_K = 8
        NUM_GROUPS = 8
        B, S, H = hidden_states.shape
        G = dominant_experts.shape[0]
        x = hidden_states.reshape(-1, H)
        logits = jnp.einsum('th,eh->te', x, gate_weight)
        probs = jax.nn.softmax(logits.astype(jnp.float32), axis=-1).astype(logits.dtype)
        top_val, top_idx = jax.lax.top_k(probs, TOP_K)
        top_val = top_val / jnp.sum(top_val, axis=-1, keepdims=True)
        sel_group = merge_groups[top_idx]
        onehot = jax.nn.one_hot(sel_group, G, dtype=top_val.dtype)
        w_tg = jnp.einsum('tk,tkg->tg', top_val, onehot)
        gu = gate_up_proj[dominant_experts]
        dn = down_proj[dominant_experts]
        h = jnp.einsum('th,goh->tgo', x, gu)
        gate, up = jnp.split(h, 2, axis=-1)
        act = jax.nn.silu(gate) * up
        y = jnp.einsum('tgi,ghi->tgh', act, dn)
        out = jnp.einsum('tg,tgh->th', w_tg, y)
        return out.reshape(B, S, H)

    def _L1_xattn_ref(k, v, q, ssm_kernel, D, head_dim):
        import jax, jax.numpy as jnp
        import numpy as np
        B, HD, L = k.shape
        H = HD // head_dim
        fft_size = 2 * L
        k_ = k.reshape(B, H, head_dim, L)
        v_ = v.reshape(B, H, head_dim, L)
        q_ = q.reshape(B, H, head_dim, L)
        kv = jnp.einsum('bhil,bhjl->bijhl', k_, v_)
        kv_f = jnp.fft.rfft(kv, n=fft_size)
        kernel_f = jnp.fft.rfft(ssm_kernel, n=fft_size)
        y = jnp.fft.irfft(kv_f * kernel_f, n=fft_size)[..., :L]
        out = y + kv * D[None, None, None, :, None]
        out = jnp.einsum('bijhl,bhil->bjhl', out, q_)
        out = jnp.transpose(out, (0, 2, 1, 3)).reshape(B, H * head_dim, L)
        return out.astype(k.dtype)

    def _L1_ffn_ref(x, gate_w, expert_bias, shared_w1, shared_w2, routed_w1, routed_w2):
        import jax, jax.numpy as jnp
        import numpy as np
        TOP_K = 2
        CAPACITY_FACTOR = 1.0

        def _ffn(x, w1, w2):
            h = x @ w1
            x1, x2 = jnp.split(h, 2, axis=-1)
            return x1 * jax.nn.silu(x2) @ w2
        B, S, D = x.shape
        E_r = gate_w.shape[1]
        T = B * S
        capacity = max(1, int(CAPACITY_FACTOR * T / E_r))
        flat_x = x.reshape(T, D)
        shared_sum = jax.vmap(_ffn, in_axes=(None, 0, 0))(flat_x, shared_w1, shared_w2).sum(0)
        gate_logits = flat_x @ gate_w + expert_bias
        aff = jax.nn.sigmoid(gate_logits)
        _, topk_idx = jax.lax.top_k(aff, TOP_K)
        mask = (topk_idx[:, :, None] == jnp.arange(E_r)[None, None, :]).any(axis=1)
        score = jnp.where(mask, aff, -1.0).T
        _, sel_idx = jax.lax.top_k(score, capacity)
        kept = jnp.take_along_axis(mask.T, sel_idx, axis=1)
        w = jnp.where(kept, jnp.take_along_axis(aff.T, sel_idx, axis=1), 0.0)
        inp = flat_x[sel_idx]
        out = jax.vmap(_ffn)(inp, routed_w1, routed_w2)
        routed_sum = jnp.zeros_like(flat_x).at[sel_idx].add(out * w[:, :, None])
        return (shared_sum + routed_sum).reshape(B, S, D)
    x = x + _L0_xattn_ref(_layernorm(x, axis=-1), ctx_2048, ctx_2048, L0_xattn_Wi, L0_xattn_bi, L0_xattn_Wf, L0_xattn_bf, L0_xattn_ln_scale)
    x = x + _L0_ffn_ref(_layernorm(x, axis=-1), L0_ffn_gate_weight, L0_ffn_gate_up_proj, L0_ffn_down_proj, L0_ffn_merge_groups, L0_ffn_dominant_experts)
    x = x + _L1_xattn_ref(ctx_2048, ctx_2048, _layernorm(x, axis=-1), L1_xattn_ssm_kernel, L1_xattn_D, 8)
    x = x + _L1_ffn_ref(_layernorm(x, axis=-1), L1_ffn_gate_w, L1_ffn_expert_bias, L1_ffn_shared_w1, L1_ffn_shared_w2, L1_ffn_routed_w1, L1_ffn_routed_w2)
    return x

_drawn_inputs = setup_inputs


def setup_inputs(seed=0):
    import zlib

    import numpy as np

    out = dict(_drawn_inputs(seed))
    spreads = {'L0_xattn_ln_scale': (1.0, 0.2), 'L1_ffn_expert_bias': (0.0, 0.8)}
    factors = {'L0_xattn_bi': 64.0,
     'L0_ffn_gate_weight': 8.0,
     'L0_ffn_gate_up_proj': 6.42,
     'L0_ffn_down_proj': 6.438,
     'L1_ffn_gate_w': 6.909,
     'L1_ffn_shared_w1': 5.28,
     'L1_ffn_shared_w2': 5.292,
     'L1_ffn_routed_w1': 6.382,
     'L1_ffn_routed_w2': 6.38}
    for name, (base, spread) in spreads.items():
        noise = np.random.default_rng([zlib.crc32(name.encode()), seed]).standard_normal(out[name].shape)
        drawn = base * np.exp(spread * noise) if base else spread * noise
        out[name] = jnp.asarray(drawn.astype(out[name].dtype))
    for name, factor in factors.items():
        out[name] = (out[name] * factor).astype(out[name].dtype)
    return out
```

```python
from contextlib import ExitStack

import concourse.bass as bass
from concourse import mybir

F32 = mybir.dt.float32
I32 = mybir.dt.int32
ALU = mybir.AluOpType
ACT = mybir.ActivationFunctionType
AX = mybir.AxisListType.X

P = 128
BANK = 512


class Producer:

    def __init__(self, sem, by):
        self.sem, self.by, self.count = sem, by, 0

    def mark(self, ins):
        ins.then_inc(self.sem, self.by)
        self.count += self.by
        return (self, self.count)


class Engine(Producer):

    def __init__(self, queue, sem):
        super().__init__(sem, 1)
        self.q, self.seen = queue, {}

    def wait(self, *marks):
        for source, count in marks:
            if self.seen.get(id(source), 0) < count:
                self.q.wait_ge(source.sem, count)
                self.seen[id(source)] = count

    def then(self, ins):
        m = self.mark(ins)
        self.wait(m)
        return m


class Bank:

    def __init__(self, tensor):
        self.t, self.read = tensor, ()


def run_together(*parts):
    live = [[g, n, 0] for g, n in parts]
    while live:
        live.sort(key=lambda r: r[2] / r[1])
        r = live[0]
        try:
            next(r[0])
            r[2] += 1
        except StopIteration:
            live.remove(r)


def build_program(nc, io, shapes, phases="ABCD"):
    B, S, D = shapes["x"]
    T = B * S
    KT = D // P
    NH = shapes["bi"][0]
    DH = D // NH
    NE, NG = shapes["gate_weight"][0], shapes["dominant"][0]
    FI = shapes["down_t"][1]
    JT = NG * FI // P
    CH, L = shapes["ssm"]
    HR = S // CH
    ER = shapes["gate_w"][1]
    FF = shapes["shared_w2"][0]
    CAP = max(1, int(1.0 * T / ER))
    TOKT = T // P
    ST = S // P
    BLK = 4
    NB = BLK * P
    EPS_LN, EPS_X = 1e-5, 1e-6
    ones_col = DH
    VW = DH + 1

    main = ExitStack()
    with main:
        def semaphore(name):
            return main.enter_context(nc.semaphore(name))

        pe = Engine(nc.tensor, semaphore("pe_progress"))
        dve = Engine(nc.vector, semaphore("dve_progress"))
        act = Engine(nc.scalar, semaphore("act_progress"))
        pool = Engine(nc.gpsimd, semaphore("pool_progress"))
        sp = Engine(nc.sync, semaphore("sp_progress"))
        engines = (pe, dve, act, pool, sp)

        lanes = {}

        def lane(name):
            if name not in lanes:
                lanes[name] = Producer(semaphore("dma_" + name), 16)
            return lanes[name]

        def load(name, out, in_, queue=sp, **more):
            return lane(name).mark(queue.q.dma_start(out, in_, **more))

        banks = [Bank(main.enter_context(nc.psum_tensor(f"bank{i}", [P, BANK], F32)))
                 for i in range(8)]

        def claim(bank):
            pe.wait(*bank.read)
            return bank.t

        def meet():
            marks = [(e, e.count) for e in engines if e.count] + [(l, l.count) for l in lanes.values()]
            for e in engines:
                e.wait(*marks)

        x2_d = nc.dram_tensor("x2_scratch", [T, D], F32)
        q3_d = nc.dram_tensor("xn3_t_scratch", [D, T], F32)
        x3_d = nc.dram_tensor("x3_scratch", [T, D], F32)
        kpad_d = nc.dram_tensor("ssm_padded_scratch", [CH, P - 1 + L + 1], F32)

        def sbuf(ctx, name, shape, dt=F32):
            return ctx.enter_context(nc.sbuf_tensor(name, shape, dt))

        ident = sbuf(main, "ident", [P, P])
        causal = sbuf(main, "causal", [P, 2, 2 * P])
        minus_half = sbuf(main, "minus_half", [P, 2 * NH])
        m_c = dve.then(dve.q.memset(ident[:, :], 0.0))
        dve.then(dve.q.memset(causal[:, :, :], 1.0))
        m_c = dve.mark(dve.q.memset(minus_half[:, :], -0.5))
        pool.wait(m_c)
        pool.then(pool.q.affine_select(out=ident[:, :], in_=ident[:, :], compare_op=ALU.not_equal,
                                       fill=1.0, base=0, pattern=[[-1, P]], channel_multiplier=1))
        for r in range(2):
            consts = pool.then(pool.q.affine_select(out=causal[:, r, 0:P], in_=causal[:, r, 0:P],
                                                    compare_op=ALU.is_ge, fill=0.0, base=0,
                                                    pattern=[[1, P]], channel_multiplier=-1))
        pe.wait(consts)

        bn = sbuf(main, "bn", [P, BLK, 6])
        mv = sbuf(main, "mv", [P, BLK, 2])
        rstd = sbuf(main, "rstd", [P, BLK])

        def layernorm(src, dst, n, ready, dst_free=()):
            dve.wait(*ready)
            for i in range(n):
                dve.then(dve.q.bn_stats(bn[:, i, :], src[:, i, :]))
            for i in range(n):
                dve.then(dve.q.bn_aggr(mv[:, i, :], bn[:, i, :]))
            m = dve.then(dve.q.tensor_scalar(rstd[:, 0:n], mv[:, 0:n, 1], EPS_LN, None, ALU.add))
            pool.wait(m)
            m = pool.mark(pool.q.tensor_tensor(rstd[:, 0:n], rstd[:, 0:n], minus_half[:, 0:n], ALU.pow))
            dve.wait(m, *dst_free)
            for i in range(n):
                m = dve.mark(dve.q.tensor_scalar(dst[:, i, :], src[:, i, :], mv[:, i, 0:1],
                                                 rstd[:, i:i + 1], ALU.subtract, ALU.mult))
            dve.wait(m)
            return m

        def to_features(src_tile, dst, bank, evac, ready, dst_free=()):
            t = claim(bank)
            pe.wait(*ready)
            for k in range(KT):
                ins = pe.q.transpose(t[:, k * P:(k + 1) * P], src_tile[:, k * P:(k + 1) * P], ident[:, :])
            m = pe.mark(ins)
            evac.wait(m, *dst_free)
            v = t[:, :].rearrange("p (k n) -> p k n", k=KT)
            ins = (evac.q.tensor_copy(dst, v) if evac is dve else evac.q.copy(dst, v))
            m = evac.mark(ins)
            bank.read = (m,)
            return m

        ab = ExitStack()
        with ab:
            def sb(name, shape, dt=F32):
                return sbuf(ab, name, shape, dt)

            dom = sb("dom", [1, NG], I32)
            w_gate = sb("w_gate", [P, KT, NG * FI])
            w_up = sb("w_up", [P, KT, NG * FI])
            w_down = sb("w_down", [P, JT, D])
            w_router = sb("w_router", [P, KT, NE])
            merge_i = sb("merge_i", [NE, 1], I32)
            merge_f = sb("merge_f", [NE, 1])
            of_group = sb("of_group", [NE, NG, FI])

            w_if = sb("w_if", [P, 3, KT, 2 * NH])
            b_if = sb("b_if", [P, 2 * NH])
            ln_s = sb("ln_s", [P, D])

            x_t = [sb(f"x_t{i}", [P, BLK, D]) for i in range(2)]
            ctx_t = [sb(f"ctx_t{i}", [P, KT, NB]) for i in range(2)]
            v_t = [sb(f"v_t{i}", [P, ST, NH * VW]) for i in range(2)]
            xn = sb("xn", [P, 2, D])
            q_t = sb("q_t", [P, KT, S])
            gb = sb("gb", [P, ST, 2 * NH])
            la = sb("la", [P, ST, NH])
            nlf = sb("nlf", [P, ST, NH])
            gm = sb("gm", [48, 2, S])
            g_tok = sb("g_tok", [P, ST, NH])
            en_tok = sb("en_tok", [P, ST, NH])
            e_t = [sb(f"e_t{i}", [P, 4, 3, P]) for i in range(2)]
            h_t = sb("h_t", [P, ST, NH, VW])
            hc = sb("hc", [P, ST, NH, DH])
            hq = sb("hq", [P, ST, NH, DH])
            den = sb("den", [P, ST, NH])
            mu = sb("mu", [P, ST, NH])
            va = sb("va", [P, ST, NH])

            xn2 = sb("xn2", [P, D])
            xn_t = sb("xn_t", [P, KT, NB])
            lg = sb("lg", [P, BLK, NE])
            top = sb("top", [P, BLK, 8])
            nmx = sb("nmx", [P, BLK])
            ex = sb("ex", [P, BLK, NE])
            rep = sb("rep", [P, BLK, NE])
            ssum = sb("ssum", [P, BLK])
            sel_t = sb("sel_t", [NE, NB])
            silu = [sb(f"silu{i}", [P, NB]) for i in range(2)]
            a_t = sb("a_t", [P, JT, NB])

            xr = io["x"].rearrange("(m t p) d -> m p t d", p=P, t=BLK)
            ctr = io["ctx_t"].rearrange("(k p) n -> p k n", p=P)
            vr = io["ctx_v"].rearrange("(b t p) c -> b p t c", p=P, t=ST)

            got_x, got_c, got_v = {}, {}, {}
            stored_x2 = {}
            c_read, v_read = {}, {}

            def load_pair(m):
                if m >= T // NB:
                    return
                if m >= 2:
                    sp.wait(stored_x2[m - 2])
                got_x[m] = load(f"x{m % 2}", x_t[m % 2][:, :, :], xr[m])
                if m >= 2:
                    sp.wait(c_read[m - 2])
                got_c[m] = load(f"c{m % 2}", ctx_t[m % 2][:, :, :], ctr[:, :, m * NB:(m + 1) * NB])

            def load_v(b):
                if b >= B:
                    return
                if b >= 2:
                    sp.wait(v_read[b - 2])
                got_v[b] = load(f"v{b % 2}", v_t[b % 2][:, :, :], vr[b])

            load_pair(0)
            got_wif = load("wif", w_if[:, :, :, :], io["w_if"].rearrange("(c k p) n -> p c k n", p=P, c=3))
            load("wif", b_if[:, 0:NH], io["bi"].rearrange("(a n) -> a n", a=1).broadcast_to([P, NH]))
            load("wif", b_if[:, NH:2 * NH], io["bf"].rearrange("(a n) -> a n", a=1).broadcast_to([P, NH]))
            got_wif = load("wif", ln_s[:, :], io["ln_scale"].rearrange("(a n) -> a n", a=1).broadcast_to([P, D]))
            load_v(0)
            got_dom = load("dom", dom[:, :], io["dominant"].rearrange("(a n) -> a n", a=1))
            load("router", w_router[:, :, :], io["gate_weight_t"].rearrange("(k p) n -> p k n", p=P))
            got_router = load("router", merge_i[:, :], io["merge"].rearrange("(n a) -> n a", a=1))
            sp.wait(got_dom)
            gu = io["gate_up_t"].rearrange("e (k p) n -> e p k n", p=P)
            for g in range(NG):
                e = sp.q.value_load(dom[0:1, g:g + 1], min_val=0, max_val=NE - 1)
                src = gu[bass.ds(e, 1)].rearrange("a p k n -> (a p) k n")
                for k in range(KT):
                    load("wgu", w_gate[:, k, g * FI:(g + 1) * FI], src[:, k, 0:FI])
                    got_wgu = load("wgu", w_up[:, k, g * FI:(g + 1) * FI], src[:, k, FI:2 * FI])
                dn = io["down_t"][bass.ds(e, 1)].rearrange("a i d -> (a i) d")
                row = 0
                while row < FI:
                    at = g * FI + row
                    n = min(FI - row, P - at % P)
                    got_wd = load("wd", w_down[at % P:at % P + n, at // P, :], dn[row:row + n, :])
                    row += n
            load_pair(1)

            dve.wait(got_wif)
            gates_w = dve.mark(dve.q.tensor_tensor(w_if[:, 1, :, :], w_if[:, 1, :, :], w_if[:, 2, :, :], ALU.add))
            m = pool.mark(pool.q.iota(of_group[:, :, :], pattern=[[1, NG], [0, FI]], base=0,
                                      channel_multiplier=0, allow_small_or_imprecise_dtypes=True))
            dve.wait(got_router, m)
            dve.then(dve.q.tensor_copy(merge_f[:, :], merge_i[:, :]))
            group_ready = dve.mark(dve.q.tensor_scalar(of_group[:, :, :], of_group[:, :, :], merge_f[:, 0:1], None,
                                                       ALU.is_equal))

            b_misc, b_m, b_qk, b_h, b_gate, b_up, b_w, b_down = banks
            x1_ready = {}
            state = {"xn": (), "q": (), "h_t": (), "gm": (), "g_tok": (), "en": (), "xn2": (), "xn_t": (), "a_t": (),
                     "e": [(), ()], "hs": (), "silu": [(), ()], "sel": ()}

            def attention(b):
                m_, half = divmod(b, 2)
                load_v(b + 1)
                x = x_t[m_ % 2][:, half * ST:(half + 1) * ST, :]
                cx = ctx_t[m_ % 2][:, :, half * S:(half + 1) * S]
                v = v_t[b % 2][:, :, :].rearrange("p t (h c) -> p t h c", c=VW)
                ln = layernorm(x, xn, ST, (got_x[m_],), state["xn"])
                yield
                for t in range(ST):
                    q_ready = to_features(xn[:, t, :], q_t[:, :, t * P:(t + 1) * P], b_misc, act, (ln,), state["q"])
                    yield
                state["xn"] = (q_ready,)
                t0 = claim(b_misc)
                pe.wait(gates_w, q_ready, got_c[m_])
                for t in range(ST):
                    for k in range(2 * KT):
                        src = q_t[:, k, :] if k < KT else cx[:, k - KT, :]
                        ins = pe.q.matmul(t0[:, t * 2 * NH:(t + 1) * 2 * NH], src[:, t * P:(t + 1) * P],
                                          w_if[:, k // KT, k % KT, :], start=(k == 0), stop=(k == 2 * KT - 1))
                m = pe.mark(ins)
                dve.wait(m, *state["g_tok"])
                m = dve.then(dve.q.tensor_tensor(gb[:, :, :], t0[:, 0:ST * 2 * NH].rearrange("p (t n) -> p t n", t=ST),
                                                 b_if[:, :].unsqueeze(1).broadcast_to([P, ST, 2 * NH]), ALU.add))
                b_misc.read = (m,)
                yield
                dve_abs = dve.mark(dve.q.scalar_tensor_tensor(la[:, :, :], gb[:, :, NH:2 * NH], -1.0,
                                                              gb[:, :, NH:2 * NH], ALU.mult, ALU.max))
                act.wait(dve_abs)
                act.then(act.q.activation(la[:, :, :], la[:, :, :], ACT.Exp, scale=-1.0))
                m = act.mark(act.q.activation(la[:, :, :], la[:, :, :], ACT.Ln, bias=1.0))
                dve.wait(m)
                m = dve.then(dve.q.scalar_tensor_tensor(nlf[:, :, :], gb[:, :, NH:2 * NH], 0.0, la[:, :, :],
                                                        ALU.min, ALU.subtract))
                m = dve.then(dve.q.tensor_scalar(nlf[:, :, :], nlf[:, :, :], -1.0, None, ALU.mult))
                yield
                t0 = claim(b_misc)
                pe.wait(m)
                both = t0[0:NH, 0:2 * S].rearrange("p (r s) -> p r s", r=2)
                pe.q.matmul(both, nlf[:, 0, :], causal[:, :, :], start=True, stop=False, skip_group_check=True)
                pe.q.matmul(both[:, :, P:S], nlf[:, 1, :], causal[:, :, 0:P], start=False, stop=False,
                            skip_group_check=True)
                for t in range(ST):
                    ins = pe.q.matmul(both[:, 0, t * P:(t + 1) * P], gb[:, t, 0:NH], ident[:, :], start=False,
                                      stop=(t == ST - 1), skip_group_check=True)
                m = pe.mark(ins)
                dve.wait(m, *state["gm"])
                dve.then(dve.q.tensor_copy(gm[0:NH, 0, :], both[:, 0, :]))
                dve.then(dve.q.tensor_tensor_scan(gm[0:NH, 1, :], gm[0:NH, 0, :], gm[0:NH, 0, :], -3.0e38,
                                                  ALU.max, ALU.max))
                m = dve.then(dve.q.tensor_tensor(gm[32:32 + NH, 0, :], both[:, 1, :], gm[0:NH, 1, :], ALU.subtract))
                b_misc.read = (m,)
                run_max = m
                yield
                t0 = claim(b_misc)
                pe.wait(m)
                for t in range(ST):
                    ins = pe.q.transpose(t0[:, t * 64:t * 64 + 48], gm[:, 0, t * P:(t + 1) * P], ident[0:48, 0:48])
                m = pe.mark(ins)
                tv = t0[:, 0:ST * 64].rearrange("p (t n) -> p t n", t=ST)
                act.wait(m, *state["en"])
                act.q.activation(en_tok[:, :, :], tv[:, :, 32:32 + NH], ACT.Exp)
                g_ready = act.mark(act.q.copy(g_tok[:, :, :], tv[:, :, 0:NH]))
                b_misc.read = (g_ready,)
                yield
                h_evac = []
                for quad in range(NH // 4):
                    e = e_t[quad % 2]
                    act.wait(*state["e"][quad % 2])
                    for pair in range(2):
                        t1 = claim(b_m)
                        pe.wait(run_max)
                        for i in range(2):
                            h = quad * 4 + pair * 2 + i
                            ins = pe.q.matmul(t1[:, i * S:(i + 1) * S],
                                              ident[0:NH, h:h + 1].broadcast_to([NH, P]), gm[0:NH, 1, :],
                                              start=True, stop=True)
                        m = pe.mark(ins)
                        act.wait(m, g_ready)
                        for i in range(2):
                            h = quad * 4 + pair * 2 + i
                            act.q.activation(e[:, pair * 2 + i, 0:3:2, :], t1[:, i * S:(i + 1) * S].rearrange("p (a c) -> p a c", a=2),
                                             ACT.Exp, bias=g_tok[:, 0, h:h + 1], scale=-1.0)
                            m = act.mark(act.q.activation(e[:, pair * 2 + i, 1, :], t1[:, i * S + P:(i + 1) * S],
                                                          ACT.Exp, bias=g_tok[:, 1, h:h + 1], scale=-1.0))
                        b_m.read = (m,)
                        yield
                    pool.wait(m)
                    diag = e[:, :, 0:2, :].rearrange("p h a c -> p h (a c)")
                    masked = pool.mark(pool.q.affine_select(
                        out=diag, in_=diag, compare_op=ALU.is_ge, fill=0.0, base=0,
                        pattern=[[0, 4], [0, 2], [1, P]], channel_multiplier=-1))
                    for i in range(4):
                        h = quad * 4 + i
                        r0, k = (h % 4) * DH, h // 4
                        t2 = claim(b_qk)
                        off_diag = t2[:, 0:3 * P].rearrange("p (a c) -> p a c", a=3)[:, 0:3:2, :]
                        pe.q.matmul(off_diag, cx[r0:r0 + DH, k, 0:P], q_t[r0:r0 + DH, k, :], start=True, stop=True,
                                    tile_position=(r0, 0))
                        m = pe.mark(pe.q.matmul(t2[:, P:2 * P], cx[r0:r0 + DH, k, P:S], q_t[r0:r0 + DH, k, P:S],
                                                start=True, stop=True, tile_position=(r0, 0)))
                        dve.wait(m, masked)
                        c = e[:, i, :, :].rearrange("p a b -> p (a b)")
                        scored = dve.mark(dve.q.scalar_tensor_tensor(c, t2[:, 0:S + P], float(DH) ** -0.5, c,
                                                                     ALU.mult, ALU.mult))
                        b_qk.read = (scored,)
                        yield
                    t3 = claim(b_h)
                    pe.wait(scored, got_v[b])
                    hv = t3[:, 0:ST * 4 * VW].rearrange("p (t h c) -> p t h c", t=ST, h=4)
                    for i in range(4):
                        h = quad * 4 + i
                        pe.q.matmul(hv[:, 0, i, :], e[:, i, 0, :], v[:, 0, h, :], start=True, stop=True)
                        pe.q.matmul(hv[:, 1, i, :], e[:, i, 2, :], v[:, 0, h, :], start=True, stop=False)
                        ins = pe.q.matmul(hv[:, 1, i, :], e[:, i, 1, :], v[:, 1, h, :], start=False, stop=True)
                    m = pe.mark(ins)
                    state["e"][quad % 2] = (m,)
                    act.wait(m, *state["h_t"])
                    h_ready = act.mark(act.q.copy(h_t[:, :, quad * 4:quad * 4 + 4, :], hv))
                    b_h.read = (h_ready,)
                    yield
                v_read[b] = c_read[m_] = m
                state["q"] = state["gm"] = (m,)
                dve.wait(h_ready)
                total = h_t[:, :, :, ones_col]
                dve.then(dve.q.scalar_tensor_tensor(den[:, :, :], total, -1.0, total, ALU.mult, ALU.max))
                dve.then(dve.q.tensor_tensor(den[:, :, :], den[:, :, :], en_tok[:, :, :], ALU.max))
                dve.then(dve.q.tensor_scalar(den[:, :, :], den[:, :, :], EPS_X, None, ALU.add))
                m = dve.then(dve.q.reciprocal(den[:, :, :], den[:, :, :]))
                pool.wait(m)
                def per_head(a):
                    return a[:, :, :].unsqueeze(3).broadcast_to([P, ST, NH, DH])
                m = pool.mark(pool.q.tensor_tensor(hc[:, :, :, :], h_t[:, :, :, 0:DH], per_head(den), ALU.mult))
                state["h_t"] = state["g_tok"] = state["en"] = (m,)
                yield
                dve.wait(m)
                dve.then(dve.q.tensor_reduce(mu[:, :, :], hc[:, :, :, :], AX, ALU.add))
                dve.then(dve.q.tensor_scalar(mu[:, :, :], mu[:, :, :], 1.0 / DH, None, ALU.mult))
                m = dve.then(dve.q.tensor_tensor(hc[:, :, :, :], hc[:, :, :, :], per_head(mu), ALU.subtract))
                act.wait(m)
                m = act.mark(act.q.activation(hq[:, :, :, :], hc[:, :, :, :], ACT.Square))
                yield
                dve.wait(m)
                dve.then(dve.q.tensor_reduce(va[:, :, :], hq[:, :, :, :], AX, ALU.add))
                m = dve.then(dve.q.tensor_scalar(va[:, :, :], va[:, :, :], 1.0 / DH, EPS_X, ALU.mult, ALU.add))
                pool.wait(m)
                m = pool.then(pool.q.tensor_tensor(va[:, :, :], va[:, :, :],
                                                   minus_half[:, :].rearrange("p (t h) -> p t h", t=ST), ALU.pow))
                pool.then(pool.q.tensor_tensor(hc[:, :, :, :], hc[:, :, :, :], per_head(va), ALU.mult))
                m = pool.then(pool.q.tensor_tensor(
                    hc[:, :, :, :], hc[:, :, :, :],
                    ln_s[:, :].rearrange("p (h c) -> p h c", c=DH).unsqueeze(1).broadcast_to([P, ST, NH, DH]), ALU.mult))
                yield
                dve.wait(m)
                x1_ready[b] = dve.then(dve.q.tensor_tensor(
                    x, x, hc[:, :, :, :].rearrange("p t h c -> p t (h c)"), ALU.add))
                yield

            def merged_ffn(m_):
                x = x_t[m_ % 2]
                for i in range(BLK):
                    ln = layernorm(x[:, i:i + 1, :], xn2[:, :].unsqueeze(1), 1, (x1_ready[2 * m_ + 1],), state["xn2"])
                    xt = to_features(xn2, xn_t[:, :, i * P:(i + 1) * P], b_down, act, (ln,), state["xn_t"])
                    state["xn2"] = (xt,)
                    yield
                t7 = claim(b_down)
                pe.wait(xt, got_router)
                for i in range(BLK):
                    for k in range(KT):
                        ins = pe.q.matmul(t7[:, i * NE:(i + 1) * NE], xn_t[:, k, i * P:(i + 1) * P], w_router[:, k, :],
                                          start=(k == 0), stop=(k == KT - 1))
                m = pe.mark(ins)
                dve.wait(m)
                m = dve.then(dve.q.tensor_copy(lg[:, :, :], t7[:, 0:BLK * NE].rearrange("p (t n) -> p t n", t=BLK)))
                b_down.read = (m,)
                dve.then(dve.q.tensor_reduce(nmx[:, :], lg[:, :, :], AX, ALU.max))
                m = dve.then(dve.q.tensor_tensor(lg[:, :, :], lg[:, :, :], nmx[:, :].unsqueeze(2).broadcast_to([P, BLK, NE]),
                                                 ALU.subtract))
                act.wait(m)
                m = act.mark(act.q.activation(ex[:, :, :], lg[:, :, :], ACT.Exp))
                dve.wait(m)
                for i in range(BLK):
                    dve.then(dve.q.max(top[:, i, :], ex[:, i, :]))
                for i in range(BLK):
                    dve.then(dve.q.match_replace(rep[:, i, :], top[:, i, :], ex[:, i, :], 0.0))
                dve.then(dve.q.tensor_tensor(ex[:, :, :], ex[:, :, :], rep[:, :, :], ALU.subtract))
                dve.then(dve.q.tensor_reduce(ssum[:, :], top[:, :, :], AX, ALU.add))
                dve.then(dve.q.reciprocal(ssum[:, :], ssum[:, :]))
                m = dve.then(dve.q.tensor_tensor(ex[:, :, :], ex[:, :, :], ssum[:, :].unsqueeze(2).broadcast_to([P, BLK, NE]),
                                                 ALU.mult))
                yield
                t7 = claim(b_down)
                pe.wait(m)
                for i in range(BLK):
                    ins = pe.q.transpose(t7[0:NE, i * P:(i + 1) * P], ex[:, i, :], ident[:, :])
                m = pe.mark(ins)
                act.wait(m, *state["sel"])
                sel_ready = act.mark(act.q.copy(sel_t[:, :], t7[0:NE, :]))
                b_down.read = (sel_ready,)
                yield
                ogr = of_group[:, :, :].rearrange("e g i -> e (g i)")
                for j in range(JT):
                    cols = slice(j * P, (j + 1) * P)
                    t4 = claim(b_gate)
                    pe.wait(got_wgu, xt)
                    for k in range(KT):
                        ins = pe.q.matmul(t4[:, :], w_gate[:, k, cols], xn_t[:, k, :], start=(k == 0), stop=(k == KT - 1))
                    m_gate = pe.mark(ins)
                    yield
                    t5 = claim(b_up)
                    for k in range(KT):
                        ins = pe.q.matmul(t5[:, :], w_up[:, k, cols], xn_t[:, k, :], start=(k == 0), stop=(k == KT - 1))
                    m_up = pe.mark(ins)
                    t6 = claim(b_w)
                    pe.wait(sel_ready, group_ready)
                    m_w = pe.mark(pe.q.matmul(t6[:, :], ogr[:, cols], sel_t[:, :], start=True, stop=True))
                    sg = silu[j % 2]
                    act.wait(m_gate, *state["silu"][j % 2])
                    m = act.mark(act.q.activation(sg[:, :], t4[:, :], ACT.Silu))
                    b_gate.read = (m,)
                    dve.wait(m, m_up)
                    m = dve.then(dve.q.tensor_tensor(sg[:, :], sg[:, :], t5[:, :], ALU.mult))
                    b_up.read = (m,)
                    dve.wait(m_w, *state["a_t"])
                    act_ready = dve.mark(dve.q.tensor_tensor(a_t[:, j, :], sg[:, :], t6[:, :], ALU.mult))
                    b_w.read = state["silu"][j % 2] = (act_ready,)
                    yield
                state["sel"] = (m_w,)
                state["xn_t"] = (m_up,)
                for i in range(BLK):
                    bank = (b_down, b_gate)[i % 2]
                    t7 = claim(bank)
                    pe.wait(act_ready, got_wd)
                    for j in range(JT):
                        ins = pe.q.matmul(t7[:, :], a_t[:, j, i * P:(i + 1) * P], w_down[:, j, :],
                                          start=(j == 0), stop=(j == JT - 1))
                        if j == JT // 2:
                            yield
                    m = pe.mark(ins)
                    dve.wait(m)
                    m = dve.then(dve.q.tensor_tensor(x[:, i, :], x[:, i, :], t7[:, :], ALU.add))
                    bank.read = (m,)
                    sp.wait(m)
                    st = load(f"x2s{m_ % 2}", x2_d[(m_ * BLK + i) * P:(m_ * BLK + i + 1) * P, :], x[:, i, :])
                    ln = layernorm(x[:, i:i + 1, :], xn2[:, :].unsqueeze(1), 1, (m,), state["xn2"])
                    xt = to_features(xn2, xn_t[:, :, i * P:(i + 1) * P], b_up, act, (ln,), state["xn_t"])
                    state["xn2"] = (xt,)
                    yield
                state["a_t"] = (m_w,)
                state["a_t"] = ((pe, pe.count),)
                stored_x2[m_] = st
                sp.wait(xt)
                st = load("q3", q3_d[:, m_ * NB:(m_ + 1) * NB].rearrange("(k p) n -> p k n", p=P), xn_t[:, :, :])
                state["xn_t"] = (st,)
                load_pair(m_ + 2)
                yield

            def two_attentions(m_):
                for b in (2 * m_, 2 * m_ + 1):
                    yield from attention(b)

            for m_ in range(T // NB + 1):
                parts = []
                if m_ > 0:
                    parts.append((merged_ffn(m_ - 1), 47.0))
                if m_ < T // NB:
                    parts.append((two_attentions(m_), 94.0))
                run_together(*parts)
        meet()

        cc = ExitStack()
        HB = B // 2
        HT = HB * S
        NP_ = HR * (HR // 2) + HR // 2
        with cc:
            def sb(name, shape, dt=F32):
                return sbuf(cc, name, shape, dt)

            ssm = sb("ssm", [CH, P + L])
            dskip = sb("dskip", [CH, 1])
            cr = sb("cr", [P, KT, HT])
            qo = sb("qo", [P, KT, HT])
            toep = [sb(f"toep{i}", [P, L]) for i in range(3)]
            kx = sb("kx", [P, KT, HB, 12])
            kv = [sb(f"kv{i}", [P, KT, HB, NP_]) for i in range(2)]
            qx = sb("qx", [P, KT, HB, 16])
            yf = sb("yf", [P, KT, HB, HR, HR])
            x3 = [sb(f"x3_{i}", [P, D]) for i in range(2)]
            x2l = [sb(f"x2l{i}", [P, D]) for i in range(2)]

            m = dve.mark(dve.q.memset(ssm[:, :], 0.0))
            sp.wait(m)
            load("ssm", ssm[:, P - 1:P - 1 + L], io["ssm"][:, :])
            m = load("ssm", dskip[:, :], io["skip"].rearrange("(n a) -> n a", a=1))
            dve.wait(m)
            m = dve.then(dve.q.tensor_scalar(ssm[:, P - 1:P], ssm[:, P - 1:P], dskip[:, 0:1], None, ALU.add))
            sp.wait(m)
            kpad = load("ssm", kpad_d[:, :], ssm[:, :])
            sp.wait(kpad)
            ct = io["ctx_rev"].rearrange("(k p) n -> p k n", p=P)
            qd = q3_d[:, :].rearrange("(k p) n -> p k n", p=P)
            toep_read = [(), (), ()]
            kx_free = qx_free = yf_free = ()
            kv_free = [(), ()]
            conv_banks, tr_banks = banks[0:4], banks[4:6]
            x3_free = [(), ()]
            x2l_free = [(), ()]
            out_stored = ()
            for half in range(2):
                cols = slice(half * HT, (half + 1) * HT)
                sp.wait(*kx_free, *qx_free)
                for k in range(KT):
                    got_cr = load("cr", cr[:, k, :], ct[:, k, cols])
                sp.wait(*out_stored)
                for k in range(KT):
                    got_q = load("qo", qo[:, k, :], qd[:, k, cols])
                cv = cr[:, :, :].rearrange("p k (b h i) -> p k b h i", b=HB, i=HR)
                qv = qo[:, :, :].rearrange("p k (b h i) -> p k b h i", b=HB, i=HR)
                for h in range(CH):
                    n = half * CH + h
                    sp.wait(*toep_read[n % 3])
                    row = kpad_d[h:h + 1, :]
                    src = bass.AP(row.tensor, row.offset, [[1, P], [1, L]])
                    got_t = load(f"toep{n % 3}", toep[n % 3][:, :], src)
                    kvn = kv[n % 2]
                    pool.wait(got_cr, *kx_free)
                    pool.q.tensor_copy(kx[:, :, :, 0:8], cv[:, :, :, h, :])
                    pool.then(pool.q.tensor_copy(kx[:, :, :, 8:12], cv[:, :, :, h, 0:4]))
                    pool.wait(*kv_free[n % 2])
                    for d in range(5):
                        w = HR if d < 4 else HR // 2
                        m_kv = pool.mark(pool.q.tensor_tensor(kvn[:, :, :, d * HR:d * HR + w], kx[:, :, :, 0:w],
                                                              kx[:, :, :, d:d + w], ALU.mult))
                    pool.wait(m_kv)
                    kx_free = (m_kv,)
                    dve.wait(got_q, *qx_free)
                    dve.q.tensor_copy(qx[:, :, :, 0:8], qv[:, :, :, h, :])
                    m_qx = dve.mark(dve.q.tensor_copy(qx[:, :, :, 8:15], qv[:, :, :, h, 0:7]))
                    pe.wait(got_t, m_kv)
                    for o in range(KT):
                        t = claim(conv_banks[o])
                        for k in range(o + 1):
                            ins = pe.q.matmul(t[:, 0:HB * NP_], toep[n % 3][:, (o - k) * P:(o - k + 1) * P],
                                              kvn[:, k, :, :].rearrange("p b c -> p (b c)"),
                                              start=(k == 0), stop=(k == o))
                        m_y = pe.mark(ins)
                        y = t[:, 0:HB * NP_].rearrange("p (b c) -> p b c", b=HB)
                        act.wait(m_y, *yf_free)
                        f = yf[:, o]
                        act.q.copy(f[:, :, 0:4, :].rearrange("p b d j -> p b (d j)"), y[:, :, 0:32])
                        for w in range(2):
                            act.q.copy(f[:, :, 4, 4 * w:4 * w + 4], y[:, :, 32:36])
                        for d in range(5, 8):
                            c = 8 - d
                            act.q.copy(f[:, :, d, 0:c], y[:, :, c * 8 + d:c * 8 + 8])
                            m_f = act.mark(act.q.copy(f[:, :, d, c:8], y[:, :, c * 8:c * 8 + 8 - c]))
                        conv_banks[o].read = (m_f,)
                        dve.wait(m_f, m_qx)
                        base = qx[:, o, :, :]
                        win = bass.AP(base.tensor, base.offset, [list(base.ap[0]), [16, HB], [1, 8], [1, 8]])
                        dve.then(dve.q.tensor_tensor(f, f, win, ALU.mult))
                        m_o = dve.then(dve.q.tensor_reduce(qv[:, o, :, h, :], f.rearrange("p b d j -> p b j d"), AX, ALU.add))
                    toep_read[n % 3] = (m_y,)
                    kv_free[n % 2] = (m_y,)
                    yf_free = (m_o,)
                    qx_free = (m_o,)
                for i in range(HT // P):
                    g = half * (HT // P) + i
                    s = i % 2
                    sp.wait(*x2l_free[s])
                    got = load(f"x2l{s}", x2l[s][:, :], x2_d[g * P:(g + 1) * P, :])
                    t = claim(tr_banks[s])
                    pe.wait(m_o)
                    for k in range(KT):
                        ins = pe.q.transpose(t[:, k * P:(k + 1) * P], qo[:, k, i * P:(i + 1) * P], ident[:, :])
                    m = pe.mark(ins)
                    dve.wait(m, got, *x3_free[s])
                    m = dve.mark(dve.q.tensor_tensor(x3[s][:, :], x2l[s][:, :], t[:, :], ALU.add))
                    tr_banks[s].read = x2l_free[s] = (m,)
                    sp.wait(m)
                    st = load(f"x3s{s}", x3_d[g * P:(g + 1) * P, :], x3[s][:, :])
                    x3_free[s] = (st,)
                out_stored = ((pe, pe.count),)
        meet()

        dd = ExitStack()
        with dd:
            def sb(name, shape, dt=F32):
                return sbuf(dd, name, shape, dt)

            xt4 = sb("xt4", [P, KT, T])
            x3 = [sb(f"x3d{i}", [P, D]) for i in range(3)]
            xn = [sb(f"xn4_{i}", [P, D]) for i in range(2)]
            w1 = [sb(f"w1_{i}", [P, KT, 2 * FF]) for i in range(2)]
            w2 = [sb(f"w2_{i}", [P, FF // P, D]) for i in range(2)]
            gw = sb("gw", [P, KT, ER])
            eb = sb("eb", [P, ER])
            aff = sb("aff", [P, TOKT, ER])
            gt = sb("gt", [P, TOKT, ER, ER])
            before = sb("before", [P, ER, ER])
            rank = sb("rank", [P, TOKT, ER])
            score = sb("score", [P, ER, TOKT])
            thr = sb("thr", [P, ER])
            cand = sb("cand", [P, ER])
            hit = sb("hit", [P, ER, TOKT])
            cnt = sb("cnt", [P, ER])
            keep = sb("keep", [P, ER])
            earlier = sb("earlier", [P, P])
            ones = sb("ones", [P, P])
            wts = sb("wts", [P, TOKT, ER])
            tot = sb("tot", [P, ER, TOKT])
            scan = sb("scan", [P, ER, TOKT])
            zero = sb("zero", [P, TOKT])
            sg = [sb(f"sg{i}", [P, NB]) for i in range(2)]
            at = sb("at", [P, FF // P, NB])
            o_t = [sb(f"o_t{i}", [P, BLK, D]) for i in range(2)]

            dve.q.memset(zero[:, :], 0.0)
            dve.q.memset(ones[:, :], 1.0)
            m = dve.then(dve.q.memset(earlier[:, :], 1.0))
            m = dve.then(dve.q.memset(before[:, :, :], 1.0))
            pool.wait(m)
            pool.q.affine_select(out=earlier[:, :], in_=earlier[:, :], compare_op=ALU.is_gt, fill=0.0, base=0,
                                 pattern=[[1, P]], channel_multiplier=-1)
            consts = pool.then(pool.q.affine_select(out=before[:, :, :], in_=before[:, :, :], compare_op=ALU.is_gt,
                                                    fill=0.0, base=0, pattern=[[1, ER], [-1, ER]], channel_multiplier=0))
            pe.wait(consts)
            dve.wait(consts)
            got = load("gw", gw[:, :, :], io["gate_w"].rearrange("(k p) n -> p k n", p=P))
            got = load("gw", eb[:, :], io["expert_bias"].rearrange("(a n) -> a n", a=1).broadcast_to([P, ER]))
            xn_free, x3_free = [(), ()], [(), (), ()]
            b_lg = banks[7]
            lgt = claim(b_lg)
            pe.wait(got)
            for i in range(TOKT):
                s = i % 2
                sp.wait(*x3_free[i % 3])
                gx = load(f"x3l{i % 3}", x3[i % 3][:, :], x3_d[i * P:(i + 1) * P, :])
                ln = layernorm(x3[i % 3][:, :].unsqueeze(1), xn[s][:, :].unsqueeze(1), 1, (gx,), xn_free[s])
                x3_free[i % 3] = (ln,)
                m = to_features(xn[s], xt4[:, :, i * P:(i + 1) * P], banks[s], act, (ln,))
                xn_free[s] = (m,)
                pe.wait(m)
                for k in range(KT):
                    ins = pe.q.matmul(lgt[:, i * ER:(i + 1) * ER], xt4[:, k, i * P:(i + 1) * P], gw[:, k, :],
                                      start=(k == 0), stop=(k == KT - 1))
            m = pe.mark(ins)
            dve.wait(m, got)
            m = dve.mark(dve.q.tensor_tensor(aff[:, :, :], lgt[:, 0:TOKT * ER].rearrange("p (t n) -> p t n", n=ER),
                                             eb[:, :].unsqueeze(1).broadcast_to([P, TOKT, ER]), ALU.add))
            b_lg.read = (m,)
            act.wait(m)
            m = act.mark(act.q.activation(aff[:, :, :], aff[:, :, :], ACT.Exp, scale=-1.0))
            dve.wait(m)
            dve.then(dve.q.tensor_scalar(aff[:, :, :], aff[:, :, :], 1.0, None, ALU.add))
            dve.then(dve.q.reciprocal(aff[:, :, :], aff[:, :, :]))
            full = [P, TOKT, ER, ER]
            mine = aff[:, :, :].unsqueeze(3).broadcast_to(full)
            other = aff[:, :, :].unsqueeze(2).broadcast_to(full)
            dve.then(dve.q.tensor_tensor(gt[:, :, :, :], other, mine, ALU.is_equal))
            dve.then(dve.q.tensor_tensor(gt[:, :, :, :], gt[:, :, :, :],
                                         before[:, :, :].unsqueeze(1).broadcast_to(full), ALU.mult))
            dve.then(dve.q.tensor_reduce(rank[:, :, :], gt[:, :, :, :], AX, ALU.add))
            dve.then(dve.q.tensor_tensor(gt[:, :, :, :], other, mine, ALU.is_gt))
            dve.then(dve.q.tensor_reduce(wts[:, :, :], gt[:, :, :, :], AX, ALU.add))
            dve.then(dve.q.tensor_tensor(rank[:, :, :], rank[:, :, :], wts[:, :, :], ALU.add))
            dve.then(dve.q.tensor_scalar(rank[:, :, :], rank[:, :, :], 1.5, None, ALU.is_lt))
            dve.then(dve.q.tensor_tensor(wts[:, :, :], aff[:, :, :], rank[:, :, :], ALU.mult))
            dve.then(dve.q.scalar_tensor_tensor(score[:, :, :].rearrange("p e t -> p t e"), rank[:, :, :], -1.0,
                                                wts[:, :, :], ALU.add, ALU.add))
            dve.then(dve.q.memset(thr[:, :], 0.0))

            def count_ge(limit, op):
                dve.then(dve.q.tensor_tensor(hit[:, :, :], score[:, :, :],
                                             limit[:, :].unsqueeze(2).broadcast_to([P, ER, TOKT]), op))
                m = dve.then(dve.q.tensor_reduce(cnt[:, :], hit[:, :, :], AX, ALU.add))
                t = claim(b_lg)
                pe.wait(m)
                m = pe.mark(pe.q.matmul(t[:, 0:ER], ones[:, :], cnt[:, :], start=True, stop=True))
                dve.wait(m)
                return t

            for bit in range(29, -1, -1):
                dve.then(dve.q.tensor_scalar(cand[:, :].bitcast(I32), thr[:, :].bitcast(I32), 1 << bit, None, ALU.bitwise_or))
                t = count_ge(cand, ALU.is_ge)
                m = dve.then(dve.q.tensor_scalar(keep[:, :], t[:, 0:ER], float(CAP) - 0.5, None, ALU.is_gt))
                b_lg.read = (m,)
                dve.then(dve.q.copy_predicated(thr[:, :], keep[:, :].bitcast(I32), cand[:, :]))
            t = count_ge(thr, ALU.is_gt)
            m = dve.then(dve.q.tensor_scalar(keep[:, :], t[:, 0:ER], -1.0, float(CAP) - 0.5, ALU.mult, ALU.add))
            b_lg.read = (m,)
            over = hit
            dve.then(dve.q.tensor_copy(wts[:, :, :].rearrange("p t e -> p (t e)"), over[:, :, :].rearrange("p e t -> p (e t)")))
            m = dve.then(dve.q.tensor_tensor(hit[:, :, :], score[:, :, :],
                                             thr[:, :].unsqueeze(2).broadcast_to([P, ER, TOKT]), ALU.is_equal))
            N7 = ER * TOKT
            t = claim(b_lg)
            pe.wait(m)
            flat = hit[:, :, :].rearrange("p e t -> p (e t)")
            pe.q.matmul(t[:, 0:N7], ones[:, :], flat, start=True, stop=True)
            m = pe.mark(pe.q.matmul(t[:, N7:2 * N7], earlier[:, :], flat, start=True, stop=True))
            dve.wait(m)
            dve.then(dve.q.tensor_copy(tot[:, :, :].rearrange("p e t -> p (e t)"), t[:, 0:N7]))
            for e in range(ER):
                dve.q.tensor_tensor_scan(scan[:, e, :], tot[:, e, :], zero[:, :], 0.0, ALU.add, ALU.add)
            m = dve.then(dve.q.memset(cnt[:, :], 0.0))
            dve.then(dve.q.tensor_tensor(scan[:, :, :], scan[:, :, :], tot[:, :, :], ALU.subtract))
            m = dve.then(dve.q.tensor_tensor(scan[:, :, :].rearrange("p e t -> p (e t)"),
                                             scan[:, :, :].rearrange("p e t -> p (e t)"), t[:, N7:2 * N7], ALU.add))
            b_lg.read = (m,)
            dve.then(dve.q.tensor_tensor(scan[:, :, :], scan[:, :, :],
                                         keep[:, :].unsqueeze(2).broadcast_to([P, ER, TOKT]), ALU.is_lt))
            dve.then(dve.q.tensor_tensor(scan[:, :, :], scan[:, :, :], hit[:, :, :], ALU.mult))
            dve.then(dve.q.tensor_tensor(scan[:, :, :].rearrange("p e t -> p (e t)"),
                                         scan[:, :, :].rearrange("p e t -> p (e t)"),
                                         wts[:, :, :].rearrange("p t e -> p (t e)"), ALU.add))
            dve.then(dve.q.tensor_tensor(rank[:, :, :], rank[:, :, :], scan[:, :, :].rearrange("p e t -> p t e"), ALU.mult))
            w_ready = dve.then(dve.q.tensor_tensor(wts[:, :, :], aff[:, :, :], rank[:, :, :], ALU.mult))

            w_free = [(), ()]
            o_free = [(), ()]
            at_free = ()
            sg_free = [(), ()]
            n = 0
            for blk in range(T // NB):
                o = o_t[blk % 2]
                sp.wait(*o_free[blk % 2])
                got_o = load(f"o{blk % 2}", o[:, :, :],
                             x3_d[blk * NB:(blk + 1) * NB, :].rearrange("(t p) d -> p t d", p=P))
                for e in range(ER + 1):
                    s = n % 2
                    n += 1
                    a = io["shared_w1"] if e == 0 else io["routed_w1"][e - 1]
                    c = io["shared_w2"] if e == 0 else io["routed_w2"][e - 1]
                    sp.wait(*w_free[s])
                    load(f"w{s}", w1[s][:, :, :], a.rearrange("(k p) n -> p k n", p=P))
                    got_w = load(f"w{s}", w2[s][:, :, :], c.rearrange("(k p) n -> p k n", p=P))
                    pe.wait(got_w)
                    xs = xt4[:, :, blk * NB:(blk + 1) * NB]
                    for f in range(FF // P):
                        up, ga = banks[0 + 2 * f], banks[1 + 2 * f]
                        for bank, off in ((ga, FF), (up, 0)):
                            t = claim(bank)
                            for k in range(KT):
                                ins = pe.q.matmul(t[:, :], w1[s][:, k, off + f * P:off + (f + 1) * P], xs[:, k, :],
                                                  start=(k == 0), stop=(k == KT - 1))
                            m = pe.mark(ins)
                            if bank is ga:
                                act.wait(m, *sg_free[f])
                                ms = act.mark(act.q.activation(sg[f][:, :], t[:, :], ACT.Silu))
                                ga.read = (ms,)
                        dve.wait(m, ms, *at_free)
                        ma = dve.mark(dve.q.tensor_tensor(at[:, f, :], sg[f][:, :], t[:, :], ALU.mult))
                        up.read = sg_free[f] = (ma,)
                    for i in range(BLK):
                        bank = banks[4 + i % 3]
                        t = claim(bank)
                        pe.wait(ma)
                        for f in range(FF // P):
                            ins = pe.q.matmul(t[:, :], at[:, f, i * P:(i + 1) * P], w2[s][:, f, :],
                                              start=(f == 0), stop=(f == FF // P - 1))
                        m = pe.mark(ins)
                        dve.wait(m, got_o)
                        g = blk * BLK + i
                        if e == 0:
                            m = dve.then(dve.q.tensor_tensor(o[:, i, :], o[:, i, :], t[:, :], ALU.add))
                        else:
                            m = dve.then(dve.q.scalar_tensor_tensor(o[:, i, :], t[:, :], wts[:, g, e - 1:e], o[:, i, :],
                                                                    ALU.mult, ALU.add))
                        bank.read = (m,)
                    at_free = w_free[s] = ((pe, pe.count),)
                sp.wait(m)
                st = load(f"out{blk % 2}", io["out"][blk * NB:(blk + 1) * NB, :].rearrange("(t p) d -> p t d", p=P), o[:, :, :])
                o_free[blk % 2] = (st,)
        meet()


def kernel(**inputs):
    import numpy as np
    import concourse.bacc as bacc
    from concourse.bass_utils import run_bass_kernel_spmd

    a = {k: np.asarray(v) for k, v in inputs.items()}
    B, S, D = a["x"].shape
    T = B * S
    NH = a["L0_xattn_bi"].shape[0]
    ctx = a["ctx_2048"].reshape(T, D)
    ctx_t = np.ascontiguousarray(ctx.T)
    arrays = {
        "x": a["x"].reshape(T, D),
        "ctx_t": ctx_t,
        "ctx_rev": np.ascontiguousarray(ctx_t.reshape(D // 128, 128, T)[:, ::-1, :]).reshape(D, T),
        "ctx_v": np.concatenate([ctx.reshape(T, NH, D // NH), np.ones((T, NH, 1), ctx.dtype)], axis=2).reshape(T, -1),
        "w_if": np.concatenate([a["L0_xattn_Wi"], a["L0_xattn_Wf"]], axis=1),
        "bi": a["L0_xattn_bi"], "bf": a["L0_xattn_bf"], "ln_scale": a["L0_xattn_ln_scale"],
        "gate_weight_t": np.ascontiguousarray(a["L0_ffn_gate_weight"].T),
        "gate_up_t": np.ascontiguousarray(a["L0_ffn_gate_up_proj"].transpose(0, 2, 1)),
        "down_t": np.ascontiguousarray(a["L0_ffn_down_proj"].transpose(0, 2, 1)),
        "merge": a["L0_ffn_merge_groups"], "dominant": a["L0_ffn_dominant_experts"],
        "ssm": a["L1_xattn_ssm_kernel"], "skip": a["L1_xattn_D"],
        "gate_w": a["L1_ffn_gate_w"], "expert_bias": a["L1_ffn_expert_bias"],
        "shared_w1": a["L1_ffn_shared_w1"][0], "shared_w2": a["L1_ffn_shared_w2"][0],
        "routed_w1": a["L1_ffn_routed_w1"], "routed_w2": a["L1_ffn_routed_w2"],
    }
    arrays = {k: np.ascontiguousarray(v) for k, v in arrays.items()}
    nc = bacc.Bacc("TRN2", target_bir_lowering=False, num_devices=1)
    io = {k: nc.dram_tensor("in_" + k, list(v.shape), mybir.dt.from_np(v.dtype), kind="ExternalInput").ap()
          for k, v in arrays.items()}
    io["out"] = nc.dram_tensor("out_x", [T, D], F32, kind="ExternalOutput").ap()
    shapes = {k: v.shape for k, v in arrays.items()}
    shapes["x"] = (B, S, D)
    shapes["gate_weight"] = a["L0_ffn_gate_weight"].shape
    build_program(nc, io, shapes)
    r = run_bass_kernel_spmd(nc, [{"in_" + k: v for k, v in arrays.items()}], core_ids=[0])
    return r.results[0]["out_x"].reshape(B, S, D)
```

```python
from contextlib import ExitStack

import concourse.bass as bass
from concourse import mybir

F32 = mybir.dt.float32
I32 = mybir.dt.int32
U32 = mybir.dt.uint32
F32R = mybir.dt.float32r
ALU = mybir.AluOpType
ACT = mybir.ActivationFunctionType
AX = mybir.AxisListType.X

P = 128
BANK = 512


class Producer:

    def __init__(self, sem, by):
        self.sem, self.by, self.count = sem, by, 0

    def mark(self, ins):
        ins.then_inc(self.sem, self.by)
        self.count += self.by
        return (self, self.count)


class Engine(Producer):

    def __init__(self, queue, sem):
        super().__init__(sem, 1)
        self.q, self.seen = queue, {}

    def wait(self, *marks):
        for source, count in marks:
            if self.seen.get(id(source), 0) < count:
                self.q.wait_ge(source.sem, count)
                self.seen[id(source)] = count

    def then(self, ins):
        m = self.mark(ins)
        self.wait(m)
        return m


class Bank:

    def __init__(self, tensor):
        self.t, self.read = tensor, ()


def run_together(*parts):
    live = [[g, n, 0] for g, n in parts]
    while live:
        live.sort(key=lambda r: r[2] / r[1])
        r = live[0]
        try:
            next(r[0])
            r[2] += 1
        except StopIteration:
            live.remove(r)


def build_program(nc, io, shapes, phases="ABCD"):
    B, S, D = shapes["x"]
    T = B * S
    KT = D // P
    NH = shapes["bi"][0]
    DH = D // NH
    NE, NG = shapes["gate_weight"][0], shapes["dominant"][0]
    FI = shapes["down_t"][1]
    JT = NG * FI // P
    CH, L = shapes["ssm"]
    HR = S // CH
    ER = shapes["gate_w"][1]
    FF = shapes["shared_w2"][0]
    CAP = max(1, int(1.0 * T / ER))
    TOKT = T // P
    ST = S // P
    BLK = 4
    NB = BLK * P
    EPS_LN, EPS_X = 1e-5, 1e-6
    ones_col = DH
    VW = DH + 1

    main = ExitStack()
    with main:
        def semaphore(name):
            return main.enter_context(nc.semaphore(name))

        pe = Engine(nc.tensor, semaphore("pe_progress"))
        dve = Engine(nc.vector, semaphore("dve_progress"))
        act = Engine(nc.scalar, semaphore("act_progress"))
        pool = Engine(nc.gpsimd, semaphore("pool_progress"))
        sp = Engine(nc.sync, semaphore("sp_progress"))
        engines = (pe, dve, act, pool, sp)

        lanes = {}

        def lane(name):
            if name not in lanes:
                lanes[name] = Producer(semaphore("dma_" + name), 16)
            return lanes[name]

        def load(name, out, in_, queue=sp, ins=None):
            return lane(name).mark(queue.q.dma_start(out, in_) if ins is None else ins)

        banks = [Bank(main.enter_context(nc.psum_tensor(f"bank{i}", [P, BANK], F32)))
                 for i in range(8)]

        def claim(bank):
            pe.wait(*bank.read)
            return bank.t

        def meet():
            marks = [(e, e.count) for e in engines if e.count] + [(l, l.count) for l in lanes.values()]
            for e in engines:
                e.wait(*marks)

        x2_d = nc.dram_tensor("x2_scratch", [T, D], F32)
        q3_d = nc.dram_tensor("xn3_t_scratch", [D, T], F32)
        x3_d = nc.dram_tensor("x3_scratch", [T, D], F32)
        slots_d = nc.dram_tensor("slots_scratch", [ER * (-(-CAP // 8) * 8), D + 8], F32)
        kpad_d = nc.dram_tensor("ssm_padded_scratch", [CH, P - 1 + L + 1], F32)

        def sbuf(ctx, name, shape, dt=F32):
            return ctx.enter_context(nc.sbuf_tensor(name, shape, dt))

        ident = sbuf(main, "ident", [P, P])
        causal = sbuf(main, "causal", [P, 2, 2 * P])
        minus_half = sbuf(main, "minus_half", [P, 2 * NH])
        m_c = dve.then(dve.q.memset(ident[:, :], 0.0))
        dve.then(dve.q.memset(causal[:, :, :], 1.0))
        m_c = dve.mark(dve.q.memset(minus_half[:, :], -0.5))
        pool.wait(m_c)
        pool.then(pool.q.affine_select(out=ident[:, :], in_=ident[:, :], compare_op=ALU.not_equal,
                                       fill=1.0, base=0, pattern=[[-1, P]], channel_multiplier=1))
        for r in range(2):
            consts = pool.then(pool.q.affine_select(out=causal[:, r, 0:P], in_=causal[:, r, 0:P],
                                                    compare_op=ALU.is_ge, fill=0.0, base=0,
                                                    pattern=[[1, P]], channel_multiplier=-1))
        pe.wait(consts)

        bn = sbuf(main, "bn", [P, BLK, 6])
        mv = sbuf(main, "mv", [P, BLK, 2])
        rstd = sbuf(main, "rstd", [P, BLK])

        def layernorm(src, dst, n, ready, dst_free=()):
            dve.wait(*ready)
            for i in range(n):
                dve.then(dve.q.bn_stats(bn[:, i, :], src[:, i, :]))
            for i in range(n):
                dve.then(dve.q.bn_aggr(mv[:, i, :], bn[:, i, :]))
            m = dve.then(dve.q.tensor_scalar(rstd[:, 0:n], mv[:, 0:n, 1], EPS_LN, None, ALU.add))
            pool.wait(m)
            m = pool.mark(pool.q.tensor_tensor(rstd[:, 0:n], rstd[:, 0:n], minus_half[:, 0:n], ALU.pow))
            dve.wait(m, *dst_free)
            for i in range(n):
                m = dve.mark(dve.q.tensor_scalar(dst[:, i, :], src[:, i, :], mv[:, i, 0:1],
                                                 rstd[:, i:i + 1], ALU.subtract, ALU.mult))
            dve.wait(m)
            return m

        def to_features(src_tile, dst, bank, evac, ready, dst_free=()):
            t = claim(bank)
            pe.wait(*ready)
            for k in range(KT):
                ins = pe.q.transpose(t[:, k * P:(k + 1) * P], src_tile[:, k * P:(k + 1) * P], ident[:, :])
            m = pe.mark(ins)
            evac.wait(m, *dst_free)
            v = t[:, :].rearrange("p (k n) -> p k n", k=KT)
            ins = (evac.q.tensor_copy(dst, v) if evac is dve else evac.q.copy(dst, v))
            m = evac.mark(ins)
            bank.read = (m,)
            return m

        ab = ExitStack()
        with ab:
            def sb(name, shape, dt=F32):
                return sbuf(ab, name, shape, dt)

            dom = sb("dom", [1, NG], I32)
            w_gate = sb("w_gate", [P, KT, NG * FI])
            w_up = sb("w_up", [P, KT, NG * FI])
            w_down = sb("w_down", [P, JT, D])
            w_router = sb("w_router", [P, KT, NE])
            merge_i = sb("merge_i", [NE, 1], I32)
            merge_f = sb("merge_f", [NE, 1])
            of_group = sb("of_group", [NE, NG, FI])

            w_if = sb("w_if", [P, 3, KT, 2 * NH])
            b_if = sb("b_if", [P, 2 * NH])
            ln_s = sb("ln_s", [P, D])

            x_t = [sb(f"x_t{i}", [P, BLK, D]) for i in range(2)]
            ctx_t = [sb(f"ctx_t{i}", [P, KT, NB]) for i in range(2)]
            v_t = [sb(f"v_t{i}", [P, ST, NH * VW]) for i in range(2)]
            xn = sb("xn", [P, 2, D])
            q_t = sb("q_t", [P, KT, S])
            gb = sb("gb", [P, ST, 2 * NH])
            la = sb("la", [P, ST, NH])
            nlf = sb("nlf", [P, ST, NH])
            gm = sb("gm", [48, 2, S])
            g_tok = sb("g_tok", [P, ST, NH])
            en_tok = sb("en_tok", [P, ST, NH])
            e_t = [sb(f"e_t{i}", [P, 4, 3, P]) for i in range(2)]
            h_t = sb("h_t", [P, ST, NH, VW])
            hc = sb("hc", [P, ST, NH, DH])
            hq = sb("hq", [P, ST, NH, DH])
            den = sb("den", [P, ST, NH])
            mu = sb("mu", [P, ST, NH])
            va = sb("va", [P, ST, NH])

            xn2 = sb("xn2", [P, D])
            xn_t = sb("xn_t", [P, KT, NB])
            lg = sb("lg", [P, BLK, NE])
            top = sb("top", [P, BLK, 8])
            nmx = sb("nmx", [P, BLK])
            ex = sb("ex", [P, BLK, NE])
            rep = sb("rep", [P, BLK, NE])
            ssum = sb("ssum", [P, BLK])
            sel_t = sb("sel_t", [NE, NB])
            silu = [sb(f"silu{i}", [P, NB]) for i in range(2)]
            a_t = sb("a_t", [P, JT, NB])

            xr = io["x"].rearrange("(m t p) d -> m p t d", p=P, t=BLK)
            ctr = io["ctx_t"].rearrange("(k p) n -> p k n", p=P)
            vr = io["ctx_v"].rearrange("(b t p) c -> b p t c", p=P, t=ST)

            got_x, got_c, got_v = {}, {}, {}
            stored_x2 = {}
            c_read, v_read = {}, {}

            def load_pair(m):
                if m >= T // NB:
                    return
                if m >= 2:
                    sp.wait(stored_x2[m - 2])
                got_x[m] = load(f"x{m % 2}", x_t[m % 2][:, :, :], xr[m])
                if m >= 2:
                    sp.wait(c_read[m - 2])
                got_c[m] = load(f"c{m % 2}", ctx_t[m % 2][:, :, :], ctr[:, :, m * NB:(m + 1) * NB])

            def load_v(b):
                if b >= B:
                    return
                if b >= 2:
                    sp.wait(v_read[b - 2])
                got_v[b] = load(f"v{b % 2}", v_t[b % 2][:, :, :], vr[b])

            load_pair(0)
            got_wif = load("wif", w_if[:, :, :, :], io["w_if"].rearrange("(c k p) n -> p c k n", p=P, c=3))
            load("wif", b_if[:, 0:NH], io["bi"].rearrange("(a n) -> a n", a=1).broadcast_to([P, NH]))
            load("wif", b_if[:, NH:2 * NH], io["bf"].rearrange("(a n) -> a n", a=1).broadcast_to([P, NH]))
            got_wif = load("wif", ln_s[:, :], io["ln_scale"].rearrange("(a n) -> a n", a=1).broadcast_to([P, D]))
            load_v(0)
            got_dom = load("dom", dom[:, :], io["dominant"].rearrange("(a n) -> a n", a=1))
            load("router", w_router[:, :, :], io["gate_weight_t"].rearrange("(k p) n -> p k n", p=P))
            got_router = load("router", merge_i[:, :], io["merge"].rearrange("(n a) -> n a", a=1))
            sp.wait(got_dom)
            gu = io["gate_up_t"].rearrange("e (k p) n -> e p k n", p=P)
            for g in range(NG):
                e = sp.q.value_load(dom[0:1, g:g + 1], min_val=0, max_val=NE - 1)
                src = gu[bass.ds(e, 1)].rearrange("a p k n -> (a p) k n")
                for k in range(KT):
                    load("wgu", w_gate[:, k, g * FI:(g + 1) * FI], src[:, k, 0:FI])
                    got_wgu = load("wgu", w_up[:, k, g * FI:(g + 1) * FI], src[:, k, FI:2 * FI])
                dn = io["down_t"][bass.ds(e, 1)].rearrange("a i d -> (a i) d")
                row = 0
                while row < FI:
                    at = g * FI + row
                    n = min(FI - row, P - at % P)
                    got_wd = load("wd", w_down[at % P:at % P + n, at // P, :], dn[row:row + n, :])
                    row += n
            load_pair(1)

            dve.wait(got_wif)
            gates_w = dve.mark(dve.q.tensor_tensor(w_if[:, 1, :, :], w_if[:, 1, :, :], w_if[:, 2, :, :], ALU.add))
            m = pool.mark(pool.q.iota(of_group[:, :, :], pattern=[[1, NG], [0, FI]], base=0,
                                      channel_multiplier=0, allow_small_or_imprecise_dtypes=True))
            dve.wait(got_router, m)
            dve.then(dve.q.tensor_copy(merge_f[:, :], merge_i[:, :]))
            group_ready = dve.mark(dve.q.tensor_scalar(of_group[:, :, :], of_group[:, :, :], merge_f[:, 0:1], None,
                                                       ALU.is_equal))

            b_misc, b_m, b_qk, b_h, b_gate, b_up, b_w, b_down = banks
            x1_ready = {}
            state = {"xn": (), "q": (), "h_t": (), "gm": (), "g_tok": (), "en": (), "xn2": (), "xn_t": (), "a_t": (),
                     "e": [(), ()], "hs": (), "silu": [(), ()], "sel": ()}

            def attention(b):
                m_, half = divmod(b, 2)
                load_v(b + 1)
                x = x_t[m_ % 2][:, half * ST:(half + 1) * ST, :]
                cx = ctx_t[m_ % 2][:, :, half * S:(half + 1) * S]
                v = v_t[b % 2][:, :, :].rearrange("p t (h c) -> p t h c", c=VW)
                ln = layernorm(x, xn, ST, (got_x[m_],), state["xn"])
                yield
                for t in range(ST):
                    q_ready = to_features(xn[:, t, :], q_t[:, :, t * P:(t + 1) * P], b_misc, act, (ln,), state["q"])
                    yield
                state["xn"] = (q_ready,)
                t0 = claim(b_misc)
                pe.wait(gates_w, q_ready, got_c[m_])
                for t in range(ST):
                    for k in range(2 * KT):
                        src = q_t[:, k, :] if k < KT else cx[:, k - KT, :]
                        ins = pe.q.matmul(t0[:, t * 2 * NH:(t + 1) * 2 * NH], src[:, t * P:(t + 1) * P],
                                          w_if[:, k // KT, k % KT, :], start=(k == 0), stop=(k == 2 * KT - 1))
                m = pe.mark(ins)
                dve.wait(m, *state["g_tok"])
                m = dve.then(dve.q.tensor_tensor(gb[:, :, :], t0[:, 0:ST * 2 * NH].rearrange("p (t n) -> p t n", t=ST),
                                                 b_if[:, :].unsqueeze(1).broadcast_to([P, ST, 2 * NH]), ALU.add))
                b_misc.read = (m,)
                yield
                dve_abs = dve.mark(dve.q.scalar_tensor_tensor(la[:, :, :], gb[:, :, NH:2 * NH], -1.0,
                                                              gb[:, :, NH:2 * NH], ALU.mult, ALU.max))
                act.wait(dve_abs)
                act.then(act.q.activation(la[:, :, :], la[:, :, :], ACT.Exp, scale=-1.0))
                m = act.mark(act.q.activation(la[:, :, :], la[:, :, :], ACT.Ln, bias=1.0))
                dve.wait(m)
                m = dve.then(dve.q.scalar_tensor_tensor(nlf[:, :, :], gb[:, :, NH:2 * NH], 0.0, la[:, :, :],
                                                        ALU.min, ALU.subtract))
                m = dve.then(dve.q.tensor_scalar(nlf[:, :, :], nlf[:, :, :], -1.0, None, ALU.mult))
                yield
                t0 = claim(b_misc)
                pe.wait(m)
                both = t0[0:NH, 0:2 * S].rearrange("p (r s) -> p r s", r=2)
                pe.q.matmul(both, nlf[:, 0, :], causal[:, :, :], start=True, stop=False, skip_group_check=True)
                pe.q.matmul(both[:, :, P:S], nlf[:, 1, :], causal[:, :, 0:P], start=False, stop=False,
                            skip_group_check=True)
                for t in range(ST):
                    ins = pe.q.matmul(both[:, 0, t * P:(t + 1) * P], gb[:, t, 0:NH], ident[:, :], start=False,
                                      stop=(t == ST - 1), skip_group_check=True)
                m = pe.mark(ins)
                dve.wait(m, *state["gm"])
                dve.then(dve.q.tensor_copy(gm[0:NH, 0, :], both[:, 0, :]))
                dve.then(dve.q.tensor_tensor_scan(gm[0:NH, 1, :], gm[0:NH, 0, :], gm[0:NH, 0, :], -3.0e38,
                                                  ALU.max, ALU.max))
                m = dve.then(dve.q.tensor_tensor(gm[32:32 + NH, 0, :], both[:, 1, :], gm[0:NH, 1, :], ALU.subtract))
                b_misc.read = (m,)
                run_max = m
                yield
                t0 = claim(b_misc)
                pe.wait(m)
                for t in range(ST):
                    ins = pe.q.transpose(t0[:, t * 64:t * 64 + 48], gm[:, 0, t * P:(t + 1) * P], ident[0:48, 0:48])
                m = pe.mark(ins)
                tv = t0[:, 0:ST * 64].rearrange("p (t n) -> p t n", t=ST)
                act.wait(m, *state["en"])
                act.q.activation(en_tok[:, :, :], tv[:, :, 32:32 + NH], ACT.Exp)
                g_ready = act.mark(act.q.copy(g_tok[:, :, :], tv[:, :, 0:NH]))
                b_misc.read = (g_ready,)
                yield
                h_evac = []
                for quad in range(NH // 4):
                    e = e_t[quad % 2]
                    act.wait(*state["e"][quad % 2])
                    for pair in range(2):
                        t1 = claim(b_m)
                        pe.wait(run_max)
                        for i in range(2):
                            h = quad * 4 + pair * 2 + i
                            ins = pe.q.matmul(t1[:, i * S:(i + 1) * S],
                                              ident[0:NH, h:h + 1].broadcast_to([NH, P]), gm[0:NH, 1, :],
                                              start=True, stop=True)
                        m = pe.mark(ins)
                        act.wait(m, g_ready)
                        for i in range(2):
                            h = quad * 4 + pair * 2 + i
                            act.q.activation(e[:, pair * 2 + i, 0:3:2, :], t1[:, i * S:(i + 1) * S].rearrange("p (a c) -> p a c", a=2),
                                             ACT.Exp, bias=g_tok[:, 0, h:h + 1], scale=-1.0)
                            m = act.mark(act.q.activation(e[:, pair * 2 + i, 1, :], t1[:, i * S + P:(i + 1) * S],
                                                          ACT.Exp, bias=g_tok[:, 1, h:h + 1], scale=-1.0))
                        b_m.read = (m,)
                        yield
                    pool.wait(m)
                    diag = e[:, :, 0:2, :].rearrange("p h a c -> p h (a c)")
                    masked = pool.mark(pool.q.affine_select(
                        out=diag, in_=diag, compare_op=ALU.is_ge, fill=0.0, base=0,
                        pattern=[[0, 4], [0, 2], [1, P]], channel_multiplier=-1))
                    for i in range(4):
                        h = quad * 4 + i
                        r0, k = (h % 4) * DH, h // 4
                        t2 = claim(b_qk)
                        off_diag = t2[:, 0:3 * P].rearrange("p (a c) -> p a c", a=3)[:, 0:3:2, :]
                        pe.q.matmul(off_diag, cx[r0:r0 + DH, k, 0:P], q_t[r0:r0 + DH, k, :], start=True, stop=True,
                                    tile_position=(r0, 0))
                        m = pe.mark(pe.q.matmul(t2[:, P:2 * P], cx[r0:r0 + DH, k, P:S], q_t[r0:r0 + DH, k, P:S],
                                                start=True, stop=True, tile_position=(r0, 0)))
                        dve.wait(m, masked)
                        c = e[:, i, :, :].rearrange("p a b -> p (a b)")
                        scored = dve.mark(dve.q.scalar_tensor_tensor(c, t2[:, 0:S + P], float(DH) ** -0.5, c,
                                                                     ALU.mult, ALU.mult))
                        b_qk.read = (scored,)
                        yield
                    t3 = claim(b_h)
                    pe.wait(scored, got_v[b])
                    hv = t3[:, 0:ST * 4 * VW].rearrange("p (t h c) -> p t h c", t=ST, h=4)
                    for i in range(4):
                        h = quad * 4 + i
                        pe.q.matmul(hv[:, 0, i, :], e[:, i, 0, :], v[:, 0, h, :], start=True, stop=True)
                        pe.q.matmul(hv[:, 1, i, :], e[:, i, 2, :], v[:, 0, h, :], start=True, stop=False)
                        ins = pe.q.matmul(hv[:, 1, i, :], e[:, i, 1, :], v[:, 1, h, :], start=False, stop=True)
                    m = pe.mark(ins)
                    state["e"][quad % 2] = (m,)
                    act.wait(m, *state["h_t"])
                    h_ready = act.mark(act.q.copy(h_t[:, :, quad * 4:quad * 4 + 4, :], hv))
                    b_h.read = (h_ready,)
                    yield
                v_read[b] = c_read[m_] = m
                state["q"] = state["gm"] = (m,)
                dve.wait(h_ready)
                total = h_t[:, :, :, ones_col]
                dve.then(dve.q.scalar_tensor_tensor(den[:, :, :], total, -1.0, total, ALU.mult, ALU.max))
                dve.then(dve.q.tensor_tensor(den[:, :, :], den[:, :, :], en_tok[:, :, :], ALU.max))
                dve.then(dve.q.tensor_scalar(den[:, :, :], den[:, :, :], EPS_X, None, ALU.add))
                m = dve.then(dve.q.reciprocal(den[:, :, :], den[:, :, :]))
                pool.wait(m)
                def per_head(a):
                    return a[:, :, :].unsqueeze(3).broadcast_to([P, ST, NH, DH])
                m = pool.mark(pool.q.tensor_tensor(hc[:, :, :, :], h_t[:, :, :, 0:DH], per_head(den), ALU.mult))
                state["h_t"] = state["g_tok"] = state["en"] = (m,)
                yield
                dve.wait(m)
                dve.then(dve.q.tensor_reduce(mu[:, :, :], hc[:, :, :, :], AX, ALU.add))
                dve.then(dve.q.tensor_scalar(mu[:, :, :], mu[:, :, :], 1.0 / DH, None, ALU.mult))
                m = dve.then(dve.q.tensor_tensor(hc[:, :, :, :], hc[:, :, :, :], per_head(mu), ALU.subtract))
                act.wait(m)
                m = act.mark(act.q.activation(hq[:, :, :, :], hc[:, :, :, :], ACT.Square))
                yield
                dve.wait(m)
                dve.then(dve.q.tensor_reduce(va[:, :, :], hq[:, :, :, :], AX, ALU.add))
                m = dve.then(dve.q.tensor_scalar(va[:, :, :], va[:, :, :], 1.0 / DH, EPS_X, ALU.mult, ALU.add))
                pool.wait(m)
                m = pool.then(pool.q.tensor_tensor(va[:, :, :], va[:, :, :],
                                                   minus_half[:, :].rearrange("p (t h) -> p t h", t=ST), ALU.pow))
                pool.then(pool.q.tensor_tensor(hc[:, :, :, :], hc[:, :, :, :], per_head(va), ALU.mult))
                m = pool.then(pool.q.tensor_tensor(
                    hc[:, :, :, :], hc[:, :, :, :],
                    ln_s[:, :].rearrange("p (h c) -> p h c", c=DH).unsqueeze(1).broadcast_to([P, ST, NH, DH]), ALU.mult))
                yield
                dve.wait(m)
                x1_ready[b] = dve.then(dve.q.tensor_tensor(
                    x, x, hc[:, :, :, :].rearrange("p t h c -> p t (h c)"), ALU.add))
                yield

            def merged_ffn(m_):
                x = x_t[m_ % 2]
                for i in range(BLK):
                    ln = layernorm(x[:, i:i + 1, :], xn2[:, :].unsqueeze(1), 1, (x1_ready[2 * m_ + 1],), state["xn2"])
                    xt = to_features(xn2, xn_t[:, :, i * P:(i + 1) * P], b_down, act, (ln,), state["xn_t"])
                    state["xn2"] = (xt,)
                    yield
                t7 = claim(b_down)
                pe.wait(xt, got_router)
                for i in range(BLK):
                    for k in range(KT):
                        ins = pe.q.matmul(t7[:, i * NE:(i + 1) * NE], xn_t[:, k, i * P:(i + 1) * P], w_router[:, k, :],
                                          start=(k == 0), stop=(k == KT - 1))
                m = pe.mark(ins)
                dve.wait(m)
                m = dve.then(dve.q.tensor_copy(lg[:, :, :], t7[:, 0:BLK * NE].rearrange("p (t n) -> p t n", t=BLK)))
                b_down.read = (m,)
                dve.then(dve.q.tensor_reduce(nmx[:, :], lg[:, :, :], AX, ALU.max))
                m = dve.then(dve.q.tensor_tensor(lg[:, :, :], lg[:, :, :], nmx[:, :].unsqueeze(2).broadcast_to([P, BLK, NE]),
                                                 ALU.subtract))
                act.wait(m)
                m = act.mark(act.q.activation(ex[:, :, :], lg[:, :, :], ACT.Exp))
                dve.wait(m)
                for i in range(BLK):
                    dve.then(dve.q.max(top[:, i, :], ex[:, i, :]))
                for i in range(BLK):
                    dve.then(dve.q.match_replace(rep[:, i, :], top[:, i, :], ex[:, i, :], 0.0))
                dve.then(dve.q.tensor_tensor(ex[:, :, :], ex[:, :, :], rep[:, :, :], ALU.subtract))
                dve.then(dve.q.tensor_reduce(ssum[:, :], top[:, :, :], AX, ALU.add))
                dve.then(dve.q.reciprocal(ssum[:, :], ssum[:, :]))
                m = dve.then(dve.q.tensor_tensor(ex[:, :, :], ex[:, :, :], ssum[:, :].unsqueeze(2).broadcast_to([P, BLK, NE]),
                                                 ALU.mult))
                yield
                t7 = claim(b_down)
                pe.wait(m)
                for i in range(BLK):
                    ins = pe.q.transpose(t7[0:NE, i * P:(i + 1) * P], ex[:, i, :], ident[:, :])
                m = pe.mark(ins)
                act.wait(m, *state["sel"])
                sel_ready = act.mark(act.q.copy(sel_t[:, :], t7[0:NE, :]))
                b_down.read = (sel_ready,)
                yield
                ogr = of_group[:, :, :].rearrange("e g i -> e (g i)")
                for j in range(JT):
                    cols = slice(j * P, (j + 1) * P)
                    t4 = claim(b_gate)
                    pe.wait(got_wgu, xt)
                    for k in range(KT):
                        ins = pe.q.matmul(t4[:, :], w_gate[:, k, cols], xn_t[:, k, :], start=(k == 0), stop=(k == KT - 1))
                    m_gate = pe.mark(ins)
                    yield
                    t5 = claim(b_up)
                    for k in range(KT):
                        ins = pe.q.matmul(t5[:, :], w_up[:, k, cols], xn_t[:, k, :], start=(k == 0), stop=(k == KT - 1))
                    m_up = pe.mark(ins)
                    t6 = claim(b_w)
                    pe.wait(sel_ready, group_ready)
                    m_w = pe.mark(pe.q.matmul(t6[:, :], ogr[:, cols], sel_t[:, :], start=True, stop=True))
                    sg = silu[j % 2]
                    act.wait(m_gate, *state["silu"][j % 2])
                    m = act.mark(act.q.activation(sg[:, :], t4[:, :], ACT.Silu))
                    b_gate.read = (m,)
                    dve.wait(m, m_up)
                    m = dve.then(dve.q.tensor_tensor(sg[:, :], sg[:, :], t5[:, :], ALU.mult))
                    b_up.read = (m,)
                    dve.wait(m_w, *state["a_t"])
                    act_ready = dve.mark(dve.q.tensor_tensor(a_t[:, j, :], sg[:, :], t6[:, :], ALU.mult))
                    b_w.read = state["silu"][j % 2] = (act_ready,)
                    yield
                state["sel"] = (m_w,)
                state["xn_t"] = (m_up,)
                for i in range(BLK):
                    bank = (b_down, b_gate)[i % 2]
                    t7 = claim(bank)
                    pe.wait(act_ready, got_wd)
                    for j in range(JT):
                        ins = pe.q.matmul(t7[:, :], a_t[:, j, i * P:(i + 1) * P], w_down[:, j, :],
                                          start=(j == 0), stop=(j == JT - 1))
                        if j == JT // 2:
                            yield
                    m = pe.mark(ins)
                    dve.wait(m)
                    m = dve.then(dve.q.tensor_tensor(x[:, i, :], x[:, i, :], t7[:, :], ALU.add))
                    bank.read = (m,)
                    sp.wait(m)
                    st = load(f"x2s{m_ % 2}", x2_d[(m_ * BLK + i) * P:(m_ * BLK + i + 1) * P, :], x[:, i, :])
                    ln = layernorm(x[:, i:i + 1, :], xn2[:, :].unsqueeze(1), 1, (m,), state["xn2"])
                    xt = to_features(xn2, xn_t[:, :, i * P:(i + 1) * P], b_up, act, (ln,), state["xn_t"])
                    state["xn2"] = (xt,)
                    yield
                state["a_t"] = (m_w,)
                state["a_t"] = ((pe, pe.count),)
                stored_x2[m_] = st
                sp.wait(xt)
                st = load("q3", q3_d[:, m_ * NB:(m_ + 1) * NB].rearrange("(k p) n -> p k n", p=P), xn_t[:, :, :])
                state["xn_t"] = (st,)
                load_pair(m_ + 2)
                yield

            def two_attentions(m_):
                for b in (2 * m_, 2 * m_ + 1):
                    yield from attention(b)

            for m_ in range(T // NB + 1):
                parts = []
                if m_ > 0:
                    parts.append((merged_ffn(m_ - 1), 47.0))
                if m_ < T // NB:
                    parts.append((two_attentions(m_), 94.0))
                run_together(*parts)
        meet()

        cc = ExitStack()
        HB = B // 2
        HT = HB * S
        NP_ = HR * (HR // 2) + HR // 2
        with cc:
            def sb(name, shape, dt=F32):
                return sbuf(cc, name, shape, dt)

            ssm = sb("ssm", [CH, P + L])
            dskip = sb("dskip", [CH, 1])
            cr = sb("cr", [P, KT, HT])
            qo = sb("qo", [P, KT, HT])
            toep = [sb(f"toep{i}", [P, L]) for i in range(3)]
            kx = sb("kx", [P, KT, HB, 12])
            kv = [sb(f"kv{i}", [P, KT, HB, NP_]) for i in range(2)]
            qx = sb("qx", [P, KT, HB, 16])
            yf = sb("yf", [P, KT, HB, HR, HR])
            x3 = [sb(f"x3_{i}", [P, D]) for i in range(2)]
            x2l = [sb(f"x2l{i}", [P, D]) for i in range(2)]

            m = dve.mark(dve.q.memset(ssm[:, :], 0.0))
            sp.wait(m)
            load("ssm", ssm[:, P - 1:P - 1 + L], io["ssm"][:, :])
            m = load("ssm", dskip[:, :], io["skip"].rearrange("(n a) -> n a", a=1))
            dve.wait(m)
            m = dve.then(dve.q.tensor_scalar(ssm[:, P - 1:P], ssm[:, P - 1:P], dskip[:, 0:1], None, ALU.add))
            sp.wait(m)
            kpad = load("ssm", kpad_d[:, :], ssm[:, :])
            sp.wait(kpad)
            ct = io["ctx_rev"].rearrange("(k p) n -> p k n", p=P)
            qd = q3_d[:, :].rearrange("(k p) n -> p k n", p=P)
            toep_read = [(), (), ()]
            kx_free = qx_free = yf_free = ()
            kv_free = [(), ()]
            conv_banks, tr_banks = banks[0:4], banks[4:6]
            x3_free = [(), ()]
            x2l_free = [(), ()]
            out_stored = ()
            for half in range(2):
                cols = slice(half * HT, (half + 1) * HT)
                sp.wait(*kx_free, *qx_free)
                for k in range(KT):
                    got_cr = load("cr", cr[:, k, :], ct[:, k, cols])
                sp.wait(*out_stored)
                for k in range(KT):
                    got_q = load("qo", qo[:, k, :], qd[:, k, cols])
                cv = cr[:, :, :].rearrange("p k (b h i) -> p k b h i", b=HB, i=HR)
                qv = qo[:, :, :].rearrange("p k (b h i) -> p k b h i", b=HB, i=HR)
                for h in range(CH):
                    n = half * CH + h
                    sp.wait(*toep_read[n % 3])
                    row = kpad_d[h:h + 1, :]
                    src = bass.AP(row.tensor, row.offset, [[1, P], [1, L]])
                    got_t = load(f"toep{n % 3}", toep[n % 3][:, :], src)
                    kvn = kv[n % 2]
                    pool.wait(got_cr, *kx_free)
                    pool.q.tensor_copy(kx[:, :, :, 0:8], cv[:, :, :, h, :])
                    pool.then(pool.q.tensor_copy(kx[:, :, :, 8:12], cv[:, :, :, h, 0:4]))
                    pool.wait(*kv_free[n % 2])
                    for d in range(5):
                        w = HR if d < 4 else HR // 2
                        m_kv = pool.mark(pool.q.tensor_tensor(kvn[:, :, :, d * HR:d * HR + w], kx[:, :, :, 0:w],
                                                              kx[:, :, :, d:d + w], ALU.mult))
                    pool.wait(m_kv)
                    kx_free = (m_kv,)
                    dve.wait(got_q, *qx_free)
                    dve.q.tensor_copy(qx[:, :, :, 0:8], qv[:, :, :, h, :])
                    m_qx = dve.mark(dve.q.tensor_copy(qx[:, :, :, 8:15], qv[:, :, :, h, 0:7]))
                    pe.wait(got_t, m_kv)
                    for o in range(KT):
                        t = claim(conv_banks[o])
                        for k in range(o + 1):
                            ins = pe.q.matmul(t[:, 0:HB * NP_], toep[n % 3][:, (o - k) * P:(o - k + 1) * P],
                                              kvn[:, k, :, :].rearrange("p b c -> p (b c)"),
                                              start=(k == 0), stop=(k == o))
                        m_y = pe.mark(ins)
                        y = t[:, 0:HB * NP_].rearrange("p (b c) -> p b c", b=HB)
                        act.wait(m_y, *yf_free)
                        f = yf[:, o]
                        act.q.copy(f[:, :, 0:4, :].rearrange("p b d j -> p b (d j)"), y[:, :, 0:32])
                        for w in range(2):
                            act.q.copy(f[:, :, 4, 4 * w:4 * w + 4], y[:, :, 32:36])
                        for d in range(5, 8):
                            c = 8 - d
                            act.q.copy(f[:, :, d, 0:c], y[:, :, c * 8 + d:c * 8 + 8])
                            m_f = act.mark(act.q.copy(f[:, :, d, c:8], y[:, :, c * 8:c * 8 + 8 - c]))
                        conv_banks[o].read = (m_f,)
                        dve.wait(m_f, m_qx)
                        base = qx[:, o, :, :]
                        win = bass.AP(base.tensor, base.offset, [list(base.ap[0]), [16, HB], [1, 8], [1, 8]])
                        dve.then(dve.q.tensor_tensor(f, f, win, ALU.mult))
                        m_o = dve.then(dve.q.tensor_reduce(qv[:, o, :, h, :], f.rearrange("p b d j -> p b j d"), AX, ALU.add))
                    toep_read[n % 3] = (m_y,)
                    kv_free[n % 2] = (m_y,)
                    yf_free = (m_o,)
                    qx_free = (m_o,)
                for i in range(HT // P):
                    g = half * (HT // P) + i
                    s = i % 2
                    sp.wait(*x2l_free[s])
                    got = load(f"x2l{s}", x2l[s][:, :], x2_d[g * P:(g + 1) * P, :])
                    t = claim(tr_banks[s])
                    pe.wait(m_o)
                    for k in range(KT):
                        ins = pe.q.transpose(t[:, k * P:(k + 1) * P], qo[:, k, i * P:(i + 1) * P], ident[:, :])
                    m = pe.mark(ins)
                    dve.wait(m, got, *x3_free[s])
                    m = dve.mark(dve.q.tensor_tensor(x3[s][:, :], x2l[s][:, :], t[:, :], ALU.add))
                    tr_banks[s].read = x2l_free[s] = (m,)
                    sp.wait(m)
                    st = load(f"x3s{s}", x3_d[g * P:(g + 1) * P, :], x3[s][:, :])
                    x3_free[s] = (st,)
                out_stored = ((pe, pe.count),)
        meet()

        dd = ExitStack()
        with dd:
            def sb(name, shape, dt=F32, ctx=dd):
                return sbuf(ctx, name, shape, dt)

            FT = FF // P
            SPAD = -(-CAP // 8) * 8
            HALF = SPAD // 2
            N7 = ER * TOKT
            NBLK = T // NB
            w1_raw = sb("w1_raw", [P, KT, 2 * FF])
            w2_raw = sb("w2_raw", [P, FT, D])
            w1s = [[sb(f"w1_{i}_{c}", [P, KT, 2 * FF], F32R) for c in "hl"] for i in range(2)]
            w2s = [[sb(f"w2_{i}_{c}", [P, FT, D], F32R) for c in "hl"] for i in range(1)] * 2
            xt = [sb(f"xt_{c}", [P, KT, NB], F32R) for c in "hl"]
            sg = [sb(f"sg{i}", [P, NB]) for i in range(2)]
            pr = sb("pr", [P, NB])
            at = [sb(f"at_{c}", [P, FT, NB], F32R) for c in "hl"]
            gw = [sb(f"gw_{c}", [P, KT, ER], F32R) for c in "hl"]
            raw_free, w_free, xt_free, at_free = (), [(), ()], (), ()
            w2_free = ()
            pr_free = ()
            sg_free = [(), ()]
            w_order = [(io["shared_w1"], io["shared_w2"])] + [(io["routed_w1"][e], io["routed_w2"][e]) for e in range(ER)]
            split_done = {}

            def split(src, parts, ready, free=()):
                act.wait(*ready, *free)
                m = act.mark(act.q.copy(parts[0], src))
                dve.wait(m, *ready)
                return dve.mark(dve.q.tensor_tensor(parts[1], src, parts[0].bitcast(F32), ALU.subtract))

            def expert_weights(n):
                nonlocal raw_free
                s = n % 2
                a, c = w_order[n]
                sp.wait(*raw_free)
                load("wraw", w1_raw[:, :, :], a.rearrange("(k p) n -> p k n", p=P))
                got = load("wraw", w2_raw[:, :, :], c.rearrange("(k p) n -> p k n", p=P))
                for k in range(KT):
                    m = split(w1_raw[:, k, :], [w[:, k, :] for w in w1s[s]], (got,), w_free[s])
                    yield
                for f in range(FT):
                    m = split(w2_raw[:, f, :], [w[:, f, :] for w in w2s[s]], (got,), w2_free)
                    yield
                split_done[n] = m
                raw_free = (m,)

            def product(out, lhs, rhs, first, last):
                pe.q.matmul(out, lhs[0], rhs[0], start=first, stop=False)
                pe.q.matmul(out, lhs[0], rhs[1], start=False, stop=False)
                return pe.q.matmul(out, lhs[1], rhs[0], start=False, stop=last)

            def ffn_hidden(n, c0, w, ready):
                nonlocal pr_free
                s = n % 2
                pe.wait(split_done[n], *ready)
                for f in range(FT):
                    for half_, bank in ((1, banks[2 * f + 1]), (0, banks[2 * f])):
                        t = claim(bank)
                        for k in range(KT):
                            cols = slice(half_ * FF + f * P, half_ * FF + (f + 1) * P)
                            ins = product(t[:, 0:w], [p[:, k, cols] for p in w1s[s]],
                                          [p[:, k, c0:c0 + w] for p in xt], k == 0, k == KT - 1)
                        m = pe.mark(ins)
                        if half_:
                            act.wait(m, *sg_free[f])
                            ms = act.mark(act.q.activation(sg[f][:, 0:w], t[:, 0:w], ACT.Silu))
                            bank.read = (ms,)
                        yield
                    dve.wait(m, ms, *pr_free)
                    mp = dve.then(dve.q.tensor_tensor(pr[:, 0:w], sg[f][:, 0:w], t[:, 0:w], ALU.mult))
                    banks[2 * f].read = sg_free[f] = (mp,)
                    m = split(pr[:, 0:w], [p[:, f, c0:c0 + w] for p in at], (mp,), at_free)
                    pr_free = (m,)
                yield m

            tok = ExitStack()
            with tok:
                rows = sb("rows", [P, TOKT, D + 8], ctx=tok)
                aff = sb("aff", [P, TOKT, ER], ctx=tok)
                rk = ExitStack()
                x3i = [sb(f"x3d{i}", [P, D], ctx=tok) for i in range(3)]
                lg_t = sb("lg_t", [ER, NB], ctx=tok)
                fill = sb("fill", [P, D + 8], ctx=tok)
                before = sb("before", [P, ER, ER], ctx=tok)
                rank = sb("rank", [P, TOKT, ER], ctx=tok)
                mask = sb("mask", [P, TOKT, ER], ctx=tok)
                gt = sb("gt", [P, 8, ER, ER], ctx=tok)
                tmp = sb("tmp", [P, TOKT, ER], ctx=tok)
                score = sb("score", [P, ER, TOKT], ctx=tok)
                thr = sb("thr", [P, ER], ctx=tok)
                cand = sb("cand", [P, ER], ctx=tok)
                hit = sb("hit", [P, ER, TOKT], ctx=tok)
                over = sb("over", [P, ER, TOKT], ctx=tok)
                cnt = sb("cnt", [P, ER], ctx=tok)
                keep = sb("keep", [P, ER], ctx=tok)
                earlier = sb("earlier", [P, P], ctx=tok)
                ones = sb("ones", [P, P], ctx=tok)
                tot = sb("tot", [P, ER, TOKT], ctx=tok)
                scan = sb("scan", [P, ER, TOKT], ctx=tok)
                zero = sb("zero", [P, TOKT], ctx=tok)
                base = sb("base", [P, ER], ctx=tok)
                slot_f = sb("slot_f", [P, 2, TOKT], ctx=tok)
                slot = sb("slot", [P, 2, TOKT], I32, ctx=tok)
                gw_raw = sb("gw_raw", [P, KT, ER], ctx=tok)
                eb = sb("eb", [P, ER], ctx=tok)

                dve.q.memset(zero[:, :], 0.0)
                dve.q.memset(ones[:, :], 1.0)
                dve.q.memset(earlier[:, :], 1.0)
                dve.q.memset(fill[:, :], 0.0)
                m = dve.then(dve.q.memset(before[:, :, :], 1.0))
                pool.wait(m)
                pool.q.affine_select(out=earlier[:, :], in_=earlier[:, :], compare_op=ALU.is_gt, fill=0.0, base=0,
                                     pattern=[[1, P]], channel_multiplier=-1)
                pool.q.affine_select(out=before[:, :, :], in_=before[:, :, :], compare_op=ALU.is_gt,
                                     fill=0.0, base=0, pattern=[[1, ER], [-1, ER]], channel_multiplier=0)
                BIG = 1 << 20
                pool.q.iota(base[:, :], pattern=[[SPAD, ER]], base=-BIG, channel_multiplier=0,
                            allow_small_or_imprecise_dtypes=True)
                pool.q.iota(fill[:, D:D + 1].bitcast(I32), pattern=[[0, 1]], base=T, channel_multiplier=1)
                consts = pool.mark(pool.q.iota(rows[:, :, D:D + 1].bitcast(I32), pattern=[[P, TOKT], [0, 1]], base=0,
                                               channel_multiplier=1))
                pe.wait(consts)
                dve.wait(consts)
                act.wait(consts)
                sp.wait(consts)
                for s0 in range(0, ER * SPAD, P):
                    n = min(P, ER * SPAD - s0)
                    filled = load("fill", slots_d[s0:s0 + n, :], fill[0:n, :])
                filled = load("fill", io["out"][T:T + P, :], fill[:, 0:D])
                load("gw", gw_raw[:, :, :], io["gate_w"].rearrange("(k p) n -> p k n", p=P))
                got_gw = load("gw", eb[:, :], io["expert_bias"].rearrange("(a n) -> a n", a=1).broadcast_to([P, ER]))
                gw_ready = split(gw_raw[:, :, :], [p[:, :, :] for p in gw], (got_gw,))
                for _ in expert_weights(0):
                    pass

                def transposed(i, j, ready):
                    bank = banks[4 + i % 2]
                    t = claim(bank)
                    pe.wait(*ready)
                    for k in range(KT):
                        ins = pe.q.transpose(t[:, k * P:(k + 1) * P], rows[:, i, k * P:(k + 1) * P], ident[:, :])
                    m = pe.mark(ins)
                    v = t[:, :].rearrange("p (k n) -> p k n", k=KT)
                    m = split(v, [p[:, :, j * P:(j + 1) * P] for p in xt], (m,), xt_free)
                    bank.read = (m,)
                    return m

                b_lg, b_lt = banks[7], banks[6]
                lgt = claim(b_lg)
                x3_free = [(), (), ()]
                lt_done = ()
                for blk in range(NBLK):
                    for j in range(BLK):
                        i = blk * BLK + j
                        sp.wait(*x3_free[i % 3])
                        gx = load(f"x3l{i % 3}", x3i[i % 3][:, :], x3_d[i * P:(i + 1) * P, :])
                        ln = layernorm(x3i[i % 3][:, :].unsqueeze(1), rows[:, i:i + 1, 0:D], 1, (gx,))
                        x3_free[i % 3] = (ln,)
                        m = transposed(i, j, (ln,))
                    t = claim(b_lt)
                    pe.wait(m, gw_ready)
                    for k in range(KT):
                        ins = product(t[0:ER, :], [p[:, k, :] for p in gw], [p[:, k, :] for p in xt], k == 0, k == KT - 1)
                    m = pe.mark(ins)
                    xt_free = (m,)
                    act.wait(m, *lt_done)
                    m = act.mark(act.q.copy(lg_t[:, :], t[0:ER, :]))
                    b_lt.read = (m,)
                    pe.wait(m)
                    for j in range(BLK):
                        i = blk * BLK + j
                        ins = pe.q.transpose(lgt[:, i * ER:(i + 1) * ER], lg_t[:, j * P:(j + 1) * P], ident[0:ER, 0:ER])
                    m_lg = pe.mark(ins)
                    lt_done = (m_lg,)

                def route():
                    dve.wait(m_lg, got_gw)
                    m = dve.mark(dve.q.tensor_tensor(
                        aff[:, :, :], lgt[:, 0:N7].rearrange("p (t n) -> p t n", n=ER),
                        eb[:, :].unsqueeze(1).broadcast_to([P, TOKT, ER]), ALU.add))
                    b_lg.read = (m,)
                    act.wait(m)
                    m = act.mark(act.q.activation(aff[:, :, :], aff[:, :, :], ACT.Exp, scale=-1.0))
                    dve.wait(m)
                    dve.then(dve.q.tensor_scalar(aff[:, :, :], aff[:, :, :], 1.0, None, ALU.add))
                    dve.then(dve.q.reciprocal(aff[:, :, :], aff[:, :, :]))
                    yield
                    for c in range(0, TOKT, 8):
                        full = [P, 8, ER, ER]
                        mine = aff[:, c:c + 8, :].unsqueeze(3).broadcast_to(full)
                        other = aff[:, c:c + 8, :].unsqueeze(2).broadcast_to(full)
                        dve.then(dve.q.tensor_tensor(gt[:, :, :, :], other, mine, ALU.is_equal))
                        dve.then(dve.q.tensor_tensor(gt[:, :, :, :], gt[:, :, :, :],
                                                     before[:, :, :].unsqueeze(1).broadcast_to(full), ALU.mult))
                        dve.then(dve.q.tensor_reduce(rank[:, c:c + 8, :], gt[:, :, :, :], AX, ALU.add))
                        dve.then(dve.q.tensor_tensor(gt[:, :, :, :], other, mine, ALU.is_gt))
                        dve.then(dve.q.tensor_reduce(tmp[:, c:c + 8, :], gt[:, :, :, :], AX, ALU.add))
                        yield
                    dve.then(dve.q.tensor_tensor(rank[:, :, :], rank[:, :, :], tmp[:, :, :], ALU.add))
                    dve.then(dve.q.tensor_scalar(mask[:, :, :], rank[:, :, :], 1.5, None, ALU.is_lt))
                    dve.then(dve.q.tensor_tensor(tmp[:, :, :], aff[:, :, :], mask[:, :, :], ALU.mult))
                    dve.then(dve.q.scalar_tensor_tensor(score[:, :, :].rearrange("p e t -> p t e"), mask[:, :, :], -1.0,
                                                        tmp[:, :, :], ALU.add, ALU.add))
                    dve.then(dve.q.memset(thr[:, :], 0.0))
                    yield

                    def per_expert(a):
                        return a[:, :].unsqueeze(2).broadcast_to([P, ER, TOKT])

                    def flat(a):
                        return a[:, :, :].rearrange("p e t -> p (e t)")

                    def count(limit, op, into):
                        dve.then(dve.q.tensor_tensor(into[:, :, :], score[:, :, :], per_expert(limit), op))
                        m = dve.then(dve.q.tensor_reduce(cnt[:, :], into[:, :, :], AX, ALU.add))
                        t = claim(b_lg)
                        pe.wait(m)
                        m = pe.mark(pe.q.matmul(t[:, 0:ER], ones[:, :], cnt[:, :], start=True, stop=True))
                        return t, m

                    for bit in range(29, -1, -1):
                        dve.then(dve.q.tensor_scalar(cand[:, :].bitcast(I32), thr[:, :].bitcast(I32), 1 << bit, None,
                                                     ALU.bitwise_or))
                        t, m = count(cand, ALU.is_ge, hit)
                        yield
                        dve.wait(m)
                        m = dve.then(dve.q.tensor_scalar(keep[:, :], t[:, 0:ER], float(CAP) - 0.5, None, ALU.is_gt))
                        b_lg.read = (m,)
                        dve.then(dve.q.copy_predicated(thr[:, :], keep[:, :].bitcast(I32), cand[:, :]))
                    t, m = count(thr, ALU.is_gt, over)
                    yield
                    dve.wait(m)
                    m = dve.then(dve.q.tensor_scalar(keep[:, :], t[:, 0:ER], -1.0, float(CAP) - 0.5, ALU.mult, ALU.add))
                    b_lg.read = (m,)
                    m = dve.then(dve.q.tensor_tensor(hit[:, :, :], score[:, :, :], per_expert(thr), ALU.is_equal))

                    def positions(of, m):
                        t = claim(b_lg)
                        pe.wait(m)
                        pe.q.matmul(t[:, 0:N7], ones[:, :], flat(of), start=True, stop=True)
                        m = pe.mark(pe.q.matmul(t[:, N7:2 * N7], earlier[:, :], flat(of), start=True, stop=True))
                        yield
                        dve.wait(m)
                        dve.then(dve.q.tensor_copy(flat(tot), t[:, 0:N7]))
                        for e in range(ER):
                            m = dve.mark(dve.q.tensor_tensor_scan(scan[:, e, :], tot[:, e, :], zero[:, :], 0.0,
                                                                  ALU.add, ALU.add))
                        dve.wait(m)
                        dve.then(dve.q.tensor_tensor(flat(scan), flat(scan), flat(tot), ALU.subtract))
                        m = dve.then(dve.q.tensor_tensor(flat(scan), flat(scan), t[:, N7:2 * N7], ALU.add))
                        b_lg.read = (m,)

                    yield from positions(hit, m)
                    dve.then(dve.q.tensor_tensor(scan[:, :, :], scan[:, :, :], per_expert(keep), ALU.is_lt))
                    dve.then(dve.q.tensor_tensor(scan[:, :, :], scan[:, :, :], hit[:, :, :], ALU.mult))
                    dve.then(dve.q.tensor_tensor(over[:, :, :], over[:, :, :], scan[:, :, :], ALU.add))
                    m = dve.then(dve.q.tensor_tensor(over[:, :, :], over[:, :, :],
                                                     mask[:, :, :].rearrange("p t e -> p e t"), ALU.mult))
                    kept = over[:, :, :].rearrange("p e t -> p t e")
                    dve.then(dve.q.tensor_tensor(rows[:, :, D + 1:D + 1 + ER], aff[:, :, :], kept, ALU.mult))
                    yield from positions(over, m)
                    dve.then(dve.q.tensor_tensor(scan[:, :, :], scan[:, :, :], per_expert(base), ALU.add))
                    dve.then(dve.q.tensor_tensor(scan[:, :, :], scan[:, :, :], over[:, :, :], ALU.mult))
                    for c in range(2):
                        dve.then(dve.q.tensor_scalar(tmp[:, :, :], rank[:, :, :], float(c), None, ALU.is_equal))
                        dve.then(dve.q.tensor_tensor(tmp[:, :, :], tmp[:, :, :],
                                                     scan[:, :, :].rearrange("p e t -> p t e"), ALU.mult))
                        dve.then(dve.q.tensor_reduce(slot_f[:, c, :], tmp[:, :, :], AX, ALU.add))
                    dve.then(dve.q.tensor_scalar(slot_f[:, :, :], slot_f[:, :, :], float(BIG), None, ALU.add))
                    m = dve.then(dve.q.tensor_copy(slot[:, :, :], slot_f[:, :, :]))
                    pool.wait(m, filled)
                    yield
                    for i in range(TOKT):
                        for c in range(2):
                            state["scattered"] = load("scatter", None, None, pool, ins=pool.q.indirect_dma_start(
                                out=slots_d[:, :],
                                out_offset=bass.IndirectOffsetOnAxis(ap=slot[:, c, i:i + 1].bitcast(U32), axis=0),
                                in_=rows[:, i, :], in_offset=None, bounds_check=ER * SPAD - 1, oob_is_err=False))
                        yield

                def shared():
                    nonlocal xt_free, at_free
                    for blk in range(NBLK):
                        for j in range(BLK):
                            m = transposed(blk * BLK + j, j, ())
                            yield
                        for m in ffn_hidden(0, 0, NB, (m,)):
                            yield
                        xt_free = ((pe, pe.count),)
                        for j in range(BLK):
                            i = blk * BLK + j
                            sp.wait(*x3_free[i % 3])
                            gx = load(f"x3l{i % 3}", x3i[i % 3][:, :], x3_d[i * P:(i + 1) * P, :])
                            bank = banks[2 * (j % 2)]
                            t = claim(bank)
                            pe.wait(m)
                            for f in range(FT):
                                ins = product(t[:, :], [p[:, f, j * P:(j + 1) * P] for p in at],
                                              [p[:, f, :] for p in w2s[0]], f == 0, f == FT - 1)
                            mm = pe.mark(ins)
                            dve.wait(mm, gx)
                            mo = dve.mark(dve.q.tensor_tensor(x3i[i % 3][:, :], x3i[i % 3][:, :], t[:, :], ALU.add))
                            bank.read = (mo,)
                            sp.wait(mo)
                            st = load(f"xo{i % 3}", io["out"][i * P:(i + 1) * P, :], x3i[i % 3][:, :])
                            x3_free[i % 3] = (st,)
                            yield
                        at_free = ((pe, pe.count),)
                    for st in x3_free:
                        state["out_stored"] = state.get("out_stored", ()) + tuple(st)
                    w_free[0] = ((pe, pe.count),)

                run_together((route(), 75.0), (shared(), 90.0))
                w2_free = at_free
                for _ in expert_weights(1):
                    pass
            meet()

            ex_ = ExitStack()
            with ex_:
                NT = -(-SPAD // P)
                xg = [sb(f"xg{i}", [P, D + 8], ctx=ex_) for i in range(2 * NT)]
                yg = [sb(f"yg{i}", [P, D], ctx=ex_) for i in range(3)]
                xt = [sb(f"xte_{c}", [P, KT, SPAD], F32R, ctx=ex_) for c in "hl"]
                at = [sb(f"ate_{c}", [P, FT, SPAD], F32R, ctx=ex_) for c in "hl"]
                xg_free = [() for _ in xg]
                yg_free = [(), (), ()]
                xt_free = at_free = ()
                got_g = {}
                added = ()

                def fetch(e):
                    for i in range(NT):
                        n = min(P, SPAD - i * P)
                        q = (e % 2) * NT + i
                        sp.wait(*xg_free[q])
                        got_g[e, i] = load(f"xg{q}", xg[q][0:n, :], slots_d[e * SPAD + i * P:e * SPAD + i * P + n, :])

                fetch(0)
                for e in range(ER):
                    if e + 1 < ER:
                        fetch(e + 1)
                    for i in range(NT):
                        n = min(P, SPAD - i * P)
                        q = (e % 2) * NT + i
                        bank = banks[4 + i % 2]
                        t = claim(bank)
                        pe.wait(got_g[e, i])
                        for k in range(KT):
                            ins = pe.q.transpose(t[:, k * P:k * P + n], xg[q][0:n, k * P:(k + 1) * P], ident[0:n, 0:n])
                        m = pe.mark(ins)
                        v = t[:, :].rearrange("p (k n) -> p k n", k=KT)[:, :, 0:n]
                        m = split(v, [p[:, :, i * P:i * P + n] for p in xt], (m,), xt_free)
                        bank.read = (m,)
                    nxt = expert_weights(e + 2) if e + 2 <= ER else iter(())
                    for c in range(2):
                        for m in ffn_hidden(e + 1, c * HALF, HALF, (m,)):
                            pass
                    xt_free = w_free[(e + 1) % 2] = ((pe, pe.count),)
                    for i in range(NT):
                        n = min(P, SPAD - i * P)
                        q = (e % 2) * NT + i
                        bank = banks[6 + i % 2]
                        t = claim(bank)
                        pe.wait(m)
                        for f in range(FT):
                            ins = product(t[0:n, :], [p[:, f, i * P:i * P + n] for p in at],
                                          [p[:, f, :] for p in w2s[0]], f == 0, f == FT - 1)
                        mm = pe.mark(ins)
                        y = yg[i % 3]
                        dve.wait(mm, *yg_free[i % 3])
                        mo = dve.mark(dve.q.tensor_scalar(y[0:n, :], t[0:n, :], xg[q][0:n, D + 1 + e:D + 2 + e], None, ALU.mult))
                        bank.read = (mo,)
                        pool.wait(mo, *added)
                        ad = load(f"add{i % 3}", None, None, pool, ins=pool.q.indirect_dma_start(
                            out=io["out"][:, :],
                            out_offset=bass.IndirectOffsetOnAxis(ap=xg[q][0:n, D:D + 1].bitcast(U32), axis=0),
                            in_=y[0:n, :], in_offset=None, bounds_check=T + P - 1, oob_is_err=True, compute_op=ALU.add))
                        yg_free[i % 3] = (ad,)
                        xg_free[q] = (ad,)
                    added = tuple(a for s in yg_free for a in s)
                    at_free = w2_free = ((pe, pe.count),)
                    for _ in nxt:
                        pass
        meet()


def kernel(**inputs):
    import numpy as np
    import concourse.bacc as bacc
    from concourse.bass_utils import run_bass_kernel_spmd

    a = {k: np.asarray(v) for k, v in inputs.items()}
    B, S, D = a["x"].shape
    T = B * S
    NH = a["L0_xattn_bi"].shape[0]
    ctx = a["ctx_2048"].reshape(T, D)
    ctx_t = np.ascontiguousarray(ctx.T)
    arrays = {
        "x": a["x"].reshape(T, D),
        "ctx_t": ctx_t,
        "ctx_rev": np.ascontiguousarray(ctx_t.reshape(D // 128, 128, T)[:, ::-1, :]).reshape(D, T),
        "ctx_v": np.concatenate([ctx.reshape(T, NH, D // NH), np.ones((T, NH, 1), ctx.dtype)], axis=2).reshape(T, -1),
        "w_if": np.concatenate([a["L0_xattn_Wi"], a["L0_xattn_Wf"]], axis=1),
        "bi": a["L0_xattn_bi"], "bf": a["L0_xattn_bf"], "ln_scale": a["L0_xattn_ln_scale"],
        "gate_weight_t": np.ascontiguousarray(a["L0_ffn_gate_weight"].T),
        "gate_up_t": np.ascontiguousarray(a["L0_ffn_gate_up_proj"].transpose(0, 2, 1)),
        "down_t": np.ascontiguousarray(a["L0_ffn_down_proj"].transpose(0, 2, 1)),
        "merge": a["L0_ffn_merge_groups"], "dominant": a["L0_ffn_dominant_experts"],
        "ssm": a["L1_xattn_ssm_kernel"], "skip": a["L1_xattn_D"],
        "gate_w": a["L1_ffn_gate_w"], "expert_bias": a["L1_ffn_expert_bias"],
        "shared_w1": a["L1_ffn_shared_w1"][0], "shared_w2": a["L1_ffn_shared_w2"][0],
        "routed_w1": a["L1_ffn_routed_w1"], "routed_w2": a["L1_ffn_routed_w2"],
    }
    arrays = {k: np.ascontiguousarray(v) for k, v in arrays.items()}
    nc = bacc.Bacc("TRN2", target_bir_lowering=False, num_devices=1)
    io = {k: nc.dram_tensor("in_" + k, list(v.shape), mybir.dt.from_np(v.dtype), kind="ExternalInput").ap()
          for k, v in arrays.items()}
    io["out"] = nc.dram_tensor("out_x", [T + 128, D], F32, kind="ExternalOutput").ap()
    shapes = {k: v.shape for k, v in arrays.items()}
    shapes["x"] = (B, S, D)
    shapes["gate_weight"] = a["L0_ffn_gate_weight"].shape
    build_program(nc, io, shapes)
    r = run_bass_kernel_spmd(nc, [{"in_" + k: v for k, v in arrays.items()}], core_ids=[0])
    return r.results[0]["out_x"][:T].reshape(B, S, D)
```

```python
import itertools
from contextlib import ExitStack

import concourse.bass as bass
from concourse import mybir

F32 = mybir.dt.float32
BF16 = mybir.dt.bfloat16
I32 = mybir.dt.int32
U32 = mybir.dt.uint32
F32R = mybir.dt.float32r
ALU = mybir.AluOpType
ACT = mybir.ActivationFunctionType
AX = mybir.AxisListType.X

P = 128
BANK = 512


class Producer:

    def __init__(self, sem, by):
        self.sem, self.by, self.count = sem, by, 0

    def mark(self, ins):
        ins.then_inc(self.sem, self.by)
        self.count += self.by
        return (self, self.count)


class Engine(Producer):

    def __init__(self, queue, sem):
        super().__init__(sem, 1)
        self.q, self.seen = queue, {}

    def wait(self, *marks):
        for source, count in marks:
            if self.seen.get(id(source), 0) < count:
                self.q.wait_ge(source.sem, count)
                self.seen[id(source)] = count

    def then(self, ins):
        m = self.mark(ins)
        self.wait(m)
        return m


class Bank:

    def __init__(self, tensor):
        self.t, self.read = tensor, ()


def run_together(*parts):
    live = [[g, n, 0] for g, n in parts]
    while live:
        live.sort(key=lambda r: r[2] / r[1])
        r = live[0]
        try:
            next(r[0])
            r[2] += 1
        except StopIteration:
            live.remove(r)


def build_program(nc, io, shapes):
    B, S, D = shapes["x"]
    T = B * S
    KT = D // P
    NH = shapes["bi"][0]
    DH = D // NH
    NE, NG = shapes["gate_weight"][0], shapes["dominant"][0]
    FI = shapes["down_t"][1]
    JT = NG * FI // P
    CH, L = shapes["ssm"]
    HR = S // CH
    ER = shapes["gate_w"][1]
    FF = shapes["shared_w2"][0]
    CAP = max(1, int(1.0 * T / ER))
    TOKT = T // P
    ST = S // P
    BLK = 4
    NB = BLK * P
    EPS_LN, EPS_X = 1e-5, 1e-6
    ones_col = DH
    VW = DH + 1

    main = ExitStack()
    with main:
        def semaphore(name):
            return main.enter_context(nc.semaphore(name))

        pe = Engine(nc.tensor, semaphore("pe_progress"))
        dve = Engine(nc.vector, semaphore("dve_progress"))
        act = Engine(nc.scalar, semaphore("act_progress"))
        pool = Engine(nc.gpsimd, semaphore("pool_progress"))
        sp = Engine(nc.sync, semaphore("sp_progress"))
        engines = (pe, dve, act, pool, sp)

        lanes = {}

        def lane(name):
            if name not in lanes:
                lanes[name] = Producer(semaphore("dma_" + name), 16)
            return lanes[name]

        def load(name, out, in_, queue=sp, ins=None):
            return lane(name).mark(queue.q.dma_start(out, in_) if ins is None else ins)

        psum = main.enter_context(nc.psum_tensor("psum", [P, 8 * BANK], F32))
        banks = [Bank(psum[:, i * BANK:(i + 1) * BANK]) for i in range(8)]

        def claim(bank):
            pe.wait(*bank.read)
            return bank.t

        def meet():
            marks = [(e, e.count) for e in engines if e.count] + [(l, l.count) for l in lanes.values()]
            for e in engines:
                e.wait(*marks)

        x2_d = nc.dram_tensor("x2_scratch", [T, D], F32)
        q3_d = nc.dram_tensor("xn3_t_scratch", [D, T], F32)
        xn2_d = nc.dram_tensor("xn2_scratch", [T, D], F32)
        x3_d = nc.dram_tensor("x3_scratch", [T, D], F32)
        slots_d = nc.dram_tensor("slots_scratch", [ER * (-(-CAP // 8) * 8), D + 8], F32)
        kpad_d = nc.dram_tensor("ssm_padded_scratch", [CH, P - 1 + L + 1], F32)

        def sbuf(ctx, name, shape, dt=F32):
            return ctx.enter_context(nc.sbuf_tensor(name, shape, dt))

        ident = sbuf(main, "ident", [P, P])
        ident_b = sbuf(main, "ident_b", [P, P], BF16)
        minus_half = sbuf(main, "minus_half", [P, 2 * NH])
        m_c = dve.then(dve.q.memset(ident[:, :], 0.0))
        m_c = dve.mark(dve.q.memset(minus_half[:, :], -0.5))
        pool.wait(m_c)
        consts = pool.then(pool.q.affine_select(out=ident[:, :], in_=ident[:, :], compare_op=ALU.not_equal,
                                                fill=1.0, base=0, pattern=[[-1, P]], channel_multiplier=1))
        pe.wait(consts)

        bn = sbuf(main, "bn", [P, BLK, 6])
        mv = sbuf(main, "mv", [P, BLK, 2])
        rstd = sbuf(main, "rstd", [P, BLK])

        def layernorm_steps(src, dst, n, ready, dst_free=()):
            dve.wait(*ready)
            for i in range(n):
                dve.then(dve.q.bn_stats(bn[:, i, :], src[:, i, :]))
            for i in range(n):
                dve.then(dve.q.bn_aggr(mv[:, i, :], bn[:, i, :]))
            m = dve.then(dve.q.tensor_scalar(rstd[:, 0:n], mv[:, 0:n, 1], EPS_LN, None, ALU.add))
            pool.wait(m)
            m = pool.mark(pool.q.tensor_tensor(rstd[:, 0:n], rstd[:, 0:n], minus_half[:, 0:n], ALU.pow))
            yield
            dve.wait(m, *dst_free)
            for i in range(n):
                m = dve.mark(dve.q.tensor_scalar(dst[:, i, :], src[:, i, :], mv[:, i, 0:1],
                                                 rstd[:, i:i + 1], ALU.subtract, ALU.mult))
            dve.wait(m)
            return m

        def layernorm(*args):
            steps = layernorm_steps(*args)
            while True:
                try:
                    next(steps)
                except StopIteration as done:
                    return done.value

        def to_features(src_tile, dst, bank, evac, ready, dst_free=()):
            t = claim(bank)
            pe.wait(*ready)
            for k in range(KT):
                ins = pe.q.transpose(t[:, k * P:(k + 1) * P], src_tile[:, k * P:(k + 1) * P], ident[:, :])
            m = pe.mark(ins)
            evac.wait(m, *dst_free)
            v = t[:, :].rearrange("p (k n) -> p k n", k=KT)
            ins = (evac.q.tensor_copy(dst, v) if evac is dve else evac.q.copy(dst, v))
            m = evac.mark(ins)
            bank.read = (m,)
            return m

        def split(src, parts, ready, free=()):
            act.wait(*ready, *free)
            m = act.mark(act.q.copy(parts[0], src))
            dve.wait(m, *ready)
            return dve.mark(dve.q.tensor_tensor(parts[1], src, parts[0].bitcast(F32), ALU.subtract))

        def product(out, lhs, rhs, first, last):
            pe.q.matmul(out, lhs[0], rhs[0], start=first, stop=False)
            pe.q.matmul(out, lhs[0], rhs[1], start=False, stop=False)
            return pe.q.matmul(out, lhs[1], rhs[0], start=False, stop=last)

        GH = NG // 2
        JH = GH * FI // P
        NV = NH * VW
        both = ExitStack()
        with both:
            def sb(name, shape, dt=F32, ctx=both):
                return sbuf(ctx, name, shape, dt)

            dom = sb("dom", [1, NG], I32)
            w_gate = [sb(f"w_gate_{c}", [P, KT, GH * FI], F32R) for c in "hl"]
            w_up = [sb(f"w_up_{c}", [P, KT, GH * FI], F32R) for c in "hl"]
            w_down = [sb(f"w_down_{c}", [P, JH, D], F32R) for c in "hl"]
            of_group = sb("of_group", [3 * NE, NG, FI], BF16)
            sel = sb("sel", [3 * NE, T], BF16)
            xn_t = [sb(f"xn_t_{c}", [P, KT, S], F32R) for c in "hl"]
            xn2 = sb("xn2", [P, ST, D])
            th = [sb(f"th{i}", [P, S]) for i in range(2)]
            a_t = [sb(f"a_t_{c}", [P, JH, S], F32R) for c in "hl"]
            b_misc, b_m, b_qk0, b_qk1, b_h, b_gu0, b_gu1, b_down = banks
            free = {"xn_t": (), "a_t": (), "th": [(), ()], "w": (), "xn2": ()}
            gu = io["gate_up_t"].rearrange("e (k p) n -> e p k n", p=P)
            x2v = x2_d[:, :].rearrange("(b t p) d -> b p t d", p=P, t=ST)
            xn2v = xn2_d[:, :].rearrange("(b t p) d -> b p t d", p=P, t=ST)

            def half_weights(half, stages):
                sp.wait(got_dom)
                n_stage = itertools.count()
                for gl in range(GH):
                    g = half * GH + gl
                    e = sp.q.value_load(dom[0:1, g:g + 1], min_val=0, max_val=NE - 1)
                    expert_of[gl] = e
                    s = next(n_stage) % len(stages)
                    sp.wait(*stage_read[s])
                    v = stages[s].rearrange("p (k n) -> p k n", k=KT)
                    got = load(f"stage{s}", v, gu[bass.ds(e, 1)].rearrange("a p k n -> (a p) k n"))
                    for w, c in ((w_gate, 0), (w_up, FI)):
                        cols = slice(gl * FI, (gl + 1) * FI)
                        m = split(v[:, :, c:c + FI], [p[:, :, cols] for p in w], (got,), free["w"])
                    stage_read[s] = (m,)
                    yield
                per = KT * 2 * FI // D
                for j0 in range(0, JH, per):
                    s = next(n_stage) % len(stages)
                    sp.wait(*stage_read[s])
                    v = stages[s].rearrange("p (j n) -> p j n", n=D)
                    for row in range(j0 * P, (j0 + per) * P):
                        if row % P == 0 or row % FI == 0:
                            n = min(P - row % P, FI - row % FI)
                            dn = io["down_t"][bass.ds(expert_of[row // FI], 1)].rearrange("a i d -> (a i) d")
                            got = load(f"stage{s}", v[row % P:row % P + n, row // P - j0, :],
                                       dn[row % FI:row % FI + n, :])
                    m = split(v, [p[:, j0:j0 + per, :] for p in w_down], (got,), free["w"])
                    stage_read[s] = (m,)
                    yield
                return m

            expert_of = {}
            stage_read = [()] * 4
            weights_ready = {}

            def merged_ffn(b, half, ready):
                ogr = of_group[:, :, :].rearrange("e g i -> e (g i)")
                m_a = []
                for jl in range(JH):
                    J = half * JH + jl
                    cols = slice(jl * P, (jl + 1) * P)
                    b_gu = (b_gu0, b_gu1)[jl % 2]
                    t4, t5 = claim(b_gu)[:, 0:S], b_gu.t[:, S:2 * S]
                    pe.wait(weights_ready[half], *ready)
                    for t, w in ((t4, w_gate), (t5, w_up)):
                        for k in range(KT):
                            ins = product(t, [p[:, k, cols] for p in w], [p[:, k, :] for p in xn_t], k == 0, k == KT - 1)
                    m_up = pe.mark(ins)
                    t6 = claim(b_misc)[:, 0:S]
                    m_w = pe.mark(pe.q.matmul(t6, ogr[:, J * P:(J + 1) * P], sel[:, b * S:(b + 1) * S],
                                              start=True, stop=True))
                    tj = th[jl % 2]
                    act.wait(m_up, *free["th"][jl % 2])
                    m = act.mark(act.q.activation(tj[:, :], t4, ACT.Tanh, scale=0.5))
                    dve.wait(m)
                    m = dve.then(dve.q.scalar_tensor_tensor(tj[:, :], tj[:, :], 1.0, t4, ALU.add, ALU.mult))
                    m = dve.then(dve.q.tensor_tensor(tj[:, :], tj[:, :], t5, ALU.mult))
                    b_gu.read = (m,)
                    dve.wait(m_w)
                    m = dve.then(dve.q.scalar_tensor_tensor(tj[:, :], tj[:, :], 0.5, t6, ALU.mult, ALU.mult))
                    b_misc.read = (m,)
                    m_a.append(split(tj[:, :], [p[:, jl, :] for p in a_t], (m,), free["a_t"]))
                    free["th"][jl % 2] = (m_a[-1],)
                    yield None
                free["xn_t"] = (m_up,)
                for i in range(ST):
                    bank = (b_down, b_gu0)[i % 2]
                    t7 = claim(bank)
                    for jl in range(JH):
                        pe.wait(m_a[jl])
                        ins = product(t7[:, :], [p[:, jl, i * P:(i + 1) * P] for p in a_t],
                                      [p[:, jl, :] for p in w_down], jl == 0, jl == JH - 1)
                    yield bank, pe.mark(ins)
                free["a_t"] = ((pe, pe.count),)

            one = ExitStack()
            with one:
                def sb1(name, shape, dt=F32):
                    return sbuf(one, name, shape, dt)

                GW = 32 + NH
                w_if = [sb1(f"w_if_{c}", [P, 2, KT, GW], F32R) for c in "hl"]
                b_if = sb1("b_if", [GW, 1])
                ln_s = sb1("ln_s", [P, D])
                w_router = [sb1(f"w_router_{c}", [P, KT, NE], F32R) for c in "hl"]
                merge_i = sb1("merge_i", [3 * NE, 1], I32)
                merge_f = sb1("merge_f", [3 * NE, 1])
                head_of = sb1("head_of", [3 * 32, NH], BF16)
                zero = sb1("zero_f", [NH, S])

                x_t = [sb1(f"x_t{i}", [P, ST, D]) for i in range(3)]
                c_raw = sb1("c_raw", [P, KT, S])
                c_t = [sb1(f"c_t_{c}", [P, KT, S], F32R) for c in "hl"]
                q_t = [sb1(f"q_t_{c}", [P, KT, S], F32R) for c in "hl"]
                v_raw = sb1("v_raw", [P, ST, NV])
                v3 = [sb1(f"v3_{c}", [P, ST, NV], BF16) for c in "hml"]
                xn = xn2
                fg = sb1("fg", [NH, S])
                ig = sb1("ig", [NH, S])
                la = sb1("la", [NH, S])
                gm = sb1("gm", [GW, S])
                mx = sb1("mx", [NH, S])
                mid = sb1("mid", [NH, S], BF16)
                m3 = sb1("m3", [3 * 32, S], BF16)
                e_t = [sb1(f"e_t{i}", [P, 4 * 3 * P]) for i in range(3)]
                stage = e_t[2][:, 0:KT * 2 * FI]
                n_if = 3 * KT * 2 * NH
                wif_raw = e_t[1][:, 0:n_if].rearrange("p (c k n) -> p c k n", c=3, k=KT)
                wr_raw = e_t[1][:, n_if:n_if + KT * NE].rearrange("p (k n) -> p k n", k=KT)
                c3_h = [sb1(f"c3_h{i}", [P, 4 * 3 * P], BF16) for i in range(2)]
                c3_m, c3_l = [sb1(f"c3_{c}", [P, 4 * 3 * P], BF16) for c in "ml"]
                c3 = [(c3_h[i], c3_m, c3_l) for i in range(2)]
                h_t = sb1("h_t", [P, ST, NH, VW])
                hc = sb1("hc", [P, ST, NH, DH])
                den = sb1("den", [P, ST, NH])
                mu = sb1("mu", [P, ST, NH])
                va = sb1("va", [P, ST, NH])
                lgt_s = sb1("lgt_s", [NE, S])
                lg = sb1("lg", [P, ST, NE])
                top = sb1("top", [P, ST, 8])
                nmx = sb1("nmx", [P, ST])
                ex = sb1("ex", [P, ST, NE])
                rep = sb1("rep", [P, ST, NE])
                ssum = sb1("ssum", [P, ST])
                ex3 = sb1("ex3", [P, ST, 3, NE], BF16)

                xr = io["x"].rearrange("(b t p) d -> b p t d", p=P, t=ST)
                ctr = io["ctx_t"].rearrange("(k p) n -> p k n", p=P)
                vr = io["ctx_v"].rearrange("(b t p) c -> b p t c", p=P, t=ST)
                got = {}
                stored = {}
                free.update({n: () for n in ("c_raw", "c_t", "q_t", "v_raw", "v3", "xn", "gm", "m3", "tok", "c3",
                                             "h_t", "ex", "ex3", "lgt_s")})
                free["e"] = [(), (), ()]
                free["c3_h"], free["c3_m"] = [(), ()], ()

                def load_batch(b):
                    if b >= B:
                        return
                    if b >= 3:
                        sp.wait(*stored[b - 3])
                    got["x", b] = load(f"x{b % 3}", x_t[b % 3][:, :, :], xr[b])
                    sp.wait(*free["c_raw"])
                    got["c", b] = load("c", c_raw[:, :, :], ctr[:, :, b * S:(b + 1) * S])
                    sp.wait(*free["v_raw"])
                    got["v", b] = load("v", v_raw[:, :, :], vr[b])

                load_batch(0)
                load("wif", wif_raw[:, :, :, :], io["w_if"].rearrange("(c k p) n -> p c k n", p=P, c=3))
                load("wif", b_if[0:NH, :], io["bi"].rearrange("(n a) -> n a", a=1))
                load("wif", b_if[32:32 + NH, :], io["bf"].rearrange("(n a) -> n a", a=1))
                got_wif = load("wif", ln_s[:, :], io["ln_scale"].rearrange("(a n) -> a n", a=1).broadcast_to([P, D]))
                got_dom = load("dom", dom[:, :], io["dominant"].rearrange("(a n) -> a n", a=1))
                load("router", wr_raw[:, :, :], io["gate_weight_t"].rearrange("(k p) n -> p k n", p=P))
                for c in range(3):
                    got_router = load("router", merge_i[c * NE:(c + 1) * NE, :], io["merge"].rearrange("(n a) -> n a", a=1))

                dve.q.memset(zero[:, :], 0.0)
                dve.q.memset(m3[:, :], 0.0)
                dve.q.memset(head_of[:, :], 0.0)
                dve.q.memset(gm[:, :], 0.0)
                for p in w_if:
                    dve.q.memset(p[:, :, :, :].bitcast(F32), 0.0)
                m = dve.mark(dve.q.memset(ident_b[:, :], 0.0))
                pool.wait(m)
                pool.q.affine_select(out=ident_b[:, :], in_=ident_b[:, :], compare_op=ALU.not_equal, fill=1.0, base=0,
                                     pattern=[[-1, P]], channel_multiplier=1)
                for c in range(3):
                    pool.then(pool.q.affine_select(out=head_of[:, :], in_=head_of[:, :], compare_op=ALU.not_equal,
                                                   fill=1.0, base=-32 * c, pattern=[[-1, NH]], channel_multiplier=1))
                m = pool.mark(pool.q.iota(of_group[:, :, :], pattern=[[1, NG], [0, FI]], base=0,
                                          channel_multiplier=0, allow_small_or_imprecise_dtypes=True))
                pe.wait(m)
                act.wait(m)
                dve.wait(got_router, m)
                dve.then(dve.q.tensor_copy(merge_f[:, :], merge_i[:, :]))
                group_ready = dve.mark(dve.q.tensor_scalar(of_group[:, :, :], of_group[:, :, :], merge_f[:, 0:1], None,
                                                           ALU.is_equal))
                pe.wait(group_ready)
                router_ready = split(wr_raw[:, :, :], [p[:, :, :] for p in w_router], (got_router,))
                dve.wait(got_wif)
                m = dve.then(dve.q.tensor_tensor(wif_raw[:, 1, :, :], wif_raw[:, 1, :, :], wif_raw[:, 2, :, :], ALU.add))
                act.wait(m)
                for c in range(2):
                    for lo in (0, NH):
                        at_ = 32 if lo else 0
                        gates_w = split(wif_raw[:, c, :, lo:lo + NH], [p[:, c, :, at_:at_ + NH] for p in w_if], (m,))

                free["e"][1] = (gates_w, router_ready)
                ht = h_t[:, :, :, :].rearrange("p t h c -> p (t h c)")
                pad, lag0, dskip = ht[0:CH, 0:P], ht[0:CH, P:P + 8], ht[0:CH, P + 8:P + 9]
                load("kpad", lag0, io["ssm"][:, 0:8])
                got_lag0 = load("kpad", dskip, io["skip"].rearrange("(n a) -> n a", a=1))
                dve.then(dve.q.memset(pad, 0.0))
                dve.wait(got_lag0)
                m = dve.mark(dve.q.tensor_tensor(pad[:, P - 1:P], lag0[:, 0:1], dskip, ALU.add))
                sp.wait(m)
                load("kpad", kpad_d[:, P:P - 1 + L], io["ssm"][:, 1:L])
                free["h_t"] = (load("kpad", kpad_d[:, 0:P], pad),)
                x1_ready = {}

                def per_head(a):
                    return a[:, :, :].unsqueeze(3).broadcast_to([P, ST, NH, DH])

                g_tok = [sb1(f"g_tok{i}", [P, ST, NH]) for i in range(2)]
                en_tok = [sb1(f"en_tok{i}", [P, ST, NH]) for i in range(2)]
                at_ready = {}

                def operands(b):
                    x = x_t[b % 3]
                    ln = layernorm(x, xn, ST, (got["x", b],), free["xn2"])
                    act.wait(got["c", b], *free["c_t"])
                    m = act.mark(act.q.copy(c_t[0][:, :, :], c_raw[:, :, :]))
                    pool.wait(m, got["c", b])
                    c_ready = pool.mark(pool.q.tensor_tensor(c_t[1][:, :, :], c_raw[:, :, :], c_t[0][:, :, :].bitcast(F32),
                                                             ALU.subtract))
                    free["c_raw"] = (c_ready,)
                    yield
                    for t in range(ST):
                        bank = (b_qk0, b_qk1)[t % 2]
                        tb = claim(bank)
                        pe.wait(ln)
                        for k in range(KT):
                            ins = pe.q.transpose(tb[:, k * P:(k + 1) * P], xn[:, t, k * P:(k + 1) * P], ident[:, :])
                        m = pe.mark(ins)
                        q_ready = split(tb[:, :].rearrange("p (k n) -> p k n", k=KT),
                                        [p[:, :, t * P:(t + 1) * P] for p in q_t], (m,), free["q_t"])
                        bank.read = (q_ready,)
                        yield
                    free["xn2"] = (m,)
                    tb = claim(b_m)
                    pe.wait(gates_w, q_ready, c_ready)
                    for k in range(2 * KT):
                        src = q_t if k < KT else c_t
                        ins = product(tb[0:GW, 0:S], [p[:, k // KT, k % KT, :] for p in w_if],
                                      [p[:, k % KT, :] for p in src], k == 0, k == 2 * KT - 1)
                    m = pe.mark(ins)
                    dve.wait(m)
                    dve.q.tensor_scalar(fg[:, :], tb[32:32 + NH, 0:S], b_if[32:32 + NH, 0:1], None, ALU.add)
                    m = dve.then(dve.q.tensor_scalar(ig[:, :], tb[0:NH, 0:S], b_if[0:NH, 0:1], None, ALU.add))
                    b_m.read = (m,)
                    m = dve.mark(dve.q.scalar_tensor_tensor(la[:, :], fg[:, :], -1.0, fg[:, :], ALU.mult, ALU.max))
                    act.wait(m)
                    act.then(act.q.activation(la[:, :], la[:, :], ACT.Exp, scale=-1.0))
                    m = act.mark(act.q.activation(la[:, :], la[:, :], ACT.Ln, bias=1.0))
                    yield
                    dve.wait(m, *free["gm"])
                    dve.then(dve.q.scalar_tensor_tensor(la[:, :], fg[:, :], 0.0, la[:, :], ALU.min, ALU.subtract))
                    dve.then(dve.q.tensor_tensor_scan(fg[:, :], la[:, :], zero[:, :], 0.0, ALU.add, ALU.add))
                    dve.then(dve.q.tensor_tensor(gm[0:NH, :], ig[:, :], fg[:, :], ALU.subtract))
                    dve.then(dve.q.tensor_tensor_scan(mx[:, :], gm[0:NH, :], gm[0:NH, :], -3.0e38, ALU.max, ALU.max))
                    m_gm = dve.mark(dve.q.scalar_tensor_tensor(gm[32:32 + NH, :], fg[:, :], -1.0, mx[:, :], ALU.mult,
                                                               ALU.subtract))
                    dve.wait(*free["m3"])
                    dve.then(dve.q.tensor_copy(m3[0:NH, :], mx[:, :]))
                    dve.then(dve.q.tensor_tensor(mx[:, :], mx[:, :], m3[0:NH, :], ALU.subtract))
                    m = dve.then(dve.q.tensor_copy(mid[:, :], mx[:, :]))
                    m_lo = dve.mark(dve.q.tensor_tensor(m3[64:64 + NH, :], mx[:, :], mid[:, :], ALU.subtract))
                    act.wait(m)
                    m_mid = act.mark(act.q.copy(m3[32:32 + NH, :], mid[:, :]))
                    dve.wait(m_mid)
                    tb = claim(b_m)
                    pe.wait(m_gm)
                    for t in range(ST):
                        ins = pe.q.transpose(tb[:, t * 64:t * 64 + GW], gm[:, t * P:(t + 1) * P], ident[0:GW, 0:GW])
                    m = pe.mark(ins)
                    free["gm"] = (m,)
                    tv = tb[:, 0:ST * 64].rearrange("p (t n) -> p t n", t=ST)
                    act.wait(m, *free["tok"][b % 2])
                    act.q.activation(en_tok[b % 2][:, :, :], tv[:, :, 32:32 + NH], ACT.Exp)
                    g_ready = act.mark(act.q.copy(g_tok[b % 2][:, :, :], tv[:, :, 0:NH]))
                    b_m.read = (g_ready,)
                    at_ready[b] = {"m3": (m_lo, m_mid), "g": g_ready}
                    yield

                def values(b):
                    act.wait(got["v", b], *free["v3"])
                    m = act.mark(act.q.copy(v3[0][:, :, :], v_raw[:, :, :]))
                    pool.wait(m, got["v", b])
                    m = pool.then(pool.q.tensor_tensor(v_raw[:, :, :], v_raw[:, :, :], v3[0][:, :, :], ALU.subtract))
                    act.wait(m)
                    m = act.mark(act.q.copy(v3[1][:, :, :], v_raw[:, :, :]))
                    pool.wait(m)
                    v_ready = pool.mark(pool.q.tensor_tensor(v3[2][:, :, :], v_raw[:, :, :], v3[1][:, :, :], ALU.subtract))
                    free["v_raw"] = (v_ready,)
                    at_ready[b]["v"] = v_ready
                    load_batch(b + 1)

                QUADS = NH // 4
                done = {}

                def blocks_of(quad):
                    return e_t[quad % 3][:, :].rearrange("p (i a c) -> p i a c", i=4, a=3)

                def decays(b, quad, pair):
                    ev = blocks_of(quad)
                    bank = (b_m, b_gu0)[pair]
                    t1 = claim(bank)
                    pe.wait(*at_ready[b]["m3"])
                    for i in range(2):
                        h = quad * 4 + pair * 2 + i
                        ins = pe.q.matmul(t1[:, i * S:(i + 1) * S], head_of[:, h:h + 1].broadcast_to([3 * 32, P]),
                                          m3[:, :], start=True, stop=True)
                    m = pe.mark(ins)
                    act.wait(m, at_ready[b]["g"], *free["e"][quad % 3])
                    for i in range(2):
                        h = quad * 4 + pair * 2 + i
                        act.q.activation(ev[:, pair * 2 + i, 0:3:2, :],
                                         t1[:, i * S:(i + 1) * S].rearrange("p (a c) -> p a c", a=2),
                                         ACT.Exp, bias=g_tok[b % 2][:, 0, h:h + 1], scale=-1.0)
                        m = act.mark(act.q.activation(ev[:, pair * 2 + i, 1, :], t1[:, i * S + P:(i + 1) * S],
                                                      ACT.Exp, bias=g_tok[b % 2][:, 1, h:h + 1], scale=-1.0))
                    bank.read = (m,)
                    if pair:
                        free["m3"] = ((pe, pe.count),)
                        pool.wait(m)
                        diag = ev[:, :, 0:2, :].rearrange("p h a c -> p h (a c)")
                        done["mask", b, quad] = pool.mark(pool.q.affine_select(
                            out=diag, in_=diag, compare_op=ALU.is_ge, fill=0.0, base=0,
                            pattern=[[0, 4], [0, 2], [1, P]], channel_multiplier=-1))

                def scores(b, quad, i):
                    h = quad * 4 + i
                    r, k = slice((h % 4) * DH, (h % 4 + 1) * DH), h // 4
                    bank = (b_qk0, b_qk1, b_gu1)[(quad * 4 + i) % 3]
                    t2 = claim(bank)
                    off_diag = t2[:, 0:3 * P].rearrange("p (a c) -> p a c", a=3)[:, 0:3:2, :]
                    for out, ks, qs in ((off_diag, slice(0, P), slice(0, S)), (t2[:, P:2 * P], slice(P, S), slice(P, S))):
                        for n, (a, c) in enumerate(((0, 0), (0, 1), (1, 0))):
                            ins = pe.q.matmul(out, c_t[a][r, k, ks], q_t[c][r, k, qs], start=(n == 0), stop=(n == 2),
                                              tile_position=((h % 4) * DH, 0))
                    m = pe.mark(ins)
                    free["q_t"] = free["c_t"] = (m,)
                    dve.wait(m, done["mask", b, quad])
                    c = blocks_of(quad)[:, i, :, :].rearrange("p a b -> p (a b)")
                    done["scores", b, quad] = dve.mark(dve.q.scalar_tensor_tensor(
                        c, t2[:, 0:3 * P], float(DH) ** -0.5, c, ALU.mult, ALU.mult))
                    bank.read = (done["scores", b, quad],)

                def high(b, quad):
                    e = e_t[quad % 3]
                    act.wait(done["scores", b, quad], *free["c3_h"][quad % 2])
                    m = act.mark(act.q.copy(c3[quad % 2][0][:, :], e[:, :]))
                    dve.wait(m, done["scores", b, quad])
                    done["rest", b, quad] = dve.then(dve.q.tensor_tensor(e[:, :], e[:, :], c3[quad % 2][0][:, :], ALU.subtract))

                def middle(b, quad):
                    act.wait(done["rest", b, quad], *free["c3_m"])
                    done["middle", b, quad] = act.mark(act.q.copy(c3_m[:, :], e_t[quad % 3][:, :]))

                def low(b, quad):
                    dve.wait(done["middle", b, quad])
                    m = dve.mark(dve.q.tensor_tensor(c3_l[:, :], e_t[quad % 3][:, :], c3_m[:, :], ALU.subtract))
                    free["e"][quad % 3] = (m,)
                    done["parts", b, quad] = m

                def weighted_values(b, quad):
                    th_ = claim(b_h)
                    pe.wait(done["parts", b, quad], at_ready[b]["v"])
                    hv = th_[:, 0:ST * 4 * VW].rearrange("p (t h c) -> p t h c", t=ST, h=4)
                    terms = [(0, 0), (0, 1), (1, 0), (1, 1), (0, 2), (2, 0)]
                    for i in range(4):
                        h = quad * 4 + i
                        for st, blk, tt in ((0, 0, 0), (1, 2, 0), (1, 1, 1)):
                            for n, (a, c) in enumerate(terms):
                                ins = pe.q.matmul(hv[:, st, i, :], c3[quad % 2][a][:, (i * 3 + blk) * P:(i * 3 + blk + 1) * P],
                                                  v3[c][:, tt, h * VW:(h + 1) * VW],
                                                  start=(n == 0 and blk != 1), stop=(n == 5 and blk != 2))
                    m = pe.mark(ins)
                    free["c3_h"][quad % 2] = free["c3_m"] = free["v3"] = (m,)
                    act.wait(m, *free["h_t"])
                    m = act.mark(act.q.copy(h_t[:, :, quad * 4:quad * 4 + 4, :], hv))
                    b_h.read = done["h", b] = (m,)

                def stages(b, s):
                    if 0 <= s - 2 < QUADS:
                        high(b, s - 2)
                    for i in range(4):
                        if i % 2 == 0 and s < QUADS:
                            decays(b, s, i // 2)
                            yield
                        if 0 <= s - 1 < QUADS:
                            scores(b, s - 1, i)
                            yield
                        if i == 1 and 0 <= s - 3 < QUADS:
                            weighted_values(b, s - 3)
                            yield
                        if i == 2 and 0 <= s - 2 < QUADS:
                            middle(b, s - 2)
                    if 0 <= s - 2 < QUADS:
                        low(b, s - 2)
                        yield

                def quads(b):
                    values(b)
                    for s in range(QUADS + 1):
                        yield from stages(b, s)

                def last_quads(b):
                    for s in range(QUADS + 1, QUADS + 3):
                        yield from stages(b, s)

                def attention_end(b):
                    x = x_t[b % 3]
                    dve.wait(*done["h", b])
                    total = h_t[:, :, :, ones_col]
                    dve.then(dve.q.scalar_tensor_tensor(den[:, :, :], total, -1.0, total, ALU.mult, ALU.max))
                    dve.then(dve.q.tensor_tensor(den[:, :, :], den[:, :, :], en_tok[b % 2][:, :, :], ALU.max))
                    dve.then(dve.q.tensor_scalar(den[:, :, :], den[:, :, :], EPS_X, None, ALU.add))
                    m = dve.then(dve.q.reciprocal(den[:, :, :], den[:, :, :]))
                    free["tok"][b % 2] = (m,)
                    dve.then(dve.q.tensor_tensor(hc[:, :, :, :], h_t[:, :, :, 0:DH], per_head(den), ALU.mult))
                    yield
                    dve.then(dve.q.tensor_reduce(mu[:, :, :], hc[:, :, :, :], AX, ALU.add))
                    dve.then(dve.q.tensor_scalar(mu[:, :, :], mu[:, :, :], 1.0 / DH, None, ALU.mult))
                    m = dve.then(dve.q.tensor_tensor(hc[:, :, :, :], hc[:, :, :, :], per_head(mu), ALU.subtract))
                    act.wait(m)
                    m = act.mark(act.q.activation(h_t[:, :, :, 0:DH], hc[:, :, :, :], ACT.Square))
                    yield
                    dve.wait(m)
                    dve.then(dve.q.tensor_reduce(va[:, :, :], h_t[:, :, :, 0:DH], AX, ALU.add))
                    m = dve.then(dve.q.tensor_scalar(va[:, :, :], va[:, :, :], 1.0 / DH, EPS_X, ALU.mult, ALU.add))
                    free["h_t"] = (m,)
                    pool.wait(m)
                    m = pool.mark(pool.q.tensor_tensor(va[:, :, :], va[:, :, :],
                                                       minus_half[:, :].rearrange("p (t h) -> p t h", t=ST), ALU.pow))
                    yield
                    yield
                    dve.wait(m)
                    dve.then(dve.q.tensor_tensor(hc[:, :, :, :], hc[:, :, :, :], per_head(va), ALU.mult))
                    dve.then(dve.q.tensor_tensor(
                        hc[:, :, :, :], hc[:, :, :, :],
                        ln_s[:, :].rearrange("p (h c) -> p h c", c=DH).unsqueeze(1).broadcast_to([P, ST, NH, DH]), ALU.mult))
                    x1_ready[b] = dve.then(dve.q.tensor_tensor(
                        x[:, :, :], x[:, :, :], hc[:, :, :, :].rearrange("p t h c -> p t (h c)"), ALU.add))
                    yield

                ffn_ready = {}

                def normalise_and_route(b):
                    x = x_t[b % 3]
                    ln = yield from layernorm_steps(x, xn2, ST, (x1_ready[b],), free["xn2"])
                    sp.wait(ln)
                    xn_saved = load("xn2s", xn2v[b], xn2[:, :, :])
                    yield
                    yield
                    yield
                    for i in range(ST):
                        t7 = claim(b_down)
                        pe.wait(ln)
                        for k in range(KT):
                            ins = pe.q.transpose(t7[:, k * P:(k + 1) * P], xn2[:, i, k * P:(k + 1) * P], ident[:, :])
                        m = pe.mark(ins)
                        xt = split(t7[:, :].rearrange("p (k n) -> p k n", k=KT), [p[:, :, i * P:(i + 1) * P] for p in xn_t],
                                   (m,), free["xn_t"])
                        b_down.read = (xt,)
                        yield
                    free["xn2"] = (m, xn_saved)
                    t7 = claim(b_down)
                    pe.wait(xt, router_ready)
                    for k in range(KT):
                        ins = product(t7[0:NE, 0:S], [p[:, k, :] for p in w_router], [p[:, k, :] for p in xn_t],
                                      k == 0, k == KT - 1)
                    m = pe.mark(ins)
                    act.wait(m, *free["lgt_s"])
                    m = act.mark(act.q.copy(lgt_s[:, :], t7[0:NE, 0:S]))
                    b_down.read = (m,)
                    yield
                    t7 = claim(b_down)
                    pe.wait(m)
                    for i in range(ST):
                        ins = pe.q.transpose(t7[:, i * NE:(i + 1) * NE], lgt_s[:, i * P:(i + 1) * P], ident[0:NE, 0:NE])
                    m = pe.mark(ins)
                    free["lgt_s"] = (m,)
                    dve.wait(m)
                    tv = t7[:, 0:ST * NE].rearrange("p (t n) -> p t n", t=ST)
                    dve.then(dve.q.tensor_reduce(nmx[:, :], tv, AX, ALU.max))
                    m = dve.then(dve.q.tensor_tensor(lg[:, :, :], tv, nmx[:, :].unsqueeze(2).broadcast_to([P, ST, NE]),
                                                     ALU.subtract))
                    b_down.read = (m,)
                    act.wait(m)
                    m = act.mark(act.q.activation(ex[:, :, :], lg[:, :, :], ACT.Exp))
                    dve.wait(m)
                    for i in range(ST):
                        m = dve.mark(dve.q.max(top[:, i, :], ex[:, i, :]))
                    dve.wait(m)
                    for i in range(ST):
                        m = dve.mark(dve.q.match_replace(rep[:, i, :], top[:, i, :], ex[:, i, :], 0.0))
                    dve.wait(m)
                    dve.q.tensor_tensor(ex[:, :, :], ex[:, :, :], rep[:, :, :], ALU.subtract)
                    dve.then(dve.q.tensor_reduce(ssum[:, :], top[:, :, :], AX, ALU.add))
                    dve.then(dve.q.reciprocal(ssum[:, :], ssum[:, :]))
                    dve.then(dve.q.tensor_tensor(ex[:, :, :], ex[:, :, :], ssum[:, :].unsqueeze(2).broadcast_to([P, ST, NE]),
                                                 ALU.mult))
                    dve.wait(*free["ex3"])
                    for c in range(3):
                        m = dve.then(dve.q.tensor_copy(ex3[:, :, c, :], ex[:, :, :]))
                        if c < 2:
                            dve.then(dve.q.tensor_tensor(ex[:, :, :], ex[:, :, :], ex3[:, :, c, :], ALU.subtract))
                    yield
                    t7 = claim(b_down)[:, :].bitcast(BF16)
                    pe.wait(m)
                    for i in range(ST):
                        ins = pe.q.transpose(t7[0:3 * NE, i * P:(i + 1) * P], ex3[:, i, :, :].rearrange("p c n -> p (c n)"),
                                             ident_b[:, :])
                    m = pe.mark(ins)
                    free["ex3"] = (m,)
                    act.wait(m)
                    m = act.mark(act.q.copy(sel[:, b * S:(b + 1) * S], t7[0:3 * NE, 0:S]))
                    b_down.read = (m,)
                    yield
                    ffn_ready[b] = (xt, m)

                def first_groups(b):
                    x = x_t[b % 3]
                    i = 0
                    for done in merged_ffn(b, 0, ffn_ready[b]):
                        if done:
                            bank, mm = done
                            dve.wait(mm)
                            m = dve.mark(dve.q.tensor_tensor(x[:, i, :], x[:, i, :], bank.t[:, :], ALU.add))
                            bank.read = (m,)
                            i += 1
                        yield
                    sp.wait(m)
                    stored[b] = (load(f"x2s{b % 3}", x2v[b], x[:, :, :]),)
                    yield

                def weights_first():
                    weights_ready[0] = yield from half_weights(0, [stage])

                free["tok"] = [(), ()]

                def end_of(b):
                    yield from attention_end(b)
                    yield from normalise_and_route(b)

                run_together((weights_first(), 1.0), (operands(0), 1.0))
                free["e"][2] = (weights_ready[0],)
                for b in range(B + 1):
                    first, second = [], []
                    if b > 0:
                        first.append((end_of(b - 1), 11.0))
                    if b < B:
                        first.append((quads(b), 28.0))
                        second.append((last_quads(b), 6.0))
                    if b + 1 < B:
                        second.append((operands(b + 1), 4.5))
                    if b > 0:
                        second.append((first_groups(b - 1), 9.0))
                    run_together(*first)
                    run_together(*second)
                free["w"] = ((pe, pe.count),)
            meet()

            two = ExitStack()
            with two:
                def sb2(name, shape, dt=F32):
                    return sbuf(two, name, shape, dt)

                stages = [sb2(f"stage{i}", [P, KT * 2 * FI])[:, :] for i in range(4)]
                stage_read = [()] * 4
                for _ in half_weights(1, stages):
                    pass
                weights_ready[1] = (dve, dve.count)
                xp = [sb2(f"xp{i}", [P, ST, D]) for i in range(3)]
                xl = [sb2(f"xl{i}", [P, ST, D]) for i in range(2)]
                xn3 = sb2("xn3", [P, ST, D])
                xn3_t = [sb2(f"xn3_t{i}", [P, KT, S]) for i in range(2)]
                xn_t2 = [xn_t, [sb2(f"xn_t2_{c}", [P, KT, S], F32R) for c in "hl"]]
                xl_free, xp_free, t2_free, t3_free = [(), ()], [(), (), ()], [(), ()], [(), ()]
                xn3_free = ()
                got2, xt2 = {}, {}

                def fetch(b):
                    if b >= B:
                        return
                    sp.wait(*xl_free[b % 2])
                    got2["n", b] = load(f"xl{b % 2}", xl[b % 2][:, :, :], xn2v[b])
                    sp.wait(*xp_free[b % 3])
                    got2["x", b] = load(f"xp{b % 3}", xp[b % 3][:, :, :], x2v[b])

                def turn(b):
                    for i in range(ST):
                        bank = (b_qk1, b_m)[i % 2]
                        t = claim(bank)
                        pe.wait(got2["n", b])
                        for k in range(KT):
                            ins = pe.q.transpose(t[:, k * P:(k + 1) * P], xl[b % 2][:, i, k * P:(k + 1) * P], ident[:, :])
                        m = pe.mark(ins)
                        xt2[b] = split(t[:, :].rearrange("p (k n) -> p k n", k=KT),
                                       [p[:, :, i * P:(i + 1) * P] for p in xn_t2[b % 2]], (m,), t2_free[b % 2])
                        bank.read = (xt2[b],)
                    xl_free[b % 2] = (m,)

                def complete(b, ready):
                    xb = xp[b % 3]
                    sp.wait(ready)
                    st = load(f"x2f{b % 3}", x2v[b], xb[:, :, :])
                    ln = layernorm(xb, xn3, ST, (ready,), xn3_free)
                    xp_free[b % 3] = (st, ln)
                    return ln

                def queries(b, ln):
                    nonlocal xn3_free
                    act.wait(*t3_free[b % 2])
                    for i in range(ST):
                        m = to_features(xn3[:, i, :], xn3_t[b % 2][:, :, i * P:(i + 1) * P], (b_qk0, b_h)[i % 2], act, (ln,))
                    xn3_free = (m,)
                    sp.wait(m)
                    t3_free[b % 2] = (load(f"q3_{b % 2}", q3_d[:, b * S:(b + 1) * S].rearrange("(k p) n -> p k n", p=P),
                                           xn3_t[b % 2][:, :, :]),)

                fetch(0)
                fetch(1)
                turn(0)
                before = None
                for b in range(B):
                    xn_t = xn_t2[b % 2]
                    n = i = 0
                    for done in merged_ffn(b, 1, (xt2[b],)):
                        n += 1
                        if n == 1 and b + 1 < B:
                            turn(b + 1)
                        if n == 2 and before:
                            ln = complete(*before)
                        if n == 3:
                            fetch(b + 2)
                        if n == 4 and before:
                            queries(before[0], ln)
                        if done:
                            bank, mm = done
                            dve.wait(mm, got2["x", b])
                            m = dve.mark(dve.q.tensor_tensor(xp[b % 3][:, i, :], xp[b % 3][:, i, :], bank.t[:, :], ALU.add))
                            bank.read = (m,)
                            i += 1
                    t2_free[b % 2] = free["xn_t"]
                    before = (b, m)
                queries(before[0], complete(*before))
        meet()

        late = main.enter_context(ExitStack())
        ROW = D + 8
        SPAD = -(-CAP // 8) * 8
        store = sbuf(late, "store", [P, max(KT * T, TOKT * ROW)])
        rows = store[:, 0:TOKT * ROW].rearrange("p (t c) -> p t c", c=ROW)
        cc = ExitStack()
        HB = B // 2
        NP_ = HR * (HR // 2) + HR // 2
        EARLY = 4
        units = ([(h, 0) for h in range(EARLY)] + [(h, i) for h in range(EARLY, CH) for i in range(2)]
                 + [(h, 1) for h in range(EARLY)])
        uses = [h for n, (h, i) in enumerate(units) if n == 0 or units[n - 1][0] != h]
        use_of = list(itertools.accumulate(int(n > 0 and units[n - 1][0] != h) for n, (h, i) in enumerate(units)))
        with cc:
            def sb(name, shape, dt=F32):
                return sbuf(cc, name, shape, dt)

            cr = store[:, 0:KT * T].rearrange("p (k n) -> p k n", k=KT)
            qo = sb("qo", [P, KT, T])
            toep_raw = [sb(f"toep_raw{i}", [P, L]) for i in range(2)]
            toep = [[sb(f"toep{i}_{c}", [P, L], F32R) for c in "hl"] for i in range(2)]
            kxs = [sb(f"kx{i}", [P, KT * HB, 12]) for i in range(2)]
            kv_raw = [sb(f"kv_raw{i}", [P, KT * HB, NP_]) for i in range(2)]
            kv = [[sb(f"kv{i}_{c}", [P, KT * HB, NP_], F32R) for c in "hl"] for i in range(2)]
            qx = sb("qx", [P, KT, HB, 16])
            yf = [sb(f"yf{i}", [P, KT, HB, HR, HR]) for i in range(2)]
            xl3 = [sb(f"xl3_{i}", [P, 2, D]) for i in range(3)]
            fill = sb("fill", [P, ROW])
            less_mean = sb("less_mean", [P, BLK])

            m = dve.mark(dve.q.memset(fill[:, :], 0.0))
            pool.wait(m)
            m_fill = pool.mark(pool.q.iota(fill[:, D:D + 1].bitcast(I32), pattern=[[0, 1]], base=T, channel_multiplier=1))

            ct = io["ctx_rev"].rearrange("(k p) n -> p k n", p=P)
            qd = q3_d[:, :].rearrange("(k p) n -> p k n", p=P)
            raw_read, toep_ready, toep_read = [(), ()], {}, [(), ()]
            kx_read, kv_raw_read, kv_read, yf_read = [(), ()], [(), ()], [(), ()], [(), ()]
            extended, products, parts_ready, convolved = {}, {}, {}, {}
            got_cr, got_q, got_t = {}, {}, {}

            def fetch_toep(u):
                if u < len(uses):
                    sp.wait(*raw_read[u % 2])
                    row = kpad_d[uses[u]:uses[u] + 1, :]
                    got_t[u] = load(f"toep{u % 2}", toep_raw[u % 2][:, :], bass.AP(row.tensor, row.offset, [[1, P], [1, L]]))

            def split_toep(u):
                toep_ready[u] = split(toep_raw[u % 2][:, :], [p[:, :] for p in toep[u % 2]], (got_t[u],), toep_read[u % 2])
                raw_read[u % 2] = (toep_ready[u],)

            def extend_rows(n):
                h, half = units[n]
                c = cr[:, :, half * HB * S:(half + 1) * HB * S].rearrange("p k (b h i) -> p k b h i", b=HB, i=HR)
                x = kxs[n % 2][:, :, :].rearrange("p (k b) i -> p k b i", k=KT)
                act.wait(got_cr[half], *kx_read[n % 2])
                act.q.copy(x[:, :, :, 0:HR], c[:, :, :, h, :])
                extended[n] = act.mark(act.q.copy(x[:, :, :, HR:12], c[:, :, :, h, 0:4]))

            def pair_products(n):
                kx = kxs[n % 2]
                pool.wait(extended[n], *kv_raw_read[n % 2])
                base = kx[:, :, :]
                near = bass.AP(base.tensor, base.offset, [list(base.ap[0]), [12, KT * HB], [1, 4], [1, HR]])
                out = kv_raw[n % 2][:, :, 0:4 * HR].rearrange("p n (d i) -> p n d i", d=4)
                pool.q.tensor_tensor(out, kx[:, :, 0:HR].unsqueeze(2).broadcast_to([P, KT * HB, 4, HR]), near, ALU.mult)
                products[n] = pool.mark(pool.q.tensor_tensor(kv_raw[n % 2][:, :, 4 * HR:], kx[:, :, 0:4], kx[:, :, 4:8], ALU.mult))
                kx_read[n % 2] = (products[n],)

            def split_products(n):
                raw, (hi, lo) = kv_raw[n % 2], kv[n % 2]
                act.wait(products[n], *kv_read[n % 2])
                m = act.mark(act.q.copy(hi[:, :, :], raw[:, :, :]))
                pool.wait(m, products[n])
                parts_ready[n] = pool.mark(pool.q.tensor_tensor(lo[:, :, :], raw[:, :, :], hi[:, :, :].bitcast(F32), ALU.subtract))
                kv_raw_read[n % 2] = (parts_ready[n],)

            def convolve(n):
                u = use_of[n]
                w = toep[u % 2]
                pe.wait(toep_ready[u], parts_ready[n])
                for o in range(KT):
                    t = claim(banks[(n % 2) * KT + o])
                    for k in range(o + 1):
                        ins = product(t[:, 0:HB * NP_], [p[:, (o - k) * P:(o - k + 1) * P] for p in w],
                                      [p[:, k * HB:(k + 1) * HB, :].rearrange("p b c -> p (b c)") for p in kv[n % 2]],
                                      k == 0, k == o)
                convolved[n] = pe.mark(ins)
                kv_read[n % 2] = toep_read[u % 2] = (convolved[n],)

            def sum_pairs(n):
                h, half = units[n]
                f = yf[n % 2]
                y = psum[:, (n % 2) * KT * BANK:(n % 2 + 1) * KT * BANK].rearrange("p (o c) -> p o c", o=KT)[
                    :, :, 0:HB * NP_].rearrange("p o (b c) -> p o b c", b=HB)
                act.wait(convolved[n], *yf_read[n % 2])
                act.q.copy(f[:, :, :, 0:4, :].rearrange("p o b d j -> p o b (d j)"), y[:, :, :, 0:32])
                for w in range(2):
                    act.q.copy(f[:, :, :, 4, 4 * w:4 * w + 4], y[:, :, :, 32:36])
                for d in range(5, 8):
                    c = 8 - d
                    act.q.copy(f[:, :, :, d, 0:c], y[:, :, :, c * 8 + d:c * 8 + 8])
                    m_f = act.mark(act.q.copy(f[:, :, :, d, c:8], y[:, :, :, c * 8:c * 8 + 8 - c]))
                for o in range(KT):
                    banks[(n % 2) * KT + o].read = (m_f,)
                qv = qo[:, :, half * HB * S:(half + 1) * HB * S].rearrange("p k (b h i) -> p k b h i", b=HB, i=HR)
                dve.wait(got_q[half])
                dve.q.tensor_copy(qx[:, :, :, 0:8], qv[:, :, :, h, :])
                m = dve.mark(dve.q.tensor_copy(qx[:, :, :, 8:15], qv[:, :, :, h, 0:7]))
                dve.wait(m, m_f)
                base = qx[:, :, :, :]
                win = bass.AP(base.tensor, base.offset, [list(base.ap[0]), [16, KT * HB], [1, 8], [1, 8]])
                fv = f[:, :, :, :, :].rearrange("p o b d j -> p (o b) d j")
                dve.then(dve.q.tensor_tensor(fv, fv, win, ALU.mult))
                m = dve.then(dve.q.tensor_reduce(qv[:, :, :, h, :], f[:, :, :, :, :].rearrange("p o b d j -> p o b j d"),
                                                 AX, ALU.add))
                yf_read[n % 2] = (m,)
                return m

            fetch_toep(0)
            for half in range(2):
                cols = slice(half * HB * S, (half + 1) * HB * S)
                for k in range(KT):
                    got_cr[half] = load(f"cr{half}", cr[:, k, cols], ct[:, k, cols])
                for k in range(KT):
                    got_q[half] = load(f"qo{half}", qo[:, k, cols], qd[:, k, cols])
                if half == 0:
                    fetch_toep(1)
            split_toep(0)
            for n in range(2):
                extend_rows(n)
                pair_products(n)
            split_products(0)
            extend_rows(2)
            for n in range(len(units) + 1):
                if n < len(units):
                    convolve(n)
                if n + 2 < len(units):
                    pair_products(n + 2)
                if n + 1 < len(units):
                    split_products(n + 1)
                if n > 0:
                    m_o = sum_pairs(n - 1)
                if n + 3 < len(units):
                    extend_rows(n + 3)
                if n < len(units) and (n == 0 or use_of[n] != use_of[n - 1]) and use_of[n] + 1 < len(uses):
                    split_toep(use_of[n] + 1)
                    fetch_toep(use_of[n] + 2)
                if n == 2 * EARLY:
                    sp.wait(m_fill)
                    for s0 in range(0, ER * SPAD, P):
                        n = min(P, ER * SPAD - s0)
                        load("fill", slots_d[s0:s0 + n, :], fill[0:n, :])
                    load("fill", io["out"][T:T + P, :], fill[:, 0:D])
            x2p = x2_d[:, :].rearrange("(g t p) d -> g p t d", p=P, t=2)
            x3p = x3_d[:, :].rearrange("(g t p) d -> g p t d", p=P, t=2)
            xl3 += [y[:, :, :, :, :].rearrange("p k b d j -> p (k b d j)")[:, i * 2 * D:(i + 1) * 2 * D].rearrange(
                "p (t c) -> p t c", t=2) for y in yf for i in range(KT * HB * HR * HR // (2 * D))]
            NX = len(xl3)
            xl_free3, got_x2, stats = [()] * 3 + [yf_read[0] + yf_read[1]] * (NX - 3), {}, {}

            def fetch_x2(g):
                if g < TOKT // 2:
                    sp.wait(*xl_free3[g % NX])
                    got_x2[g] = load(f"xl3_{g % NX}", xl3[g % NX][:, :, :], x2p[g])

            def add_residual(g):
                x = xl3[g % NX]
                for j in range(2):
                    bank = banks[(2 * g + j) % 4]
                    t = claim(bank)
                    pe.wait(m_o)
                    for k in range(KT):
                        c = (2 * g + j) * P
                        ins = pe.q.transpose(t[:, k * P:(k + 1) * P], qo[:, k, c:c + P], ident[:, :])
                    m = pe.mark(ins)
                    dve.wait(m, got_x2[g])
                    m = dve.mark(dve.q.tensor_tensor(x[:, j, :], x[:, j, :], t[:, :], ALU.add))
                    bank.read = (m,)
                sp.wait(m)
                stored = load(f"x3s{g % NX}", x3p[g], x[:, :, :])
                dve.wait(m)
                s = slice(g % 2 * 2, g % 2 * 2 + 2)
                if g > 1:
                    dve.wait(*xl_free3[(g - 2) % NX])
                for j in range(2):
                    m = dve.mark(dve.q.bn_stats(bn[:, g % 2 * 2 + j, :], x[:, j, :]))
                dve.wait(m)
                for j in range(2):
                    m = dve.mark(dve.q.bn_aggr(mv[:, g % 2 * 2 + j, :], bn[:, g % 2 * 2 + j, :]))
                dve.wait(m)
                dve.q.tensor_scalar(less_mean[:, s], mv[:, s, 0], -1.0, None, ALU.mult)
                m = dve.mark(dve.q.tensor_scalar(rstd[:, s], mv[:, s, 1], EPS_LN, None, ALU.add))
                pool.wait(m)
                stats[g] = pool.mark(pool.q.tensor_tensor(rstd[:, s], rstd[:, s], minus_half[:, 0:2], ALU.pow)), stored

            def normalise(g):
                m, stored = stats[g]
                act.wait(m, *rows_free)
                for j in range(2):
                    i = g % 2 * 2 + j
                    m = act.mark(act.q.activation(rows[:, 2 * g + j, 0:D], xl3[g % NX][:, j, :], ACT.Identity,
                                                  bias=less_mean[:, i:i + 1]))
                act.wait(m)
                for j in range(2):
                    i = g % 2 * 2 + j
                    m = act.mark(act.q.activation(rows[:, 2 * g + j, 0:D], rows[:, 2 * g + j, 0:D], ACT.Identity,
                                                  scale=rstd[:, i:i + 1]))
                xl_free3[g % NX] = (stored, m)

            rows_free = ((act, act.count), (pool, pool.count))
            pool.wait(*rows_free)
            pool.q.iota(rows[:, :, D:D + 1].bitcast(I32), pattern=[[P, TOKT], [0, 1]], base=0, channel_multiplier=1)
            for g in range(NX):
                fetch_x2(g)
            for g in range(TOKT // 2 + 1):
                if g < TOKT // 2:
                    add_residual(g)
                if g > 0:
                    normalise(g - 1)
                    fetch_x2(g + NX - 1)
        meet()

        dd = ExitStack()
        with dd:
            def sb(name, shape, dt=F32, ctx=dd):
                return sbuf(ctx, name, shape, dt)

            FT = FF // P
            HALF = SPAD // 2
            N7 = ER * TOKT
            NBLK = T // NB
            w1_raw = sb("w1_raw", [P, KT, 2 * FF])
            w2_raw = sb("w2_raw", [P, FT, D])
            w1s = [[sb(f"w1_{i}_{c}", [P, KT, 2 * FF], F32R) for c in "hl"] for i in range(2)]
            w2s = [[sb(f"w2_{i}_{c}", [P, FT, D], F32R) for c in "hl"] for i in range(2)]
            sg = [sb(f"sg{i}", [P, NB]) for i in range(2)]
            pr = sb("pr", [P, NB])
            at = [sb(f"at_{c}", [P, FT, NB], F32R) for c in "hl"]
            gw = [sb(f"gw_{c}", [P, KT, ER], F32R) for c in "hl"]
            raw_free, w_free, xt_free, at_free = (), [(), ()], (), ()
            w2_free = [(), ()]
            pr_free = ()
            sg_free = [(), ()]
            w_order = [(io["shared_w1"], io["shared_w2"])] + [(io["routed_w1"][e], io["routed_w2"][e]) for e in range(ER)]
            split_done = {}

            def expert_weights(n):
                nonlocal raw_free
                s = n % 2
                a, c = w_order[n]
                sp.wait(*raw_free)
                load("wraw", w1_raw[:, :, :], a.rearrange("(k p) n -> p k n", p=P))
                got = load("wraw", w2_raw[:, :, :], c.rearrange("(k p) n -> p k n", p=P))
                for k in range(KT):
                    m = split(w1_raw[:, k, :], [w[:, k, :] for w in w1s[s]], (got,), w_free[s])
                    yield
                for f in range(FT):
                    m = split(w2_raw[:, f, :], [w[:, f, :] for w in w2s[s]], (got,), w2_free[s])
                    yield
                split_done[n] = m
                raw_free = (m,)

            hidden_done = [None]

            def ffn_hidden(n, c0, w, ready, xt):
                nonlocal pr_free
                s = n % 2
                pe.wait(split_done[n], *ready)
                marks = []
                for f in range(FT):
                    for half_, bank in ((1, banks[2 * f + 1]), (0, banks[2 * f])):
                        t = claim(bank)
                        for k in range(KT):
                            cols = slice(half_ * FF + f * P, half_ * FF + (f + 1) * P)
                            ins = product(t[:, 0:w], [p[:, k, cols] for p in w1s[s]],
                                          [p[:, k, c0:c0 + w] for p in xt], k == 0, k == KT - 1)
                        m = hidden_done[0] = pe.mark(ins)
                        if half_:
                            act.wait(m, *sg_free[f])
                            ms = act.mark(act.q.activation(sg[f][:, 0:w], t[:, 0:w], ACT.Silu))
                            bank.read = (ms,)
                        yield
                    dve.wait(m, ms, *pr_free)
                    mp = dve.then(dve.q.tensor_tensor(pr[:, 0:w], sg[f][:, 0:w], t[:, 0:w], ALU.mult))
                    banks[2 * f].read = sg_free[f] = (mp,)
                    m = split(pr[:, 0:w], [p[:, f, c0:c0 + w] for p in at], (mp,), at_free)
                    pr_free = (m,)
                    marks.append(m)
                yield marks

            tok = ExitStack()
            with tok:
                aff = sb("aff", [P, TOKT, ER], ctx=tok)
                xts = [[sb(f"xt{i}_{c}", [P, KT, NB], F32R, ctx=tok) for c in "hl"] for i in range(2)]
                xts_free = [(), ()]
                x3i = [sb(f"x3d{i}", [P, D], ctx=tok) for i in range(3)]
                lg_t = sb("lg_t", [ER, NB], ctx=tok)
                before = sb("before", [P, ER, ER], ctx=tok)
                rank = sb("rank", [P, TOKT, ER], ctx=tok)
                mask = sb("mask", [P, TOKT, ER], ctx=tok)
                gt = sb("gt", [P, 8, ER, ER], ctx=tok)
                tmp = sb("tmp", [P, TOKT, ER], ctx=tok)
                score = sb("score", [P, ER, TOKT], ctx=tok)
                thr = sb("thr", [P, ER], ctx=tok)
                cand = sb("cand", [P, ER], ctx=tok)
                hit = sb("hit", [P, ER, TOKT], ctx=tok)
                over = sb("over", [P, ER, TOKT], ctx=tok)
                cnt = sb("cnt", [P, ER], ctx=tok)
                keep = sb("keep", [P, ER], ctx=tok)
                earlier = sb("earlier", [P, P], ctx=tok)
                ones = sb("ones", [P, P], ctx=tok)
                tot = sb("tot", [P, ER, TOKT], ctx=tok)
                scan = sb("scan", [P, ER, TOKT], ctx=tok)
                zero = sb("zero", [P, TOKT], ctx=tok)
                base = sb("base", [P, ER], ctx=tok)
                slot_f = sb("slot_f", [P, 2, TOKT], ctx=tok)
                slot = sb("slot", [P, 2, TOKT], I32, ctx=tok)
                gw_raw = sb("gw_raw", [P, KT, ER], ctx=tok)
                eb = sb("eb", [P, ER], ctx=tok)

                dve.q.memset(zero[:, :], 0.0)
                dve.q.memset(ones[:, :], 1.0)
                dve.q.memset(earlier[:, :], 1.0)
                m = dve.then(dve.q.memset(before[:, :, :], 1.0))
                pool.wait(m)
                pool.q.affine_select(out=earlier[:, :], in_=earlier[:, :], compare_op=ALU.is_gt, fill=0.0, base=0,
                                     pattern=[[1, P]], channel_multiplier=-1)
                pool.q.affine_select(out=before[:, :, :], in_=before[:, :, :], compare_op=ALU.is_gt,
                                     fill=0.0, base=0, pattern=[[1, ER], [-1, ER]], channel_multiplier=0)
                BIG = 1 << 20
                consts = pool.mark(pool.q.iota(base[:, :], pattern=[[SPAD, ER]], base=-BIG, channel_multiplier=0,
                                               allow_small_or_imprecise_dtypes=True))
                pe.wait(consts)
                dve.wait(consts)
                act.wait(consts)
                load("gw", gw_raw[:, :, :], io["gate_w"].rearrange("(k p) n -> p k n", p=P))
                got_gw = load("gw", eb[:, :], io["expert_bias"].rearrange("(a n) -> a n", a=1).broadcast_to([P, ER]))
                gw_ready = split(gw_raw[:, :, :], [p[:, :, :] for p in gw], (got_gw,))
                weights0 = expert_weights(0)

                def turn_tile(i):
                    t = claim(banks[4 + i % 2])
                    for k in range(KT):
                        ins = pe.q.transpose(t[:, k * P:(k + 1) * P], rows[:, i, k * P:(k + 1) * P], ident[:, :])
                    return pe.mark(ins)

                def split_tile(i, j, m):
                    blk, bank = i // BLK % 2, banks[4 + i % 2]
                    m = split(bank.t[:, :].rearrange("p (k n) -> p k n", k=KT),
                              [p[:, :, j * P:(j + 1) * P] for p in xts[blk]], (m,), xts_free[blk])
                    bank.read = (m,)
                    return m

                def transposed_block(blk):
                    for j in range(BLK):
                        m = split_tile(blk * BLK + j, j, turn_tile(blk * BLK + j))
                    return m

                b_lg, b_lt = banks[7], banks[6]
                lgt = claim(b_lg)
                x3_free = [(), (), ()]
                lt_done = ()
                m_next = transposed_block(0)
                for blk in range(NBLK):
                    m, xt = m_next, xts[blk % 2]
                    if blk + 1 < NBLK:
                        m_next = transposed_block(blk + 1)
                    next(weights0, None)
                    t = claim(b_lt)
                    pe.wait(m, gw_ready)
                    for k in range(KT):
                        ins = product(t[0:ER, :], [p[:, k, :] for p in gw], [p[:, k, :] for p in xt], k == 0, k == KT - 1)
                    m = pe.mark(ins)
                    xts_free[blk % 2] = (m,)
                    act.wait(m, *lt_done)
                    m = act.mark(act.q.copy(lg_t[:, :], t[0:ER, :]))
                    b_lt.read = (m,)
                    pe.wait(m)
                    for j in range(BLK):
                        i = blk * BLK + j
                        ins = pe.q.transpose(lgt[:, i * ER:(i + 1) * ER], lg_t[:, j * P:(j + 1) * P], ident[0:ER, 0:ER])
                    m_lg = pe.mark(ins)
                    lt_done = (m_lg,)
                for _ in weights0:
                    pass

                def route():
                    dve.wait(m_lg, got_gw)
                    m = dve.mark(dve.q.tensor_tensor(
                        aff[:, :, :], lgt[:, 0:N7].rearrange("p (t n) -> p t n", n=ER),
                        eb[:, :].unsqueeze(1).broadcast_to([P, TOKT, ER]), ALU.add))
                    b_lg.read = (m,)
                    act.wait(m)
                    m = act.mark(act.q.activation(aff[:, :, :], aff[:, :, :], ACT.Exp, scale=-1.0))
                    dve.wait(m)
                    dve.then(dve.q.tensor_scalar(aff[:, :, :], aff[:, :, :], 1.0, None, ALU.add))
                    dve.then(dve.q.reciprocal(aff[:, :, :], aff[:, :, :]))
                    yield
                    for c in range(0, TOKT, 8):
                        full = [P, 8, ER, ER]
                        mine = aff[:, c:c + 8, :].unsqueeze(3).broadcast_to(full)
                        other = aff[:, c:c + 8, :].unsqueeze(2).broadcast_to(full)
                        dve.then(dve.q.tensor_tensor(gt[:, :, :, :], other, mine, ALU.is_equal))
                        dve.then(dve.q.tensor_tensor(gt[:, :, :, :], gt[:, :, :, :],
                                                     before[:, :, :].unsqueeze(1).broadcast_to(full), ALU.mult))
                        dve.then(dve.q.tensor_reduce(rank[:, c:c + 8, :], gt[:, :, :, :], AX, ALU.add))
                        dve.then(dve.q.tensor_tensor(gt[:, :, :, :], other, mine, ALU.is_gt))
                        dve.then(dve.q.tensor_reduce(tmp[:, c:c + 8, :], gt[:, :, :, :], AX, ALU.add))
                        yield
                    dve.then(dve.q.tensor_tensor(rank[:, :, :], rank[:, :, :], tmp[:, :, :], ALU.add))
                    dve.then(dve.q.tensor_scalar(mask[:, :, :], rank[:, :, :], 1.5, None, ALU.is_lt))
                    dve.then(dve.q.tensor_tensor(tmp[:, :, :], aff[:, :, :], mask[:, :, :], ALU.mult))
                    dve.then(dve.q.scalar_tensor_tensor(score[:, :, :].rearrange("p e t -> p t e"), mask[:, :, :], -1.0,
                                                        tmp[:, :, :], ALU.add, ALU.add))
                    dve.then(dve.q.memset(thr[:, :], 0.0))
                    yield

                    def per_expert(a):
                        return a[:, :].unsqueeze(2).broadcast_to([P, ER, TOKT])

                    def flat(a):
                        return a[:, :, :].rearrange("p e t -> p (e t)")

                    def count(limit, op, into):
                        dve.then(dve.q.tensor_tensor(into[:, :, :], score[:, :, :], per_expert(limit), op))
                        m = dve.then(dve.q.tensor_reduce(cnt[:, :], into[:, :, :], AX, ALU.add))
                        t = claim(b_lg)
                        pe.wait(m)
                        m = pe.mark(pe.q.matmul(t[:, 0:ER], ones[:, :], cnt[:, :], start=True, stop=True))
                        return t, m

                    for bit in range(29, -1, -1):
                        dve.then(dve.q.tensor_scalar(cand[:, :].bitcast(I32), thr[:, :].bitcast(I32), 1 << bit, None,
                                                     ALU.bitwise_or))
                        t, m = count(cand, ALU.is_ge, hit)
                        yield
                        dve.wait(m)
                        m = dve.then(dve.q.tensor_scalar(keep[:, :], t[:, 0:ER], float(CAP) - 0.5, None, ALU.is_gt))
                        b_lg.read = (m,)
                        dve.then(dve.q.copy_predicated(thr[:, :], keep[:, :].bitcast(I32), cand[:, :]))
                    t, m = count(thr, ALU.is_gt, over)
                    yield
                    dve.wait(m)
                    m = dve.then(dve.q.tensor_scalar(keep[:, :], t[:, 0:ER], -1.0, float(CAP) - 0.5, ALU.mult, ALU.add))
                    b_lg.read = (m,)
                    m = dve.then(dve.q.tensor_tensor(hit[:, :, :], score[:, :, :], per_expert(thr), ALU.is_equal))

                    def positions(of, m):
                        t = claim(b_lg)
                        pe.wait(m)
                        pe.q.matmul(t[:, 0:N7], ones[:, :], flat(of), start=True, stop=True)
                        m = pe.mark(pe.q.matmul(t[:, N7:2 * N7], earlier[:, :], flat(of), start=True, stop=True))
                        yield
                        dve.wait(m)
                        dve.then(dve.q.tensor_copy(flat(tot), t[:, 0:N7]))
                        for e in range(ER):
                            m = dve.mark(dve.q.tensor_tensor_scan(scan[:, e, :], tot[:, e, :], zero[:, :], 0.0,
                                                                  ALU.add, ALU.add))
                        dve.wait(m)
                        dve.then(dve.q.tensor_tensor(flat(scan), flat(scan), flat(tot), ALU.subtract))
                        m = dve.then(dve.q.tensor_tensor(flat(scan), flat(scan), t[:, N7:2 * N7], ALU.add))
                        b_lg.read = (m,)

                    yield from positions(hit, m)
                    dve.then(dve.q.tensor_tensor(scan[:, :, :], scan[:, :, :], per_expert(keep), ALU.is_lt))
                    dve.then(dve.q.tensor_tensor(scan[:, :, :], scan[:, :, :], hit[:, :, :], ALU.mult))
                    dve.then(dve.q.tensor_tensor(over[:, :, :], over[:, :, :], scan[:, :, :], ALU.add))
                    m = dve.then(dve.q.tensor_tensor(over[:, :, :], over[:, :, :],
                                                     mask[:, :, :].rearrange("p t e -> p e t"), ALU.mult))
                    kept = over[:, :, :].rearrange("p e t -> p t e")
                    dve.then(dve.q.tensor_tensor(rows[:, :, D + 1:D + 1 + ER], aff[:, :, :], kept, ALU.mult))
                    yield from positions(over, m)
                    dve.then(dve.q.tensor_tensor(scan[:, :, :], scan[:, :, :], per_expert(base), ALU.add))
                    dve.then(dve.q.tensor_tensor(scan[:, :, :], scan[:, :, :], over[:, :, :], ALU.mult))
                    for c in range(2):
                        dve.then(dve.q.tensor_scalar(tmp[:, :, :], rank[:, :, :], float(c), None, ALU.is_equal))
                        dve.then(dve.q.tensor_tensor(tmp[:, :, :], tmp[:, :, :],
                                                     scan[:, :, :].rearrange("p e t -> p t e"), ALU.mult))
                        dve.then(dve.q.tensor_reduce(slot_f[:, c, :], tmp[:, :, :], AX, ALU.add))
                    dve.then(dve.q.tensor_scalar(slot_f[:, :, :], slot_f[:, :, :], float(BIG), None, ALU.add))
                    m = dve.then(dve.q.tensor_copy(slot[:, :, :], slot_f[:, :, :]))
                    pool.wait(m)
                    yield
                    for i in range(TOKT):
                        for c in range(2):
                            state["scattered"] = load("scatter", None, None, pool, ins=pool.q.indirect_dma_start(
                                out=slots_d[:, :],
                                out_offset=bass.IndirectOffsetOnAxis(ap=slot[:, c, i:i + 1].bitcast(U32), axis=0),
                                in_=rows[:, i, :], in_offset=None, bounds_check=ER * SPAD - 1, oob_is_err=False))
                        yield

                def shared():
                    nonlocal at_free
                    m_next = transposed_block(0)
                    for blk in range(NBLK):
                        n = blk * BLK + BLK
                        for s, m in enumerate(ffn_hidden(0, 0, NB, (m_next,), xts[blk % 2])):
                            turned = s < BLK and n + s < TOKT and turn_tile(n + s)
                            yield
                            if turned:
                                m_later = split_tile(n + s, s, turned)
                        m_next = m_later
                        xts_free[blk % 2] = ((pe, pe.count),)
                        for j in range(BLK):
                            i = blk * BLK + j
                            sp.wait(*x3_free[i % 3])
                            gx = load(f"x3l{i % 3}", x3i[i % 3][:, :], x3_d[i * P:(i + 1) * P, :])
                            bank = banks[2 * (j % 2)]
                            t = claim(bank)
                            for f in range(FT):
                                pe.wait(m[f])
                                ins = product(t[:, :], [p[:, f, j * P:(j + 1) * P] for p in at],
                                              [p[:, f, :] for p in w2s[0]], f == 0, f == FT - 1)
                            mm = pe.mark(ins)
                            yield
                            dve.wait(mm, gx)
                            mo = dve.mark(dve.q.tensor_tensor(x3i[i % 3][:, :], x3i[i % 3][:, :], t[:, :], ALU.add))
                            bank.read = (mo,)
                            sp.wait(mo)
                            st = load(f"xo{i % 3}", io["out"][i * P:(i + 1) * P, :], x3i[i % 3][:, :])
                            x3_free[i % 3] = (st,)
                        at_free = ((pe, pe.count),)
                    for st in x3_free:
                        state["out_stored"] = state.get("out_stored", ()) + tuple(st)
                    w_free[0] = ((pe, pe.count),)

                state = {}
                run_together((route(), 75.0), (shared(), 65.0))
                w2_free[0] = at_free
                for _ in expert_weights(1):
                    pass
            meet()

            ex_ = ExitStack()
            with ex_:
                NT = -(-SPAD // P)
                xg = [rows[:, i, :] for i in range(2 * NT)]
                yg = [sb(f"yg{i}", [P, D], ctx=ex_) for i in range(3)]
                xts = [[sb(f"xte{i}_{c}", [P, KT, SPAD], F32R, ctx=ex_) for c in "hl"] for i in range(2)]
                at = [sb(f"ate_{c}", [P, FT, SPAD], F32R, ctx=ex_) for c in "hl"]
                xg_free = [() for _ in xg]
                yg_free = [(), (), ()]
                xts_free = [(), ()]
                at_free = ()
                got_g, turned = {}, {}
                added = ()

                def fetch(e):
                    for i in range(NT):
                        n = min(P, SPAD - i * P)
                        q = (e % 2) * NT + i
                        sp.wait(*xg_free[q])
                        got_g[e, i] = load(f"xg{q}", xg[q][0:n, :], slots_d[e * SPAD + i * P:e * SPAD + i * P + n, :])

                def turn(e, tiles):
                    for i in tiles:
                        n = min(P, SPAD - i * P)
                        bank = banks[4 + i % 2]
                        t = claim(bank)
                        pe.wait(got_g[e, i])
                        for k in range(KT):
                            ins = pe.q.transpose(t[:, k * P:k * P + n], xg[(e % 2) * NT + i][0:n, k * P:(k + 1) * P],
                                                 ident[0:n, 0:n])
                        m = pe.mark(ins)
                        v = t[:, :].rearrange("p (k n) -> p k n", k=KT)[:, :, 0:n]
                        turned[e] = split(v, [p[:, :, i * P:i * P + n] for p in xts[e % 2]], (m,), xts_free[e % 2])
                        bank.read = (turned[e],)

                fetch(0)
                turn(0, range(NT))
                for e in range(ER):
                    if e + 1 < ER:
                        fetch(e + 1)
                    ready = (turned[e],)
                    for c in range(2):
                        for m in ffn_hidden(e + 1, c * HALF, HALF, ready, xts[e % 2]):
                            pass
                        if e + 1 < ER:
                            turn(e + 1, (range(0, 2), range(2, NT))[c])
                    xts_free[e % 2] = w_free[(e + 1) % 2] = (hidden_done[0],)
                    for _ in (expert_weights(e + 2) if e + 2 <= ER else ()):
                        pass
                    for i in range(NT):
                        n = min(P, SPAD - i * P)
                        q = (e % 2) * NT + i
                        bank = banks[6 + i % 2]
                        t = claim(bank)
                        pe.wait(*m)
                        for f in range(FT):
                            ins = product(t[0:n, :], [p[:, f, i * P:i * P + n] for p in at],
                                          [p[:, f, :] for p in w2s[(e + 1) % 2]], f == 0, f == FT - 1)
                        mm = pe.mark(ins)
                        y = yg[i % 3]
                        dve.wait(mm, *yg_free[i % 3])
                        mo = dve.mark(dve.q.tensor_scalar(y[0:n, :], t[0:n, :], xg[q][0:n, D + 1 + e:D + 2 + e], None, ALU.mult))
                        bank.read = (mo,)
                        pool.wait(mo, *added)
                        ad = load(f"add{i % 3}", None, None, pool, ins=pool.q.indirect_dma_start(
                            out=io["out"][:, :],
                            out_offset=bass.IndirectOffsetOnAxis(ap=xg[q][0:n, D:D + 1].bitcast(U32), axis=0),
                            in_=y[0:n, :], in_offset=None, bounds_check=T + P - 1, oob_is_err=True, compute_op=ALU.add))
                        yg_free[i % 3] = (ad,)
                        xg_free[q] = (ad,)
                    added = tuple(a for s in yg_free for a in s)
                    at_free = w2_free[(e + 1) % 2] = (mm,)
        meet()


def kernel(**inputs):
    import numpy as np
    import concourse.bacc as bacc
    from concourse.bass_utils import run_bass_kernel_spmd

    a = {k: np.asarray(v) for k, v in inputs.items()}
    B, S, D = a["x"].shape
    T = B * S
    NH = a["L0_xattn_bi"].shape[0]
    ctx = a["ctx_2048"].reshape(T, D)
    ctx_t = np.ascontiguousarray(ctx.T)
    arrays = {
        "x": a["x"].reshape(T, D),
        "ctx_t": ctx_t,
        "ctx_rev": np.ascontiguousarray(ctx_t.reshape(D // 128, 128, T)[:, ::-1, :]).reshape(D, T),
        "ctx_v": np.concatenate([ctx.reshape(T, NH, D // NH), np.ones((T, NH, 1), ctx.dtype)], axis=2).reshape(T, -1),
        "w_if": np.concatenate([a["L0_xattn_Wi"], a["L0_xattn_Wf"]], axis=1),
        "bi": a["L0_xattn_bi"], "bf": a["L0_xattn_bf"], "ln_scale": a["L0_xattn_ln_scale"],
        "gate_weight_t": np.ascontiguousarray(a["L0_ffn_gate_weight"].T),
        "gate_up_t": np.ascontiguousarray(a["L0_ffn_gate_up_proj"].transpose(0, 2, 1)),
        "down_t": np.ascontiguousarray(a["L0_ffn_down_proj"].transpose(0, 2, 1)),
        "merge": a["L0_ffn_merge_groups"], "dominant": a["L0_ffn_dominant_experts"],
        "ssm": a["L1_xattn_ssm_kernel"], "skip": a["L1_xattn_D"],
        "gate_w": a["L1_ffn_gate_w"], "expert_bias": a["L1_ffn_expert_bias"],
        "shared_w1": a["L1_ffn_shared_w1"][0], "shared_w2": a["L1_ffn_shared_w2"][0],
        "routed_w1": a["L1_ffn_routed_w1"], "routed_w2": a["L1_ffn_routed_w2"],
    }
    arrays = {k: np.ascontiguousarray(v) for k, v in arrays.items()}
    nc = bacc.Bacc("TRN2", target_bir_lowering=False, num_devices=1)
    io = {k: nc.dram_tensor("in_" + k, list(v.shape), mybir.dt.from_np(v.dtype), kind="ExternalInput").ap()
          for k, v in arrays.items()}
    io["out"] = nc.dram_tensor("out_x", [T + 128, D], F32, kind="ExternalOutput").ap()
    shapes = {k: v.shape for k, v in arrays.items()}
    shapes["x"] = (B, S, D)
    shapes["gate_weight"] = a["L0_ffn_gate_weight"].shape
    build_program(nc, io, shapes)
    r = run_bass_kernel_spmd(nc, [{"in_" + k: v for k, v in arrays.items()}], core_ids=[0])
    return r.results[0]["out_x"][:T].reshape(B, S, D)
```
